# Optimizing a Trainium2 kernel written in Bass

```python
import numpy as np
import jax
import jax.numpy as jnp

def _softmax(x, axis=-1):
    return jax.nn.softmax(x, axis=axis)

def _gelu(x):
    return jax.nn.gelu(x, approximate=True)

def _silu(x):
    return jax.nn.silu(x)

def _sigmoid(x):
    return jax.nn.sigmoid(x)

def _layernorm(x, axis=-1, eps=1e-05):
    m = jnp.mean(x, axis=axis, keepdims=True)
    v = jnp.var(x, axis=axis, keepdims=True)
    return (x - m) / jnp.sqrt(v + eps)

def _scatter_add(tgt, idx, src, axis=0):
    return tgt.at[idx].add(src)

def _segment_sum(src, seg, n):
    return jax.ops.segment_sum(src, seg, n)
kernel_name = 'mk_early_fusion_d2_tok_img512_r4_c8302d'

def setup_inputs(seed: int=0):
    np.random.seed(seed)
    _w = jnp.asarray

    def _rec_inputs():
        import jax
        import jax.numpy as jnp
        _rk = jax.random.key(seed)
        x = -0.000356955 + 1 * jax.random.normal(jax.random.fold_in(_rk, 1), (32, 3, 224, 224), jnp.float32)
        txt = 0.0185972 + 1.43333 * jax.random.normal(jax.random.fold_in(_rk, 2), (32, 128, 128), jnp.float32)
        return (x, txt)
    x, txt = _rec_inputs()

    def _L0_tok_setup():
        import jax, jax.numpy as jnp
        import numpy as np
        key = jax.random.key(seed)
        k1, k2, k3 = jax.random.split(key, 3)
        B, C, H, W = (128, 3, 224, 224)
        E, p = (128, 16)
        K = C * p * p
        img = jax.random.normal(k1, (B, C, H, W), dtype=jnp.float32)
        w = jax.random.normal(k2, (E, K), dtype=jnp.float32) * (1.0 / np.sqrt(K))
        b = jax.random.normal(k3, (E,), dtype=jnp.float32)
        return {'img': img, 'w': w, 'b': b, 'patch_size': p}
    _L0_tok_all = _L0_tok_setup()
    _L0_tok_in = {k: v for k, v in _L0_tok_all.items() if k in ('w', 'b')}
    del _L0_tok_all

    def _L0_attn_setup():
        import jax, jax.numpy as jnp
        import numpy as np
        EPS = 1e-05
        key = jax.random.key(seed)
        ks = jax.random.split(key, 6)
        B, T, D, H = (2, 1024, 128, 8)
        bound = float(np.sqrt(6.0 / (D + D)))

        def xavier(k):
            return jax.random.uniform(k, (D, D), jnp.float32, -bound, bound)
        return {'x': jax.random.normal(ks[0], (B, T, D), jnp.float32), 'W_q': xavier(ks[1]), 'W_k': xavier(ks[2]), 'W_v': xavier(ks[3]), 'W_o': xavier(ks[4]), 'ln_gamma': jnp.ones((D,), jnp.float32), 'ln_beta': jnp.zeros((D,), jnp.float32)}
    _L0_attn_all = _L0_attn_setup()
    _L0_attn_in = {k: v for k, v in _L0_attn_all.items() if k in ('W_q', 'W_k', 'W_v', 'W_o', 'ln_gamma', 'ln_beta')}
    del _L0_attn_all

    def _L0_ffn_setup():
        import jax, jax.numpy as jnp
        import numpy as np
        B, S, H = (4, 1024, 128)
        E, K = (64, 8)
        IE, IS = (128, 352)
        key = jax.random.key(seed)
        ks = jax.random.split(key, 8)
        scale = 0.02
        return {'x': jax.random.normal(ks[0], (B, S, H), jnp.float32), 'gate_w': jax.random.normal(ks[1], (E, H), jnp.float32) * scale, 'w1': jax.random.normal(ks[2], (E, H, IE), jnp.float32) * scale, 'w3': jax.random.normal(ks[3], (E, H, IE), jnp.float32) * scale, 'w2': jax.random.normal(ks[4], (E, IE, H), jnp.float32) * scale, 'sw1': jax.random.normal(ks[5], (H, IS), jnp.float32) * scale, 'sw3': jax.random.normal(ks[6], (H, IS), jnp.float32) * scale, 'sw2': jax.random.normal(ks[7], (IS, H), jnp.float32) * scale}
    _L0_ffn_all = _L0_ffn_setup()
    _L0_ffn_in = {k: v for k, v in _L0_ffn_all.items() if k in ('gate_w', 'w1', 'w3', 'w2', 'sw1', 'sw3', 'sw2')}
    del _L0_ffn_all

    def _L1_attn_setup():
        import jax, jax.numpy as jnp
        import numpy as np
        DIM = 128
        QK_DIM = DIM // 8
        EXPAND_DIM = DIM * 2
        LN_EPS = 1e-05

        def _layer_norm(x):
            mu = jnp.mean(x, axis=-1, keepdims=True)
            var = jnp.mean(jnp.square(x - mu), axis=-1, keepdims=True)
            return (x - mu) * jax.lax.rsqrt(var + LN_EPS)
        key = jax.random.key(seed)
        k1, k2, k3 = jax.random.split(key, 3)
        B, N = (8, 512)
        x = jax.random.normal(k1, (B, N, DIM), dtype=jnp.float32)
        out_e = 2 * QK_DIM + 2 * EXPAND_DIM
        be = float(np.sqrt(6.0 / (DIM + out_e)))
        expand = jax.random.uniform(k2, (DIM, out_e), minval=-be, maxval=be, dtype=jnp.float32)
        bp = float(np.sqrt(6.0 / (EXPAND_DIM + DIM)))
        project = jax.random.uniform(k3, (EXPAND_DIM, DIM), minval=-bp, maxval=bp, dtype=jnp.float32)
        position_bias_mult = jnp.array(4.0, dtype=jnp.float32)
        return {'x': x, 'expand': expand, 'project': project, 'position_bias_mult': position_bias_mult}
    _L1_attn_all = _L1_attn_setup()
    _L1_attn_in = {k: v for k, v in _L1_attn_all.items() if k in ('expand', 'project', 'position_bias_mult')}
    del _L1_attn_all

    def _L1_ffn_setup():
        import jax, jax.numpy as jnp
        import numpy as np
        E = 8
        K = 1
        D = 128
        I = 512
        B, T = (2, 512)
        key = jax.random.key(seed)
        ks = jax.random.split(key, 7)
        s = 0.02
        x = jax.random.normal(ks[0], (B, T, D), jnp.float32)
        gate_w = jax.random.normal(ks[1], (E, D), jnp.float32) * s
        w1 = jax.random.normal(ks[2], (E, I, D), jnp.float32) * s
        w2 = jax.random.normal(ks[3], (E, D, I), jnp.float32) * s
        w3 = jax.random.normal(ks[4], (E, I, D), jnp.float32) * s
        sw1 = jax.random.normal(ks[5], (I, D), jnp.float32) * s
        sw2 = jax.random.normal(ks[6], (D, I), jnp.float32) * s
        return {'x': x, 'gate_w': gate_w, 'w1': w1, 'w2': w2, 'w3': w3, 'sw1': sw1, 'sw2': sw2}
    _L1_ffn_all = _L1_ffn_setup()
    _L1_ffn_in = {k: v for k, v in _L1_ffn_all.items() if k in ('gate_w', 'w1', 'w2', 'w3', 'sw1', 'sw2')}
    del _L1_ffn_all
    return {'x': x, 'txt': txt, 'L0_tok_w': _L0_tok_in['w'], 'L0_tok_b': _L0_tok_in['b'], 'L0_attn_W_q': _L0_attn_in['W_q'], 'L0_attn_W_k': _L0_attn_in['W_k'], 'L0_attn_W_v': _L0_attn_in['W_v'], 'L0_attn_W_o': _L0_attn_in['W_o'], 'L0_attn_ln_gamma': _L0_attn_in['ln_gamma'], 'L0_attn_ln_beta': _L0_attn_in['ln_beta'], 'L0_ffn_gate_w': _L0_ffn_in['gate_w'], 'L0_ffn_w1': _L0_ffn_in['w1'], 'L0_ffn_w3': _L0_ffn_in['w3'], 'L0_ffn_w2': _L0_ffn_in['w2'], 'L0_ffn_sw1': _L0_ffn_in['sw1'], 'L0_ffn_sw3': _L0_ffn_in['sw3'], 'L0_ffn_sw2': _L0_ffn_in['sw2'], 'L1_attn_expand': _L1_attn_in['expand'], 'L1_attn_project': _L1_attn_in['project'], 'L1_attn_position_bias_mult': _L1_attn_in['position_bias_mult'], 'L1_ffn_gate_w': _L1_ffn_in['gate_w'], 'L1_ffn_w1': _L1_ffn_in['w1'], 'L1_ffn_w2': _L1_ffn_in['w2'], 'L1_ffn_w3': _L1_ffn_in['w3'], 'L1_ffn_sw1': _L1_ffn_in['sw1'], 'L1_ffn_sw2': _L1_ffn_in['sw2']}

def reference(x, txt, L0_tok_w, L0_tok_b, L0_attn_W_q, L0_attn_W_k, L0_attn_W_v, L0_attn_W_o, L0_attn_ln_gamma, L0_attn_ln_beta, L0_ffn_gate_w, L0_ffn_w1, L0_ffn_w3, L0_ffn_w2, L0_ffn_sw1, L0_ffn_sw3, L0_ffn_sw2, L1_attn_expand, L1_attn_project, L1_attn_position_bias_mult, L1_ffn_gate_w, L1_ffn_w1, L1_ffn_w2, L1_ffn_w3, L1_ffn_sw1, L1_ffn_sw2):
    import jax
    import jax.numpy as jnp

    def _L0_tok_ref(img, w, b, patch_size):
        import jax, jax.numpy as jnp
        import numpy as np
        B, C, H, W = img.shape
        p = patch_size
        Hp, Wp = (H // p, W // p)
        S = Hp * Wp
        patches = img.reshape(B, C, Hp, p, Wp, p)
        patches = patches.transpose(0, 2, 4, 1, 3, 5).reshape(B, S, C * p * p)
        out = jnp.einsum('bsk,ek->bse', patches, w) + b
        return out

    def _L0_attn_ref(x, W_q, W_k, W_v, W_o, ln_gamma, ln_beta):
        import jax, jax.numpy as jnp
        import numpy as np
        EPS = 1e-05
        B, T, D = x.shape
        H = 8
        hd = D // H
        scale = jnp.sqrt(jnp.asarray(hd, x.dtype))

        def proj(W):
            y = jnp.einsum('btd,ed->bte', x, W)
            return y.reshape(B, T, H, hd).transpose(0, 2, 1, 3)
        Q, K, V = (proj(W_q), proj(W_k), proj(W_v))
        scores = jnp.einsum('bhtd,bhsd->bhts', Q, K) / scale
        attn = jax.nn.softmax(scores, axis=-1)
        ctx = jnp.einsum('bhts,bhsd->bhtd', attn, V)
        ctx = ctx.transpose(0, 2, 1, 3).reshape(B, T, D)
        out = jnp.einsum('btd,ed->bte', ctx, W_o)
        y = out + x
        mu = jnp.mean(y, axis=-1, keepdims=True)
        var = jnp.var(y, axis=-1, keepdims=True)
        return (y - mu) * jax.lax.rsqrt(var + EPS) * ln_gamma + ln_beta

    def _L0_ffn_ref(x, gate_w, w1, w3, w2, sw1, sw3, sw2):
        import jax, jax.numpy as jnp
        import numpy as np
        B, S, H = (4, 1024, 128)
        E, K = (64, 8)
        IE, IS = (128, 352)
        b, s, h = x.shape
        xf = x.reshape(-1, h)
        T = xf.shape[0]
        logits = xf @ gate_w.T
        topk_w, topk_idx = jax.lax.top_k(logits, K)
        topk_w = jax.nn.softmax(topk_w, axis=-1)
        expert_flat = topk_idx.reshape(-1)
        order = jnp.argsort(expert_flat)
        group_sizes = jnp.bincount(expert_flat, length=E).astype(jnp.int32)
        tok_ids = (jnp.arange(T * K) // K)[order]
        xg = xf[tok_ids]
        hid = jax.nn.silu(jax.lax.ragged_dot(xg, w1, group_sizes)) * jax.lax.ragged_dot(xg, w3, group_sizes)
        y = jax.lax.ragged_dot(hid, w2, group_sizes)
        y = y * topk_w.reshape(-1)[order][:, None]
        routed = jnp.zeros_like(xf).at[tok_ids].add(y)
        shared = jax.nn.silu(xf @ sw1) * (xf @ sw3) @ sw2
        return (routed + shared).reshape(b, s, h)

    def _L1_attn_ref(x, expand, project, position_bias_mult):
        import jax, jax.numpy as jnp
        import numpy as np
        DIM = 128
        QK_DIM = DIM // 8
        EXPAND_DIM = DIM * 2
        LN_EPS = 1e-05

        def _layer_norm(x):
            mu = jnp.mean(x, axis=-1, keepdims=True)
            var = jnp.mean(jnp.square(x - mu), axis=-1, keepdims=True)
            return (x - mu) * jax.lax.rsqrt(var + LN_EPS)
        B, N, _ = x.shape
        nx = _layer_norm(x)
        h = nx @ expand
        q = h[..., :QK_DIM]
        k = h[..., QK_DIM:2 * QK_DIM]
        linear = h[..., 2 * QK_DIM:2 * QK_DIM + EXPAND_DIM]
        pre_gelu = h[..., 2 * QK_DIM + EXPAND_DIM:]
        gated = linear * jax.nn.gelu(pre_gelu, approximate=False)
        local = gated[..., :EXPAND_DIM - DIM]
        v = gated[..., EXPAND_DIM - DIM:]
        pos = jnp.arange(N)
        rel = (pos[None, :] - pos[:, None]).astype(x.dtype)
        causal = pos[None, :] <= pos[:, None]
        mask = jnp.where(causal, jax.nn.sigmoid(rel + position_bias_mult), -jnp.inf)
        logits = jnp.einsum('bqd,bkd->bqk', q, k) / jnp.sqrt(jnp.array(QK_DIM, dtype=x.dtype)) + mask
        scores = jax.nn.softmax(logits, axis=-1)
        attn = jnp.einsum('bqk,bkd->bqd', scores, v)
        return x + jnp.concatenate([local, attn], axis=-1) @ project

    def _L1_ffn_ref(x, gate_w, w1, w2, w3, sw1, sw2):
        import jax, jax.numpy as jnp
        import numpy as np
        E = 8
        K = 1
        D = 128
        I = 512
        B, T = (2, 512)
        xf = x.reshape(-1, D)
        logits = xf @ gate_w.T
        wts, idx = jax.lax.top_k(logits, K)
        wts = jax.nn.softmax(wts, axis=-1)
        comb = jnp.einsum('nke,nk->ne', jax.nn.one_hot(idx, E, dtype=xf.dtype), wts)
        h = jax.nn.silu(jnp.einsum('nd,eid->nei', xf, w1)) * jnp.einsum('nd,eid->nei', xf, w3)
        y = jnp.einsum('nei,edi->nd', h * comb[:, :, None], w2)
        y = y + jax.nn.gelu(xf @ sw1.T, approximate=False) @ sw2.T
        return y.reshape(x.shape)
    h = _L0_tok_ref(x, L0_tok_w, L0_tok_b, 16)
    h = jnp.concatenate([h, txt], axis=1)
    h = h + _L0_attn_ref(_layernorm(h, axis=-1), L0_attn_W_q, L0_attn_W_k, L0_attn_W_v, L0_attn_W_o, L0_attn_ln_gamma, L0_attn_ln_beta)
    h = h + _L0_ffn_ref(_layernorm(h, axis=-1), L0_ffn_gate_w, L0_ffn_w1, L0_ffn_w3, L0_ffn_w2, L0_ffn_sw1, L0_ffn_sw3, L0_ffn_sw2)
    h = h + _L1_attn_ref(_layernorm(h, axis=-1), L1_attn_expand, L1_attn_project, L1_attn_position_bias_mult)
    h = h + _L1_ffn_ref(_layernorm(h, axis=-1), L1_ffn_gate_w, L1_ffn_w1, L1_ffn_w2, L1_ffn_w3, L1_ffn_sw1, L1_ffn_sw2)
    return h

_drawn_inputs = setup_inputs


def setup_inputs(seed=0):
    import zlib

    import numpy as np

    out = dict(_drawn_inputs(seed))
    spreads = {'L0_attn_ln_gamma': (1.0, 0.2), 'L0_attn_ln_beta': (0.0, 0.1)}
    factors = {'L0_ffn_gate_w': 8.0,
     'L0_ffn_w1': 8.0,
     'L0_ffn_w3': 8.0,
     'L0_ffn_w2': 8.0,
     'L0_ffn_sw1': 8.0,
     'L0_ffn_sw3': 8.0,
     'L0_ffn_sw2': 8.0,
     'L1_ffn_gate_w': 8.0,
     'L1_ffn_w1': 8.0,
     'L1_ffn_w2': 8.0,
     'L1_ffn_w3': 8.0,
     'L1_ffn_sw1': 3.648,
     'L1_ffn_sw2': 3.467}
    for name, (base, spread) in spreads.items():
        noise = np.random.default_rng([zlib.crc32(name.encode()), seed]).standard_normal(out[name].shape)
        drawn = base * np.exp(spread * noise) if base else spread * noise
        out[name] = jnp.asarray(drawn.astype(out[name].dtype))
    for name, factor in factors.items():
        out[name] = (out[name] * factor).astype(out[name].dtype)
    return out
```

```python
from contextlib import ExitStack

import numpy as np
import concourse.bass as bass
from concourse import mybir

F32 = mybir.dt.float32
BF16 = mybir.dt.bfloat16
I32 = mybir.dt.int32
U32 = mybir.dt.uint32
ALU = mybir.AluOpType
ACT = mybir.ActivationFunctionType
AX = mybir.AxisListType

D = 128
B = 32
TOK = 324
TT = 3
R = TOK // TT
NP = 196
KC = 6
NH = 8
HD = 16
EPS = 1e-5
NTILE = B * TT
QPART = (0, 0, 1, 1, 0, 2)
KPART = (0, 1, 0, 1, 2, 0)
NB = len(QPART)
SK = NB * HD
NEG = -1.0e30


def wait(eng, sem, value):
    if isinstance(value, int) and value <= 0:
        return
    eng.wait_ge(sem, value)


def stand(eng, g):
    eng.sem_inc(g.stand, 1)


def turns(eng, slots, lag_max, body, count=B):
    first = (-(-lag_max // slots) + 1) * slots
    for it in range(first):
        body(it // slots, it % slots)
    with eng.Fori(first // slots, count // slots) as m:
        for j in range(slots):
            body(m, j)
    for it in range(count // slots * slots, count + lag_max):
        body(it // slots, it % slots)


def lagged(m, j, lag, slots, count=B):
    back, slot = divmod(j - lag, slots)
    visit = m + back
    i = visit * slots + slot
    if isinstance(i, int) and not 0 <= i < count:
        return None
    return Image(j=slot, m=visit, i=i)


class Image:

    def __init__(self, j, m, i):
        self.j, self.m, self.i = j, m, i


class Shared:
    pass


class Dram(dict):
    pass


class Phase:

    def __init__(self, nc, name):
        self.nc, self.name, self.ctx, self.sems = nc, name, ExitStack(), []

    def sb(self, name, shape, dt=F32):
        return self.ctx.enter_context(self.nc.sbuf_tensor(f"{self.name}_{name}", shape, dt))

    def ps(self, name, shape, dt=F32):
        return self.ctx.enter_context(self.nc.psum_tensor(f"{self.name}_{name}", shape, dt))

    def sem(self, name):
        self.sems.append(self.ctx.enter_context(self.nc.semaphore(f"{self.name}_{name}")))
        return self.sems[-1]

    def __enter__(self):
        return self

    def __exit__(self, *a):
        if self.sems and a[0] is None:
            with self.nc.Block() as block:
                @block.gpsimd
                def _(pool):
                    for s in self.sems:
                        pool.sem_clear(s)
        return self.ctx.__exit__(*a)


def tile_of(h, i, k=0, n=TT):
    return h[:, bass.ds(i * TT + k, n), :]


def constants(nc, g):
    with Phase(nc, "const") as ph:
        s_set = ph.sem("set")
        with nc.Block() as block:
            @block.gpsimd
            def _(pool):
                pool.memset(g.minus_half[:], -0.5).then_inc(s_set, 1)
                pool.memset(g.ident[:], 0.0).then_inc(s_set, 1)
                pool.wait_ge(s_set, 2)
                pool.affine_select(out=g.ident[:], in_=g.ident[:], compare_op=ALU.not_equal, fill=1.0, base=0,
                                   pattern=[[-1, 128]], channel_multiplier=1).then_inc(s_set, 1)
                pool.wait_ge(s_set, 3)
                pool.tensor_copy(g.ident16[:], g.ident[:]).then_inc(s_set, 1)


def embed(nc, g, d):
    U = 2
    with Phase(nc, "emb") as ph:
        w_tok = ph.sb("w_tok", [128, KC, D])
        b_tok = ph.sb("b_tok", [R, D])
        wq, wk, wv = (ph.sb(n, [D, D]) for n in ("wq", "wk", "wv"))
        patches = [ph.sb(f"patches{j}", [128, KC, NP]) for j in range(U)]
        stats = [ph.sb(f"stats{j}", [R, TT, 6]) for j in range(U)]
        mv = [ph.sb(f"mv{j}", [R, TT, 2]) for j in range(U)]
        veps = [ph.sb(f"veps{j}", [R, TT]) for j in range(U)]
        rstd = [ph.sb(f"rstd{j}", [R, TT]) for j in range(U)]
        xn = [ph.sb(f"xn{j}", [R, TT, D]) for j in range(U)]
        xnT = [ph.sb(f"xnT{j}", [D, TOK]) for j in range(U)]
        part = [[ph.sb(f"{n}part{j}", [D, 3, TOK], BF16) for j in range(U)] for n in "qk"]
        rest = [[ph.sb(f"{n}rest{j}", [D, TOK]) for j in range(U)] for n in "qk"]
        vone = [ph.sb(f"v_{j}", [R, TT, NH, 2 * HD]) for j in range(U)]
        psH = [ph.ps(f"psH{j}", [128, 512]) for j in range(U)]
        psT = ph.ps("psT", [128, 512])
        psQK = [ph.ps(f"ps{n}", [128, 512]) for n in "qk"]
        psV = ph.ps("psV", [128, 512])
        s_w = ph.sem("weights_in")
        s_txt = ph.sem("text_in")
        s_patches = [ph.sem(f"patches_in{j}") for j in range(U)]
        s_patched = ph.sem("patched")
        s_h = ph.sem("h_written")
        s_stats, s_mv, s_veps, s_rstd, s_xn = (ph.sem(n) for n in ("stats", "mv", "veps", "rstd", "xn_written"))
        s_turned, s_xnT = ph.sem("turned"), ph.sem("xnT_written")
        s_qk, s_v = ph.sem("qk_projected"), ph.sem("v_projected")
        s_part1, s_rest, s_part2, s_part3, s_vone = (ph.sem(n) for n in ("part1", "rest", "part2", "part3", "vone"))
        s_ones = ph.sem("ones_set")
        s_xn_out = [ph.sem(f"xn_out{j}") for j in range(U)]
        s_qk_out = [ph.sem(f"qk_out{j}") for j in range(U)]
        s_v_out = [ph.sem(f"v_out{j}") for j in range(U)]
        LOAD, PATCH, LN, PR = 0, 1, 2, 3

        with nc.Block() as block:
            @block.sync
            def _(sp):
                for dst, src in ((w_tok[:], d["w_tok"]), (b_tok[:], d["b_tok"].partition_broadcast(R)),
                                 (wq[:], d["wq"]), (wk[:], d["wk"]), (wv[:], d["wv"])):
                    sp.dma_start(dst, src).then_inc(s_w, 16)
                n_mid = 2 * R - NP
                mid = g.h[R - n_mid:R, :, :].rearrange("p (b t) e -> p b t e", t=TT)[:, :, 1, :]
                last = g.h[:, :, :].rearrange("p (b t) e -> p b t e", t=TT)[:, :, 2, :]
                sp.dma_start(mid, d["txt"][:, 0:n_mid, :].rearrange("b p e -> p b e")).then_inc(s_txt, 16)
                sp.dma_start(last, d["txt"][:, n_mid:128, :].rearrange("b p e -> p b e")).then_inc(s_txt, 16)

                def body(m, j):
                    a = lagged(m, j, LOAD, U)
                    if a:
                        wait(sp, s_patched, a.i - 1)
                        sp.dma_start(patches[a.j][:], d["patches"][bass.ds(a.i, 1)].rearrange("o p c n -> (o p) c n")).then_inc(s_patches[a.j], 16)
                    a = lagged(m, j, LN, U)
                    if a:
                        wait(sp, s_xn, 3 * a.i + 3)
                        sp.dma_start(d["xn"][bass.ds(a.i, 1)].rearrange("o p t e -> (o p) t e"), xn[a.j][:]).then_inc(s_xn_out[a.j], 16)
                    a = lagged(m, j, PR, U)
                    if a:
                        wait(sp, s_vone, a.i + 1)
                        sp.dma_start(d["vone"][bass.ds(a.i, 1)].rearrange("o p t h e -> (o p) t h e"), vone[a.j][:]).then_inc(s_v_out[a.j], 16)
                        wait(sp, s_part1, 2 * a.i + 2)
                        wait(sp, s_part2, 2 * a.i + 2)
                        wait(sp, s_part3, 2 * a.i + 2)
                        for n, dst in enumerate((d["q_parts"], d["k_parts"])):
                            sp.dma_start(dst[bass.ds(a.i, 1)].rearrange("o h e a t -> (o h e) a t"), part[n][a.j][:]).then_inc(s_qk_out[a.j], 16)
                turns(sp, U, PR, body)
                for j in range(U):
                    sp.wait_ge(s_xn_out[j], 16 * B // U)
                    sp.wait_ge(s_v_out[j], 16 * B // U)
                    sp.wait_ge(s_qk_out[j], 32 * B // U)

            @block.tensor
            def _(pe):
                pe.wait_ge(s_w, 80)

                def body(m, j):
                    a = lagged(m, j, PATCH, U)
                    if a:
                        pe.wait_ge(s_patches[a.j], 16 * (a.m + 1))
                        wait(pe, s_h, 2 * a.i - 2)
                        for t, n in enumerate((R, NP - R)):
                            for c in range(KC):
                                mm = nc.tensor.matmul(psH[a.j][0:n, t * D:(t + 1) * D], patches[a.j][:, c, t * R:t * R + n],
                                                      w_tok[:, c, :], start=(c == 0), stop=(c == KC - 1))
                        mm.then_inc(s_patched, 1)
                    a = lagged(m, j, LN, U)
                    if a:
                        wait(pe, s_xn, 3 * a.i + 3)
                        wait(pe, s_xnT, a.i)
                        for t in range(TT):
                            mm = nc.tensor.transpose(psT[:, t * R:(t + 1) * R], xn[a.j][:, t, :], g.ident[0:R, 0:R])
                        mm.then_inc(s_turned, 1)
                    a = lagged(m, j, PR, U)
                    if a:
                        wait(pe, s_xnT, a.i + 1)
                        wait(pe, s_rest, 2 * a.i)
                        for n, w in enumerate((wq, wk)):
                            nc.tensor.matmul(psQK[n][:, 0:TOK], w[:], xnT[a.j][:], start=True, stop=True).then_inc(s_qk, 1)
                        wait(pe, s_vone, a.i)
                        for t in range(TT):
                            mm = nc.tensor.matmul(psV[0:R, t * D:(t + 1) * D], xnT[a.j][:, t * R:(t + 1) * R], wv[:],
                                                  start=True, stop=True)
                        mm.then_inc(s_v, 1)
                turns(pe, U, PR, body)

            @block.vector
            def _(dve):
                dve.wait_ge(s_w, 80)
                dve.wait_ge(s_txt, 32)

                def body(m, j):
                    a = lagged(m, j, PATCH, U)
                    if a:
                        wait(dve, s_patched, a.i + 1)
                        for t, n in enumerate((R, NP - R)):
                            nc.vector.tensor_tensor(g.h[0:n, bass.ds(a.i * TT + t, 1), :].rearrange("p o e -> p (o e)"),
                                                    psH[a.j][0:n, t * D:(t + 1) * D], b_tok[0:n, :], ALU.add).then_inc(s_h, 1)
                        wait(dve, s_h, 2 * a.i + 2)
                        wait(dve, s_mv, 3 * a.i - 3)
                        stand(dve, g)
                        for t in range(TT):
                            nc.vector.bn_stats(stats[a.j][:, t, :], g.h[:, bass.ds(a.i * TT + t, 1), :].rearrange("p o e -> p (o e)")).then_inc(s_stats, 1)
                        wait(dve, s_stats, 3 * a.i + 3)
                        wait(dve, s_xn, 3 * a.i - 3)
                        wait(dve, s_veps, a.i - 1)
                        stand(dve, g)
                        for t in range(TT):
                            nc.vector.bn_aggr(mv[a.j][:, t, :], stats[a.j][:, t, :]).then_inc(s_mv, 1)
                    a = lagged(m, j, LN, U)
                    if a:
                        wait(dve, s_rstd, a.i + 1)
                        wait(dve, s_turned, a.i - 1)
                        wait(dve, s_xn_out[a.j], 16 * a.m)
                        for t in range(TT):
                            nc.vector.tensor_scalar(xn[a.j][:, t, :], g.h[:, bass.ds(a.i * TT + t, 1), :].rearrange("p o e -> p (o e)"),
                                                    mv[a.j][:, t, 0:1], rstd[a.j][:, t:t + 1], ALU.subtract, ALU.mult).then_inc(s_xn, 1)
                    a = lagged(m, j, PR, U)
                    if a:
                        for n in range(2):
                            wait(dve, s_part1, 2 * a.i + n + 1)
                            wait(dve, s_part3, 2 * (a.i - 1))
                            nc.vector.tensor_tensor(rest[n][a.j][:], psQK[n][:, 0:TOK], part[n][a.j][:, 0, :], ALU.subtract).then_inc(s_rest, 1)
                turns(dve, U, PR, body)

            @block.scalar
            def _(act):
                def body(m, j):
                    a = lagged(m, j, LN, U)
                    if a:
                        wait(act, s_turned, a.i + 1)
                        wait(act, s_v, a.i - 1)
                        nc.scalar.copy(xnT[a.j][:], psT[:, 0:TOK]).then_inc(s_xnT, 1)
                    a = lagged(m, j, PR, U)
                    if a:
                        for n in range(2):
                            wait(act, s_qk, 2 * a.i + n + 1)
                            wait(act, s_qk_out[a.j], 32 * a.m)
                            wait(act, s_part3, 2 * (a.i - 1))
                            nc.scalar.copy(part[n][a.j][:, 0, :], psQK[n][:, 0:TOK]).then_inc(s_part1, 1)
                        wait(act, s_v, a.i + 1)
                        wait(act, s_v_out[a.j], 16 * a.m)
                        if isinstance(a.i, int) and a.i < U:
                            act.wait_ge(s_ones, U)
                        nc.scalar.copy(vone[a.j][:, :, :, 0:HD],
                                       psV[0:R, 0:TT * D].rearrange("p (t h e) -> p t h e", t=TT, h=NH)).then_inc(s_vone, 1)
                turns(act, U, PR, body)

            @block.gpsimd
            def _(pool):
                for j in range(U):
                    pool.memset(vone[j][:], 1.0).then_inc(s_ones, 1)

                def body(m, j):
                    a = lagged(m, j, PATCH, U)
                    if a:
                        wait(pool, s_mv, 3 * a.i + 3)
                        wait(pool, s_rstd, a.i - 1)
                        stand(pool, g)
                        pool.tensor_scalar(veps[a.j][:], mv[a.j][:, :, 1], EPS, None, ALU.add).then_inc(s_veps, 1)
                        wait(pool, s_veps, a.i + 1)
                        wait(pool, s_xn, 3 * (a.i - 1))
                        pool.tensor_tensor(rstd[a.j][:], veps[a.j][:], g.minus_half[0:R, 0:TT], ALU.pow).then_inc(s_rstd, 1)
                    a = lagged(m, j, PR, U)
                    if a:
                        for n in range(2):
                            wait(pool, s_rest, 2 * a.i + n + 1)
                            wait(pool, s_qk_out[a.j], 32 * a.m)
                            stand(pool, g)
                            pool.tensor_copy(part[n][a.j][:, 1, :], rest[n][a.j][:]).then_inc(s_part2, 1)
                            wait(pool, s_part2, 2 * a.i + n + 1)
                            pool.tensor_tensor(part[n][a.j][:, 2, :], rest[n][a.j][:], part[n][a.j][:, 1, :], ALU.subtract).then_inc(s_part3, 1)
                turns(pool, U, PR, body)


def attention0(nc, g, d):
    U = 4
    LOAD, SCORE, MAXT, MIX, OUT = 0, 1, 2, 3, 4
    with Phase(nc, "at0") as ph:
        q_st = [ph.sb(f"q_stack{j}", [SK + 3, NH, TOK], BF16) for j in range(U)]
        k_st = [ph.sb(f"k_stack{j}", [SK + 3, NH, TOK], BF16) for j in range(U)]
        vone = [ph.sb(f"v_{j}", [R, TT, NH, 2 * HD]) for j in range(U)]
        xn = [ph.sb(f"xn{j}", [R, TT * D]) for j in range(U)]
        wo = ph.sb("wo", [D, D])
        gamma, beta = ph.sb("gamma", [R, D]), ph.sb("beta", [R, D])
        negmax = [ph.sb(f"negmax{j}", [R, TT, NH]) for j in range(2)]
        mrest = ph.sb("mrest", [R, TT, NH])
        mpart = [ph.sb(f"mpart{j}", [R, TT, 3 * NH], BF16) for j in range(2)]
        mT = [ph.sb(f"mT{j}", [3 * NH, TOK], BF16) for j in range(2)]
        probs = [ph.sb(f"probs{j}", [R, TT, TOK]) for j in range(2)]
        recip = ph.sb("recip", [R, TT, 4])
        mixed = [ph.sb(f"mixed{j}", [128, 2, TOK]) for j in range(2)]
        ctxv = [ph.sb(f"context{j}", [R, TT, D]) for j in range(2)]
        ctxT = [ph.sb(f"contextT{j}", [D, TOK]) for j in range(2)]
        y = [ph.sb(f"y{j}", [R, TT, D]) for j in range(2)]
        z = [ph.sb(f"z{j}", [R, TT, D]) for j in range(2)]
        stats = ph.sb("stats", [R, TT, 6])
        mv = ph.sb("mv", [R, TT, 2])
        veps, rstd = ph.sb("veps", [R, TT]), ph.sb("rstd", [R, TT])
        psN = ph.ps("psN", [128, TT, 512])
        psS = ph.ps("psS", [128, TT, 512])
        psO = ph.ps("psO", [128, 512])
        psM = ph.ps("psM", [128, 512])
        psM16 = psM[:, :].bitcast(BF16)
        s_w, s_ones = ph.sem("weights_in"), ph.sem("ones_set")
        blank = ph.sb("blank", [128, FFN0.rows // B])
        s_blank, s_blanked = ph.sem("blank_set"), g.blanked
        s_qk = [ph.sem(f"qk_in{j}") for j in range(U)]
        s_vin = [ph.sem(f"v_in{j}") for j in range(U)]
        s_xn = [ph.sem(f"xn_in{j}") for j in range(U)]
        s_mout = [ph.sem(f"max_out{j}") for j in range(U)]
        s_min = [ph.sem(f"max_in{j}") for j in range(U)]
        s_scored, s_max, s_scoredT, s_exp, s_mixed = (ph.sem(n) for n in ("scored", "max", "scoredT", "exp", "mixed"))
        s_heads, s_back = ph.sem("heads_copied"), ph.sem("heads_turned")
        s_mp, s_mturn, s_mT = ph.sem("max_parts"), ph.sem("max_turned"), ph.sem("maxT_written")
        s_recip, s_ctx, s_cturn, s_ctxT = (ph.sem(n) for n in ("recip", "context", "context_turned", "contextT"))
        s_out, s_y, s_stats, s_mv, s_veps, s_rstd = (ph.sem(n) for n in ("projected", "y", "stats", "mv", "veps", "rstd"))
        s_z, s_zg, s_h = ph.sem("normalised"), ph.sem("scaled"), ph.sem("h_added")
        NDMA = 2 * NB

        with nc.Block() as block:
            @block.sync
            def _(sp):
                for dst, src in ((wo[:], d["wo"]), (gamma[:], d["gamma"].partition_broadcast(R)), (beta[:], d["beta"].partition_broadcast(R))):
                    sp.dma_start(dst, src).then_inc(s_w, 16)

                def body(m, j):
                    a = lagged(m, j, LOAD, U)
                    if a:
                        wait(sp, s_scoredT, NH * (a.i - U + 1))
                        for st, parts, src in ((q_st, QPART, d["q_parts"]), (k_st, KPART, d["k_parts"])):
                            for r, n in enumerate(parts):
                                sp.dma_start(st[a.j][r * HD:(r + 1) * HD, :, :],
                                             src[bass.ds(a.i, 1), :, :, n, :].rearrange("o h e t -> (o e) h t")).then_inc(s_qk[a.j], 16)
                    a = lagged(m, j, MAXT, U)
                    if a:
                        wait(sp, s_mixed, NH * (a.i - U + 1))
                        sp.dma_start(vone[a.j][:], d["vone"][bass.ds(a.i, 1)].rearrange("o p t h e -> (o p) t h e")).then_inc(s_vin[a.j], 16)
                        wait(sp, s_y, a.i - U + 1)
                        sp.dma_start(xn[a.j][:], d["xn"][bass.ds(a.i, 1)].rearrange("o p t e -> (o p) (t e)")).then_inc(s_xn[a.j], 16)
                        wait(sp, s_mT, a.i + 1)
                        sp.dma_start(d["maxima"][bass.ds(a.i, 1)].rearrange("o a t -> (o a) t"), mT[a.j % 2][:]).then_inc(s_mout[a.j], 16)
                        wait(sp, s_mout[a.j], 16 * (a.m + 1))
                        sp.dma_start(q_st[a.j][SK:SK + 3, :, :], d["maxima"][bass.ds(a.i, 1)].rearrange("o (a h) t -> (o a) h t", a=3)).then_inc(s_min[a.j], 16)
                turns(sp, U, MAXT, body)

            @block.tensor
            def _(pe):
                pe.wait_ge(s_w, 48)
                pe.wait_ge(s_ones, U)

                def mix(a, k):
                    wait(pe, s_exp, NH * a.i + k + 1)
                    if k % 4 == 0:
                        wait(pe, s_heads, 2 * a.i + k // 4)
                    for c in range(TT):
                        mm = nc.tensor.matmul(psO[32 * (k % 4):32 * (k % 4) + 32, 0:TOK], vone[a.j][:, c, k, :], probs[k % 2][:, c, :],
                                              start=(c == 0), stop=(c == TT - 1), tile_position=(0, 32 * (k % 4)))
                    mm.then_inc(s_mixed, 1)

                def body(m, j):
                    score, mx, mixi, out = (lagged(m, j, lag, U) for lag in (SCORE, MAXT, MIX, OUT))
                    for k in range(NH):
                        if score:
                            wait(pe, s_max, NH * score.i + k)
                        if out and k <= 2:
                            wait(pe, s_ctx, 2 * out.i + k)
                        if out and k < 2:
                            wait(pe, s_heads, 2 * out.i + k + 1)
                            if not score:
                                wait(pe, s_max, NH * B)
                            for t in range(TT):
                                mm = nc.tensor.transpose(psN[0:R, t, TOK:TOK + 128], mixed[out.j % 2][:, k, t * R:(t + 1) * R], g.ident[:])
                            mm.then_inc(s_back, 1)
                        if score:
                            if k == 0:
                                wait(pe, s_qk[score.j], 16 * NDMA * (score.m + 1))
                            for t in range(TT):
                                mm = nc.tensor.matmul(psN[0:R, t, 0:TOK], q_st[score.j][0:SK, k, t * R:(t + 1) * R],
                                                      k_st[score.j][0:SK, k, :], start=True, stop=True)
                            mm.then_inc(s_scored, 1)
                        if mixi:
                            if k == 0:
                                wait(pe, s_min[mixi.j], 16 * (mixi.m + 1))
                                wait(pe, s_vin[mixi.j], 16 * (mixi.m + 1))
                            wait(pe, s_exp, NH * mixi.i + k)
                            for c in range(TT):
                                mm = nc.tensor.matmul(psS[0:R, c, 0:TOK], k_st[mixi.j][:, k, c * R:(c + 1) * R],
                                                      q_st[mixi.j][:, k, :], start=True, stop=True)
                            mm.then_inc(s_scoredT, 1)
                            if k > 0:
                                mix(mixi, k - 1)
                        if mx and k == 2:
                            wait(pe, s_mp, 4 * mx.i + 4)
                            wait(pe, s_y, mx.i - OUT + MAXT)
                            for t in range(TT):
                                mm = nc.tensor.transpose(psM16[0:3 * NH, t * R:(t + 1) * R], mpart[mx.j % 2][:, t, :], g.ident16[0:R, 0:R])
                            mm.then_inc(s_mturn, 1)
                        if out and k == 3:
                            wait(pe, s_ctx, 2 * out.i + 2)
                            n = out.i + OUT - MAXT + 1
                            wait(pe, s_mT, min(n, B) if isinstance(n, int) else n)
                            for t in range(TT):
                                mm = nc.tensor.transpose(psM[:, t * R:(t + 1) * R], ctxv[out.j % 2][:, t, :], g.ident[0:R, 0:R])
                            mm.then_inc(s_cturn, 1)
                        if out and k == 5:
                            wait(pe, s_ctxT, out.i + 1)
                            for t in range(TT):
                                mm = nc.tensor.matmul(psM[0:R, t * D:(t + 1) * D], ctxT[out.j % 2][:, t * R:(t + 1) * R], wo[:],
                                                      start=True, stop=True)
                            mm.then_inc(s_out, 1)
                    if mixi:
                        mix(mixi, NH - 1)
                turns(pe, U, OUT, body)

            @block.scalar
            def _(act):
                def heads(a, n):
                    wait(act, s_mixed, NH * a.i + 4 * n + 4)
                    wait(act, s_back, 2 * (a.i - 1))
                    nc.scalar.copy(mixed[a.j % 2][:, n, :], psO[:, 0:TOK]).then_inc(s_heads, 1)

                def body(m, j):
                    mx, mixi, out = (lagged(m, j, lag, U) for lag in (MAXT, MIX, OUT))
                    for k in range(NH):
                        if mixi:
                            wait(act, s_scoredT, NH * mixi.i + k + 1)
                            wait(act, s_mixed, NH * mixi.i + k - 1)
                            nc.scalar.activation(probs[k % 2][:], psS[0:R, :, 0:TOK], ACT.Exp, scale=0.25).then_inc(s_exp, 1)
                        if mixi and k == 4:
                            heads(mixi, 0)
                        if mx and k == 2:
                            wait(act, s_mturn, mx.i + 1)
                            if isinstance(mx.i, int) and mx.i < 2:
                                pass
                            else:
                                wait(act, s_mout[(mx.j + 2) % U], 16 * (mx.m + (0 if mx.j < 2 else 1)))
                            nc.scalar.copy(mT[mx.j % 2][:], psM16[0:3 * NH, 0:TOK]).then_inc(s_mT, 1)
                        if out and k == 3:
                            wait(act, s_cturn, out.i + 1)
                            wait(act, s_out, out.i - 1)
                            nc.scalar.copy(ctxT[out.j % 2][:], psM[:, 0:TOK]).then_inc(s_ctxT, 1)
                    if mixi:
                        heads(mixi, 1)
                turns(act, U, OUT, body)

            @block.vector
            def _(dve):
                for j in range(U):
                    nc.vector.memset(k_st[j][SK:SK + 3, :, :], 1.0).then_inc(s_ones, 1)
                dve.wait_ge(s_w, 48)

                def body(m, j):
                    score, out = (lagged(m, j, lag, U) for lag in (SCORE, OUT))
                    for k in range(NH):
                        if score:
                            wait(dve, s_scored, NH * score.i + k + 1)
                            if k == 0:
                                wait(dve, s_mp, 4 * (score.i - 1))
                            nc.vector.tensor_reduce(negmax[score.j % 2][:, :, k], psN[0:R, :, 0:TOK], AX.X, ALU.max, negate=True).then_inc(s_max, 1)
                        if out and k < 2:
                            n = 2 * out.i + k
                            turned = psN[0:R, :, TOK:TOK + 128].rearrange("p t (h e) -> p t h e", e=2 * HD)
                            wait(dve, s_back, n + 1)
                            wait(dve, s_ctx, n)
                            nc.vector.reciprocal(recip[:], turned[:, :, :, HD]).then_inc(s_recip, 1)
                            wait(dve, s_recip, n + 1)
                            wait(dve, s_cturn, out.i - 1)
                            nc.vector.tensor_tensor(ctxv[out.j % 2][:, :, k * 64:(k + 1) * 64].rearrange("p t (h e) -> p t h e", e=HD),
                                                    turned[:, :, :, 0:HD], recip[:].unsqueeze(3).broadcast_to([R, TT, 4, HD]),
                                                    ALU.mult).then_inc(s_ctx, 1)
                        if out and k == 5:
                            wait(dve, s_out, out.i + 1)
                            wait(dve, s_xn[out.j], 16 * (out.m + 1))
                            nc.vector.tensor_tensor(y[out.j % 2][:].rearrange("p t e -> p (t e)"), psM[0:R, 0:TT * D], xn[out.j][:], ALU.add).then_inc(s_y, 1)
                            wait(dve, s_y, out.i + 1)
                            stand(dve, g)
                            for t in range(TT):
                                nc.vector.bn_stats(stats[:, t, :], y[out.j % 2][:, t, :]).then_inc(s_stats, 1)
                            wait(dve, s_stats, 3 * out.i + 3)
                            wait(dve, s_veps, out.i)
                            stand(dve, g)
                            for t in range(TT):
                                nc.vector.bn_aggr(mv[:, t, :], stats[:, t, :]).then_inc(s_mv, 1)
                    if out:
                        wait(dve, s_rstd, out.i + 1)
                        wait(dve, s_h, out.i - 1)
                        for t in range(TT):
                            nc.vector.tensor_scalar(z[out.j % 2][:, t, :], y[out.j % 2][:, t, :], mv[:, t, 0:1], rstd[:, t:t + 1],
                                                    ALU.subtract, ALU.mult).then_inc(s_z, 1)
                turns(dve, U, OUT, body)

            @block.gpsimd
            def _(pool):
                pool.wait_ge(s_w, 48)
                pool.memset(blank[:], 0.0).then_inc(s_blank, 1)
                pool.wait_ge(s_blank, 1)

                def body(m, j):
                    mx, out = (lagged(m, j, lag, U) for lag in (MAXT, OUT))
                    if mx:
                        for f in (FFN0, FFN1):
                            n = f.rows // B
                            for xs in d["xs" + str(f.layer)]:
                                pool.dma_start(xs.rearrange("(p m) e -> p (m e)", p=128)[:, bass.ds(mx.i * n, n)],
                                               blank[:, 0:n]).then_inc(s_blanked, 16)
                        mp, nm = mpart[mx.j % 2], negmax[mx.j % 2]
                        wait(pool, s_max, NH * (mx.i + 1))
                        wait(pool, s_mturn, mx.i - 1)
                        stand(pool, g)
                        pool.tensor_copy(mp[:, :, 0:NH], nm[:]).then_inc(s_mp, 1)
                        wait(pool, s_mp, 4 * mx.i + 1)
                        pool.tensor_tensor(mrest[:], nm[:], mp[:, :, 0:NH], ALU.subtract).then_inc(s_mp, 1)
                        wait(pool, s_mp, 4 * mx.i + 2)
                        stand(pool, g)
                        pool.tensor_copy(mp[:, :, NH:2 * NH], mrest[:]).then_inc(s_mp, 1)
                        wait(pool, s_mp, 4 * mx.i + 3)
                        pool.tensor_tensor(mp[:, :, 2 * NH:3 * NH], mrest[:], mp[:, :, NH:2 * NH], ALU.subtract).then_inc(s_mp, 1)
                    if out:
                        wait(pool, s_mv, 3 * out.i + 3)
                        wait(pool, s_rstd, out.i)
                        stand(pool, g)
                        pool.tensor_scalar(veps[:], mv[:, :, 1], EPS, None, ALU.add).then_inc(s_veps, 1)
                        wait(pool, s_veps, out.i + 1)
                        wait(pool, s_z, 3 * out.i)
                        pool.tensor_tensor(rstd[:], veps[:], g.minus_half[0:R, 0:TT], ALU.pow).then_inc(s_rstd, 1)
                        zz = z[out.j % 2]
                        wait(pool, s_z, 3 * out.i + 3)
                        pool.tensor_tensor(zz[:], zz[:], gamma[:].unsqueeze(1).broadcast_to([R, TT, D]), ALU.mult).then_inc(s_zg, 1)
                        wait(pool, s_zg, 2 * out.i + 1)
                        pool.tensor_tensor(zz[:], zz[:], beta[:].unsqueeze(1).broadcast_to([R, TT, D]), ALU.add).then_inc(s_zg, 1)
                        wait(pool, s_zg, 2 * out.i + 2)
                        pool.tensor_tensor(tile_of(g.h, out.i), tile_of(g.h, out.i), zz[:], ALU.add).then_inc(s_h, 1)
                turns(pool, U, OUT, body)
                pool.wait_ge(s_blanked, 16 * 2 * TT * B)


class Ffn:

    def __init__(self, layer, experts, k, chunks, shared, act_shared, fused):
        self.layer, self.E, self.K, self.C = layer, experts, k, chunks
        self.I = chunks * 128
        self.W = 3 * self.I
        self.shared = shared
        self.act_shared, self.gated = act_shared, fused
        self.G = 4 // chunks
        self.blocks = -(-(B * R * k // 128 + experts) // 4) * 4
        self.rows = self.blocks * 128


FFN0 = Ffn(0, 64, 8, 1, (128, 128, 96), ACT.Silu, True)
FFN1 = Ffn(1, 8, 1, 4, (128, 128, 128, 128), ACT.Gelu, False)


def ffn(nc, g, d, f):
    with Phase(nc, f"ffn{f.layer}") as own:
        r = Shared()
        r.top = own.sb("top", [R, NTILE, 8])
        r.expert = own.sb("expert", [R, NTILE, 8])
        r.pos = own.sb("pos", [R, NTILE, f.K], I32)
        r.counts = own.sb("counts", [128, TT, f.E])
        r.expert_row = own.sb("expert_row", [1, TT * f.blocks], I32)
        with Phase(nc, f"rank{f.layer}") as ranks:
            r.rank = ranks.sb("rank", [R, NTILE, f.E])
            r.iota = ranks.sb("iota", [R, f.E])
            route(nc, g, d, f, r)
            lists(nc, g, d, f, r)
            scatter(nc, g, d, f, r)
        experts(nc, g, d, f, r)
        combine(nc, g, d, f, r)


def route(nc, g, d, f, r):
    U = 2
    STAT, NORM, GATE, RANK = 0, 1, 2, 3
    E = f.E
    with Phase(nc, f"route{f.layer}") as ph:
        gate = ph.sb("gate", [D, E])
        before = ph.sb("before", [R, R], BF16)
        ones = ph.sb("ones", [R, 128], BF16)
        stats = [ph.sb(f"stats{j}", [R, TT, 6]) for j in range(U)]
        mv = [ph.sb(f"mv{j}", [R, TT, 2]) for j in range(U)]
        veps = [ph.sb(f"veps{j}", [R, TT]) for j in range(U)]
        rstd = [ph.sb(f"rstd{j}", [R, TT]) for j in range(U)]
        xn = [ph.sb(f"xn{j}", [R, TT, D]) for j in range(U)]
        xnT = [ph.sb(f"xnT{j}", [D, TOK]) for j in range(U)]
        logits = [ph.sb(f"logits{j}", [R, TT, E]) for j in range(U)]
        rep = ph.sb("replaced", [R, TT, E])
        top8 = [ph.sb(f"top8_{j}", [R, TT, 8]) for j in range(U)]
        where = ph.sb("where", [R, TT, 8], U32)
        mask = [ph.sb(f"mask{j}", [R, TT, E], BF16) for j in range(U)]
        total = ph.sb("gate_total", [R, NTILE])
        psT = ph.ps("psT", [128, 512])
        psG = ph.ps("psG", [128, 512])
        psR = ph.ps("psR", [128, 512])
        psC = ph.ps("psC", [128, 512])
        s_w, s_set = ph.sem("weights_in"), ph.sem("constants_set")
        s_stats, s_mv, s_veps, s_rstd, s_xn = (ph.sem(n) for n in ("stats", "mv", "veps", "rstd", "xn_written"))
        s_turned, s_xnT, s_gated, s_logits = (ph.sem(n) for n in ("turned", "xnT_written", "gated", "logits"))
        s_kept, s_first = ph.sem("top_kept"), ph.sem("first_taken")
        s_top, s_where, s_expert, s_rep, s_mask = (ph.sem(n) for n in ("top", "where", "expert", "replaced", "mask"))
        s_rankps, s_rank, s_count = ph.sem("rank_multiplied"), ph.sem("rank_written"), ph.sem("counts_added")
        s_exp, s_soft = ph.sem("gates_exp"), ph.sem("softmax_step")
        s_xn_out = [ph.sem(f"xn_out{j}") for j in range(U)]
        s_xnT_out = [ph.sem(f"xnT_out{j}") for j in range(U)]
        top_all = r.top[:, :, 0:f.K]

        with nc.Block() as block:
            @block.sync
            def _(sp):
                sp.dma_start(gate[:], d["gate" + str(f.layer)]).then_inc(s_w, 16)

                def body(m, j):
                    a = lagged(m, j, NORM, U)
                    if a:
                        wait(sp, s_xn, 3 * a.i + 3)
                        sp.dma_start(d["xn"][bass.ds(a.i, 1)].rearrange("o p t e -> (o p) t e"), xn[a.j][:]).then_inc(s_xn_out[a.j], 16)
                        wait(sp, s_xnT, a.i + 1)
                        sp.dma_start(d["xnT"][bass.ds(a.i, 1)].rearrange("o e t -> (o e) t"), xnT[a.j][:]).then_inc(s_xnT_out[a.j], 16)
                turns(sp, U, RANK, body)
                for j in range(U):
                    sp.wait_ge(s_xn_out[j], 16 * B // U)
                    sp.wait_ge(s_xnT_out[j], 16 * B // U)

            @block.gpsimd
            def _(pool):
                pool.memset(ones[:], 1.0).then_inc(s_set, 1)
                pool.memset(before[:], 1.0).then_inc(s_set, 1)
                pool.memset(r.counts[:], 0.0).then_inc(s_set, 1)
                pool.iota(r.iota[:], pattern=[[1, E]], base=0, channel_multiplier=0,
                          allow_small_or_imprecise_dtypes=True).then_inc(s_set, 1)
                pool.wait_ge(s_set, 4)
                pool.affine_select(out=before[:], in_=before[:], compare_op=ALU.is_ge, fill=0.0, base=-1,
                                   pattern=[[1, R]], channel_multiplier=-1).then_inc(s_set, 1)

                def body(m, j):
                    a = lagged(m, j, STAT, U)
                    if a:
                        wait(pool, s_mv, 3 * a.i + 3)
                        wait(pool, s_rstd, a.i - 1)
                        stand(pool, g)
                        pool.tensor_scalar(veps[a.j][:], mv[a.j][:, :, 1], EPS, None, ALU.add).then_inc(s_veps, 1)
                        wait(pool, s_veps, a.i + 1)
                        wait(pool, s_xn, 3 * (a.i - 1))
                        pool.tensor_tensor(rstd[a.j][:], veps[a.j][:], g.minus_half[0:R, 0:TT], ALU.pow).then_inc(s_rstd, 1)
                turns(pool, U, RANK, body)

            @block.tensor
            def _(pe):
                pe.wait_ge(s_w, 16)
                pe.wait_ge(s_set, 5)

                def body(m, j):
                    a = lagged(m, j, NORM, U)
                    if a:
                        wait(pe, s_xn, 3 * a.i + 3)
                        wait(pe, s_xnT, a.i)
                        for t in range(TT):
                            mm = nc.tensor.transpose(psT[:, t * R:(t + 1) * R], xn[a.j][:, t, :], g.ident[0:R, 0:R])
                        mm.then_inc(s_turned, 1)
                    a = lagged(m, j, GATE, U)
                    if a:
                        wait(pe, s_xnT, a.i + 1)
                        wait(pe, s_logits, a.i)
                        for t in range(TT):
                            mm = nc.tensor.matmul(psG[0:R, t * E:(t + 1) * E], xnT[a.j][:, t * R:(t + 1) * R], gate[:], start=True, stop=True)
                        mm.then_inc(s_gated, 1)
                    a = lagged(m, j, RANK, U)
                    if a:
                        wait(pe, s_mask, a.i + 1)
                        wait(pe, s_rank, a.i)
                        wait(pe, s_count, a.i)
                        mk = mask[a.j][:].rearrange("p t e -> p (t e)")
                        nc.tensor.matmul(psR[0:R, 0:TT * E], before[:], mk, start=True, stop=True)
                        nc.tensor.matmul(psC[:, 0:TT * E], ones[:], mk, start=True, stop=True).then_inc(s_rankps, 1)
                turns(pe, U, RANK, body)

            @block.scalar
            def _(act):
                def body(m, j):
                    a = lagged(m, j, NORM, U)
                    if a:
                        wait(act, s_turned, a.i + 1)
                        wait(act, s_gated, a.i - 1)
                        wait(act, s_xnT_out[a.j], 16 * a.m)
                        nc.scalar.copy(xnT[a.j][:], psT[:, 0:TOK]).then_inc(s_xnT, 1)
                    a = lagged(m, j, GATE, U)
                    if a:
                        wait(act, s_gated, a.i + 1)
                        wait(act, s_rep if f.K > 1 else s_where, 3 * (a.i - 1))
                        nc.scalar.copy(logits[a.j][:].rearrange("p t e -> p (t e)"), psG[0:R, 0:TT * E]).then_inc(s_logits, 1)
                turns(act, U, RANK, body)
                act.wait_ge(s_soft, 1)
                nc.scalar.activation(top_all, top_all, ACT.Exp).then_inc(s_exp, 1)

            @block.vector
            def _(dve):
                dve.wait_ge(s_set, 5)

                def tile1(t3, i, t):
                    return t3[:, bass.ds(i * TT + t, 1), :].rearrange("p o e -> p (o e)")

                def body(m, j):
                    a = lagged(m, j, STAT, U)
                    if a:
                        wait(dve, s_mv, 3 * a.i - 3)
                        stand(dve, g)
                        for t in range(TT):
                            nc.vector.bn_stats(stats[a.j][:, t, :], tile1(g.h, a.i, t)).then_inc(s_stats, 1)
                        wait(dve, s_stats, 3 * a.i + 3)
                        wait(dve, s_xn, 3 * a.i - 3)
                        wait(dve, s_veps, a.i - 1)
                        stand(dve, g)
                        for t in range(TT):
                            nc.vector.bn_aggr(mv[a.j][:, t, :], stats[a.j][:, t, :]).then_inc(s_mv, 1)
                    a = lagged(m, j, NORM, U)
                    if a:
                        wait(dve, s_rstd, a.i + 1)
                        wait(dve, s_turned, a.i - 1)
                        wait(dve, s_xn_out[a.j], 16 * a.m)
                        for t in range(TT):
                            nc.vector.tensor_scalar(xn[a.j][:, t, :], tile1(g.h, a.i, t), mv[a.j][:, t, 0:1], rstd[a.j][:, t:t + 1],
                                                    ALU.subtract, ALU.mult).then_inc(s_xn, 1)
                    a = lagged(m, j, GATE, U)
                    if a:
                        wait(dve, s_logits, a.i + 1)
                        wait(dve, s_kept, a.i - 1)
                        stand(dve, g)
                        for t in range(TT):
                            nc.vector.max(top8[a.j][:, t, :], logits[a.j][:, t, :]).then_inc(s_top, 1)
                        wait(dve, s_top, 3 * a.i + 3)
                        wait(dve, s_expert, a.i)
                        stand(dve, g)
                        for t in range(TT):
                            nc.vector.max_index(where[:, t, :], top8[a.j][:, t, :], logits[a.j][:, t, :]).then_inc(s_where, 1)
                        if f.K > 1:
                            wait(dve, s_mask, a.i)
                            stand(dve, g)
                            for t in range(TT):
                                nc.vector.match_replace(rep[:, t, :], top8[a.j][:, t, :], logits[a.j][:, t, :], NEG).then_inc(s_rep, 1)
                        nc.vector.tensor_copy(tile_of(r.top, a.i), top8[a.j][:]).then_inc(s_kept, 1)
                        wait(dve, s_where, 3 * a.i + 3)
                        nc.vector.tensor_copy(tile_of(r.expert, a.i), where[:]).then_inc(s_expert, 1)
                        wait(dve, s_rankps, a.i - 1)
                        if f.K > 1:
                            wait(dve, s_rep, 3 * a.i + 3)
                            nc.vector.tensor_tensor(mask[a.j][:], rep[:], logits[a.j][:], ALU.not_equal).then_inc(s_mask, 1)
                        else:
                            wait(dve, s_expert, a.i + 1)
                            nc.vector.tensor_tensor(mask[a.j][:], r.iota[:].unsqueeze(1).broadcast_to([R, TT, E]),
                                                    tile_of(r.expert, a.i)[:, :, 0:1].broadcast_to([R, TT, E]), ALU.is_equal).then_inc(s_mask, 1)
                    a = lagged(m, j, RANK, U)
                    if a:
                        wait(dve, s_rankps, a.i + 1)
                        wait(dve, s_count, a.i)
                        nc.vector.tensor_tensor(tile_of(r.rank, a.i), psR[0:R, 0:TT * E].rearrange("p (t e) -> p t e", t=TT),
                                                r.counts[0:R], ALU.add).then_inc(s_rank, 1)
                        wait(dve, s_rank, a.i + 1)
                        nc.vector.tensor_tensor(r.counts[:], psC[:, 0:TT * E].rearrange("p (t e) -> p t e", t=TT), r.counts[:], ALU.add).then_inc(s_count, 1)
                turns(dve, U, RANK, body)
                dve.wait_ge(s_where, 3 * B)
                if f.K > 1:
                    dve.wait_ge(s_rep, 3 * B)
                dve.wait_ge(s_kept, B)
                nc.vector.tensor_copy(total[:], r.top[:, :, 0]).then_inc(s_first, 1)
                dve.wait_ge(s_first, 1)
                nc.vector.tensor_tensor(top_all, top_all, total[:].unsqueeze(2).broadcast_to([R, NTILE, f.K]), ALU.subtract).then_inc(s_soft, 1)
                dve.wait_ge(s_exp, 1)
                nc.vector.tensor_reduce(total[:], top_all, AX.X, ALU.add).then_inc(s_soft, 1)
                dve.wait_ge(s_soft, 2)
                nc.vector.reciprocal(total[:], total[:]).then_inc(s_soft, 1)
                dve.wait_ge(s_soft, 3)
                nc.vector.tensor_tensor(top_all, top_all, total[:].unsqueeze(2).broadcast_to([R, NTILE, f.K]), ALU.mult).then_inc(s_soft, 1)


def lists(nc, g, d, f, r):
    E = f.E
    pad = E // 2
    chunks = -(-f.blocks // 128)
    with Phase(nc, f"lists{f.layer}") as ph:
        whole = ph.sb("whole", [128, TT, E], I32)
        nblk = ph.sb("nblk", [128, TT, E])
        run = [ph.sb(f"run{n}", [128, TT, pad + E]) for n in range(2)]
        block_no = ph.sb("block_no", [128, chunks])
        below = ph.sb("below", [128, E])
        owner = ph.sb("owner", [128, TT, chunks])
        owner_i = ph.sb("owner_i", [128, TT, chunks], I32)
        s_iota, s_step, s_out, s_in = (ph.sem(n) for n in ("iota_set", "step", "table_out", "table_in"))
        with nc.Block() as block:
            @block.gpsimd
            def _(pool):
                pool.iota(block_no[:], pattern=[[128, chunks]], base=0, channel_multiplier=1,
                          allow_small_or_imprecise_dtypes=True).then_inc(s_iota, 1)

            @block.vector
            def _(dve):
                done = [0]

                def step(ins):
                    done[0] += 1
                    ins.then_inc(s_step, 1)
                    dve.wait_ge(s_step, done[0])
                step(nc.vector.memset(run[0][:], 0.0))
                step(nc.vector.memset(run[1][:], 0.0))
                step(nc.vector.tensor_scalar(whole[:], r.counts[:], 127.0, None, ALU.add))
                step(nc.vector.tensor_scalar(whole[:], whole[:], 7, None, ALU.logical_shift_right))
                step(nc.vector.tensor_copy(nblk[:], whole[:]))
                step(nc.vector.tensor_scalar(nblk[:], nblk[:], 1.0, None, ALU.max))
                step(nc.vector.tensor_copy(run[0][:, :, pad:], nblk[:]))
                now, s = 0, 1
                while s < E:
                    step(nc.vector.tensor_tensor(run[1 - now][:, :, pad:], run[now][:, :, pad:], run[now][:, :, pad - s:pad + E - s], ALU.add))
                    now, s = 1 - now, 2 * s
                last = run[now][:, :, pad:]
                step(nc.vector.tensor_tensor(nblk[:], last, nblk[:], ALU.subtract))
                step(nc.vector.tensor_scalar(r.counts[:], nblk[:], 128.0, None, ALU.mult))
                dve.wait_ge(s_iota, 1)
                for t in range(TT):
                    for c in range(chunks):
                        step(nc.vector.tensor_scalar(below[:], run[now][:, t, pad:], block_no[:, c:c + 1], None, ALU.is_le))
                        step(nc.vector.tensor_reduce(owner[:, t, c:c + 1], below[:], AX.X, ALU.add))
                step(nc.vector.tensor_scalar(owner[:], owner[:], float(E - 1), None, ALU.min))
                step(nc.vector.tensor_copy(owner_i[:], owner[:]))

            @block.sync
            def _(sp):
                sp.wait_ge(s_step, 9 + E.bit_length() - 1 + 2 * TT * chunks + 2)
                for t in range(TT):
                    for c in range(chunks):
                        n = min(128, f.blocks - 128 * c)
                        sp.dma_start(d["owner"][t * f.blocks + 128 * c:t * f.blocks + 128 * c + n].unsqueeze(1),
                                     owner_i[0:n, t, c:c + 1]).then_inc(s_out, 16)
                sp.wait_ge(s_out, 16 * TT * chunks)
                sp.dma_start(r.expert_row[:], d["owner"][0:TT * f.blocks].unsqueeze(0)).then_inc(s_in, 16)
                sp.wait_ge(s_in, 16)


def scatter(nc, g, d, f, r):
    U = 2
    LOAD, PLACE, SEND, HID, ADD = 0, 1, 2, 1, 2
    E, K = f.E, f.K
    xs = d["xs" + str(f.layer)]
    NC = len(f.shared)
    per = 2 if f.gated else 1
    with Phase(nc, f"scat{f.layer}") as ph:
        xn = [ph.sb(f"xn{j}", [R, TT, D]) for j in range(2 * U)]
        xnT = [ph.sb(f"xnT{j}", [D, TOK]) for j in range(U)]
        rowf = ph.sb("row", [R, TT, E])
        hot = ph.sb("hot", [R, TT * K, E])
        posf = ph.sb("posf", [R, TT * K])
        pos = [ph.sb(f"pos{j}", [R, TT * K], I32) for j in range(U)]
        w_in = ph.sb("shared_in", [D, per, sum(f.shared)])
        w_out = ph.sb("shared_out", [128, NC, D])
        silu = [ph.sb(f"silu{j}", [128, TOK]) for j in range(2)]
        hid = [ph.sb(f"hid{j}", [128, NC, TOK]) for j in range(U)]
        psA = [ph.ps(f"psA{n}", [128, 512]) for n in range(2)]
        psB = [ph.ps(f"psB{n}", [128, 512]) for n in range(2)]
        psY = ph.ps("psY", [128, 512])
        s_w = ph.sem("weights_in")
        s_xn = [ph.sem(f"xn_in{j}") for j in range(2 * U)]
        s_xnT = [ph.sem(f"xnT_in{j}") for j in range(U)]
        s_row, s_hot, s_pick, s_posf, s_pos, s_posall = (ph.sem(n) for n in ("row", "hot", "picked", "posf", "pos", "pos_kept"))
        s_sent = g.sent[f.layer]
        s_in, s_act, s_hid, s_down, s_h = (ph.sem(n) for n in ("in_multiplied", "activated", "hidden", "down", "h_added"))

        with nc.Block() as block:
            @block.sync
            def _(sp):
                lo = 0
                for c, w in enumerate(f.shared):
                    sp.dma_start(w_out[0:w, c, :], d["sw2_" + str(f.layer)][lo:lo + w, :]).then_inc(s_w, 16)
                    lo += w
                sp.dma_start(w_in[:, 0, :], d["sw1_" + str(f.layer)]).then_inc(s_w, 16)
                if f.gated:
                    sp.dma_start(w_in[:, 1, :], d["sw3_" + str(f.layer)]).then_inc(s_w, 16)

                def body(m, j):
                    a = lagged(m, j, LOAD, 2 * U)
                    if a:
                        for t in range(TT):
                            wait(sp, s_sent[t], 16 * K * (a.i - 2 * U + 1))
                        sp.dma_start(xn[a.j][:], d["xn"][bass.ds(a.i, 1)].rearrange("o p t e -> (o p) t e")).then_inc(s_xn[a.j], 16)
                        wait(sp, s_in, NC * (a.i - 1))
                        sp.dma_start(xnT[a.j % U][:], d["xnT"][bass.ds(a.i, 1)].rearrange("o e t -> (o e) t")).then_inc(s_xnT[a.j % U], 16)
                turns(sp, 2 * U, SEND, body)

            @block.gpsimd
            def _(pool):
                def body(m, j):
                    a = lagged(m, j, SEND, 2 * U)
                    if a:
                        wait(pool, s_pos, a.i + 1)
                        stand(pool, g)
                        wait(pool, s_xn[a.j], 16 * (a.m + 1))
                        stand(pool, g)
                        for k in range(K):
                            for t in range(TT):
                                n = 16 * (K * a.i + k)
                                if not (isinstance(n, int) and n <= 0):
                                    pool.wait_ge(s_sent[t], n)
                                    stand(pool, g)
                                pool.indirect_dma_start(xs[t], bass.IndirectOffsetOnAxis(ap=pos[a.j % U][:, t * K + k:t * K + k + 1], axis=0),
                                                        xn[a.j][:, t, :], None).then_inc(s_sent[t], 16)
                turns(pool, 2 * U, SEND, body)
                for t in range(TT):
                    pool.wait_ge(s_sent[t], 16 * K * B)

            @block.tensor
            def _(pe):
                pe.wait_ge(s_w, 16 * (NC + per))

                def body(m, j):
                    a = lagged(m, j, HID, U)
                    if a:
                        wait(pe, s_xnT[a.j], 16 * (a.m + 1))
                        lo = 0
                        for c, w in enumerate(f.shared):
                            n = (a.j * NC + c) % 2
                            wait(pe, s_hid, NC * a.i + c - 1)
                            mm = nc.tensor.matmul(psA[n][0:w, 0:TOK], w_in[:, 0, lo:lo + w], xnT[a.j][:], start=True, stop=True)
                            if f.gated:
                                mm = nc.tensor.matmul(psB[n][0:w, 0:TOK], w_in[:, 1, lo:lo + w], xnT[a.j][:], start=True, stop=True)
                            mm.then_inc(s_in, 1)
                            lo += w
                    a = lagged(m, j, ADD, U)
                    if a:
                        wait(pe, s_hid, NC * a.i + NC)
                        wait(pe, s_h, a.i)
                        for t in range(TT):
                            for c, w in enumerate(f.shared):
                                mm = nc.tensor.matmul(psY[0:R, t * D:(t + 1) * D], hid[a.j][0:w, c, t * R:(t + 1) * R], w_out[0:w, c, :],
                                                      start=(c == 0), stop=(c == NC - 1))
                        mm.then_inc(s_down, 1)
                turns(pe, U, ADD, body)

            @block.scalar
            def _(act):
                def body(m, j):
                    a = lagged(m, j, HID, U)
                    if a:
                        for c, w in enumerate(f.shared):
                            n = (a.j * NC + c) % 2
                            wait(act, s_in, NC * a.i + c + 1)
                            if f.gated:
                                wait(act, s_hid, NC * a.i + c - 1)
                                nc.scalar.activation(silu[n][0:w, :], psA[n][0:w, 0:TOK], f.act_shared).then_inc(s_act, 1)
                            else:
                                wait(act, s_down, a.i - 1)
                                nc.scalar.activation(hid[a.j][0:w, c, :], psA[n][0:w, 0:TOK], f.act_shared).then_inc(s_hid, 1)
                turns(act, U, ADD, body)

            @block.vector
            def _(dve):
                def body(m, j):
                    a = lagged(m, j, HID, U)
                    if a and f.gated:
                        for c, w in enumerate(f.shared):
                            n = (a.j * NC + c) % 2
                            wait(dve, s_act, NC * a.i + c + 1)
                            wait(dve, s_down, a.i - 1)
                            nc.vector.tensor_tensor(hid[a.j][0:w, c, :], silu[n][0:w, :], psB[n][0:w, 0:TOK], ALU.mult).then_inc(s_hid, 1)
                    a = lagged(m, j, PLACE, U)
                    if a:
                        wait(dve, s_pick, a.i)
                        nc.vector.tensor_tensor(rowf[:], tile_of(r.rank, a.i), r.counts[0:R], ALU.add).then_inc(s_row, 1)
                        wait(dve, s_posf, a.i)
                        chosen = tile_of(r.expert, a.i)[:, :, 0:K]
                        hot4 = hot[:].rearrange("p (t k) e -> p t k e", k=K)
                        for t in range(TT):
                            nc.vector.tensor_tensor(hot4[:, t], r.iota[:].unsqueeze(1).broadcast_to([R, K, E]),
                                                    chosen[:, t].unsqueeze(2).broadcast_to([R, K, E]), ALU.is_equal).then_inc(s_hot, 1)
                        wait(dve, s_hot, 3 * a.i + 3)
                        wait(dve, s_row, a.i + 1)
                        nc.vector.tensor_tensor(hot4, hot4, rowf[:].unsqueeze(2).broadcast_to([R, TT, K, E]), ALU.mult).then_inc(s_pick, 1)
                        wait(dve, s_pick, a.i + 1)
                        wait(dve, s_posall, a.i)
                        nc.vector.tensor_reduce(posf[:], hot[:], AX.X, ALU.add).then_inc(s_posf, 1)
                        wait(dve, s_posf, a.i + 1)
                        for t in range(TT):
                            wait(dve, s_sent[t], 16 * K * (a.i - 1))
                        nc.vector.tensor_copy(pos[a.j][:], posf[:]).then_inc(s_pos, 1)
                        nc.vector.tensor_copy(tile_of(r.pos, a.i).rearrange("p t k -> p (t k)"), posf[:]).then_inc(s_posall, 1)
                    a = lagged(m, j, ADD, U)
                    if a:
                        wait(dve, s_down, a.i + 1)
                        nc.vector.tensor_tensor(tile_of(g.h, a.i), psY[0:R, 0:TT * D].rearrange("p (t e) -> p t e", t=TT), tile_of(g.h, a.i),
                                                ALU.add).then_inc(s_h, 1)
                turns(dve, U, ADD, body)


def experts(nc, g, d, f, r):
    U = 4
    LOAD, TURN, UP, BACK, DOWN = 0, 2, 3, 4, 5
    xs, ys = d["xs" + str(f.layer)], d["ys" + str(f.layer)]
    I, C, G = f.I, f.C, f.G
    N = f.blocks // G
    with Phase(nc, f"exp{f.layer}") as ph:
        w = ph.sb("w", [128, f.E * f.W])
        x = [ph.sb(f"x{j}", [128, G, D]) for j in range(U)]
        xT = [ph.sb(f"xT{j}", [D, G * 128]) for j in range(2)]
        silu = [ph.sb(f"silu{j}", [128, G * I]) for j in range(2)]
        hid = [ph.sb(f"hid{j}", [128, G * I]) for j in range(2)]
        hidT = [ph.sb(f"hidT{j}", [128, G * I]) for j in range(2)]
        y = [ph.sb(f"y{j}", [128, G, D]) for j in range(U)]
        psX = [ph.ps(f"psX{j}", [128, 512]) for j in range(2)]
        psH = [ph.ps(f"psH{j}", [128, 2, 512]) for j in range(2)]
        psT = ph.ps("psT", [128, 512])
        psY = ph.ps("psY", [128, 512])
        s_w = ph.sem("weights_in")
        s_x = [ph.sem(f"x_in{j}") for j in range(U)]
        s_y_out = [ph.sem(f"y_out{j}") for j in range(U)]
        s_xturn, s_xT, s_up, s_silu, s_hid, s_hturn, s_hT, s_down, s_y = (ph.sem(n) for n in (
            "x_turned", "xT_written", "up", "silu", "hidden", "hidden_turned", "hiddenT", "down", "y_written"))
        if C == 1:
            h1, h3 = ([p[:].rearrange("p n (b c e) -> p (n b) c e", b=2, e=I)[:, :, k, :] for p in psH] for k in range(2))
        else:
            h1, h3 = ([p[:, k, :].unsqueeze(1) for p in psH] for k in range(2))
        src = d["exp" + str(f.layer)]
        visits = [-(-(N - j) // U) for j in range(U)]

        def by_block(tile):
            return tile[:].rearrange("p (b e) -> p b e", e=I)

        def each_group(eng, lag_max, body):
            for t in range(TT):
                turns(eng, U, lag_max, lambda m, j: body(t, t * N, m, j), N)

        def freed(base, a):
            return base if isinstance(a.i, int) and a.i < U else base + a.i - U + 1

        with nc.Block() as block:
            @block.sync
            def _(sp):
                for e in range(0, f.E, 8):
                    sp.dma_start(w[:, e * f.W:(e + 8) * f.W].rearrange("p (e w) -> p e w", w=f.W),
                                 src[e:e + 8].rearrange("e p w -> p e w")).then_inc(s_w, 16)

                def body(t, base, m, j):
                    a = lagged(m, j, LOAD, U, N)
                    if a:
                        wait(sp, s_xturn, freed(base, a))
                        sp.dma_start(x[a.j][:], xs[t][bass.ds(a.i * G * 128, G * 128), :].rearrange("(b p) e -> p b e", p=128)
                                     ).then_inc(s_x[a.j], 16)
                each_group(sp, DOWN, body)
                for j in range(U):
                    sp.wait_ge(s_y_out[j], 16 * TT * visits[j])

            @block.tensor
            def _(pe):
                pe.wait_ge(s_w, 16 * (f.E // 8))

                def weights(t, a):
                    _, owners = nc.values_load_multi_w_load_instructions(
                        r.expert_row[0:1, bass.ds(a.i * G + t * f.blocks, G)], engines=[mybir.EngineType.PE],
                        min_val=0, max_val=f.E - 1, skip_runtime_bounds_check_because="lists() clamps them to the last expert and counts from zero")
                    return [e * f.W for e in owners]

                def body(t, base, m, j):
                    a = lagged(m, j, TURN, U, N)
                    if a:
                        n = a.j % 2
                        wait(pe, s_x[a.j], 16 * (a.m + 1 + t * visits[a.j]))
                        wait(pe, s_xT, base + a.i - 1)
                        for b in range(G):
                            mm = nc.tensor.transpose(psX[n][:, b * 128:(b + 1) * 128], x[a.j][:, b, :], g.ident[:])
                        mm.then_inc(s_xturn, 1)
                    a = lagged(m, j, UP, U, N)
                    if a:
                        n = a.j % 2
                        at = weights(t, a)
                        wait(pe, s_xT, base + a.i + 1)
                        wait(pe, s_hid, base + a.i - 1)
                        if C == 1:
                            for b in range(G):
                                mm = nc.tensor.matmul(psH[n][:, b // 2, (b % 2) * 2 * I:(b % 2 + 1) * 2 * I], xT[n][:, b * 128:(b + 1) * 128],
                                                      w[:, bass.ds(at[b], 2 * I)], start=True, stop=True)
                        else:
                            for k in range(2):
                                mm = nc.tensor.matmul(psH[n][:, k, :], xT[n][:], w[:, bass.ds(at[0] + k * I, I)], start=True, stop=True)
                        mm.then_inc(s_up, 1)
                    a = lagged(m, j, BACK, U, N)
                    if a:
                        n = a.j % 2
                        wait(pe, s_hid, base + a.i + 1)
                        wait(pe, s_hT, base + a.i)
                        for c in range(G * C):
                            mm = nc.tensor.transpose(psT[:, c * 128:(c + 1) * 128], hid[n][:, c * 128:(c + 1) * 128], g.ident[:])
                        mm.then_inc(s_hturn, 1)
                    a = lagged(m, j, DOWN, U, N)
                    if a:
                        n = a.j % 2
                        at = weights(t, a)
                        wait(pe, s_hT, base + a.i + 1)
                        wait(pe, s_y, base + a.i)
                        for b in range(G):
                            for c in range(C):
                                mm = nc.tensor.matmul(psY[:, b * D:(b + 1) * D], hidT[n][:, (b * C + c) * 128:(b * C + c + 1) * 128],
                                                      w[:, bass.ds(at[b] + 2 * I + c * D, D)], start=(c == 0), stop=(c == C - 1))
                        mm.then_inc(s_down, 1)
                each_group(pe, DOWN, body)

            @block.scalar
            def _(act):
                def body(t, base, m, j):
                    a = lagged(m, j, TURN, U, N)
                    if a:
                        wait(act, s_xturn, base + a.i + 1)
                        wait(act, s_up, base + a.i - 1)
                        nc.scalar.copy(xT[a.j % 2][:], psX[a.j % 2][:, 0:G * 128]).then_inc(s_xT, 1)
                    a = lagged(m, j, UP, U, N)
                    if a:
                        wait(act, s_up, base + a.i + 1)
                        wait(act, s_hid, base + a.i - 1)
                        nc.scalar.activation(by_block(silu[a.j % 2]), h1[a.j % 2], ACT.Silu).then_inc(s_silu, 1)
                    a = lagged(m, j, DOWN, U, N)
                    if a:
                        wait(act, s_y, base + a.i + 1)
                        act.dma_start(ys[t][bass.ds(a.i * G * 128, G * 128), :].rearrange("(b p) e -> p b e", p=128),
                                      y[a.j][:]).then_inc(s_y_out[a.j], 16)
                each_group(act, DOWN, body)

            @block.vector
            def _(dve):
                def body(t, base, m, j):
                    a = lagged(m, j, UP, U, N)
                    if a:
                        n = a.j % 2
                        wait(dve, s_silu, base + a.i + 1)
                        wait(dve, s_hturn, base + a.i - 1)
                        nc.vector.tensor_tensor(by_block(hid[n]), by_block(silu[n]), h3[n], ALU.mult).then_inc(s_hid, 1)
                    a = lagged(m, j, BACK, U, N)
                    if a:
                        n = a.j % 2
                        wait(dve, s_hturn, base + a.i + 1)
                        wait(dve, s_down, base + a.i - 1)
                        nc.vector.tensor_copy(hidT[n][:], psT[:, 0:G * I]).then_inc(s_hT, 1)
                    a = lagged(m, j, DOWN, U, N)
                    if a:
                        wait(dve, s_down, base + a.i + 1)
                        wait(dve, s_y_out[a.j], 16 * (a.m + t * visits[a.j]))
                        nc.vector.tensor_copy(y[a.j][:].rearrange("p b e -> p (b e)"), psY[:, 0:G * D]).then_inc(s_y, 1)
                each_group(dve, DOWN, body)


def combine(nc, g, d, f, r):
    U = 2
    K = f.K
    ys = d["ys" + str(f.layer)]
    with Phase(nc, f"comb{f.layer}") as ph:
        got = [ph.sb(f"rows{j}", [R, K, TT, D]) for j in range(U)]
        pos = [ph.sb(f"pos{j}", [R, TT * K], I32) for j in range(U)]
        s_pos, s_add = ph.sem("pos"), ph.sem("added")
        s_got = g.got[f.layer]
        with nc.Block() as block:
            @block.gpsimd
            def _(pool):
                def body(m, j):
                    a = lagged(m, j, 0, U)
                    if a:
                        wait(pool, s_pos, a.i + 1)
                        stand(pool, g)
                        wait(pool, s_add, TT * K * (a.i - U + 1))
                        stand(pool, g)
                        for k in range(K):
                            for t in range(TT):
                                pool.indirect_dma_start(got[a.j][:, k, t, :], None, ys[t],
                                                        bass.IndirectOffsetOnAxis(ap=pos[a.j][:, t * K + k:t * K + k + 1], axis=0)
                                                        ).then_inc(s_got[a.j], 16)
                turns(pool, U, 1, body)

            @block.vector
            def _(dve):
                def body(m, j):
                    a = lagged(m, j, 0, U)
                    if a:
                        wait(dve, s_got[a.j], 16 * TT * K * a.m)
                        nc.vector.tensor_copy(pos[a.j][:], tile_of(r.pos, a.i).rearrange("p t k -> p (t k)")).then_inc(s_pos, 1)
                    a = lagged(m, j, 1, U)
                    if a:
                        wait(dve, s_got[a.j], 16 * TT * K * (a.m + 1))
                        for k in range(K):
                            for t in range(TT):
                                if k > 0:
                                    wait(dve, s_add, TT * K * a.i + TT * (k - 1) + t + 1)
                                at = bass.ds(a.i * TT + t, 1)
                                hh = g.h[:, at, :].rearrange("p o e -> p (o e)")
                                nc.vector.scalar_tensor_tensor(hh, got[a.j][:, k, t, :], r.top[:, at, k:k + 1].rearrange("p o e -> p (o e)"), hh,
                                                               ALU.mult, ALU.add).then_inc(s_add, 1)
                turns(dve, U, 1, body)


def ffn0(nc, g, d):
    ffn(nc, g, d, FFN0)


def ffn1(nc, g, d):
    ffn(nc, g, d, FFN1)


QK = 16
EX = 256
NCAT = EX // 128


def mix1(nc, g, d):
    U = 2
    STAT, NORM, STAT2, NORM2, UP = 0, 1, 1, 2, 3
    with Phase(nc, "mix") as ph:
        w = ph.sb("expand", [D, 2 * QK + 2 * EX])
        w_qk = ph.sb("expand_qk", [D, 2, 128])
        stats = [ph.sb(f"stats{j}", [R, TT, 6]) for j in range(U)]
        mv = [ph.sb(f"mv{j}", [R, TT, 2]) for j in range(U)]
        veps = [ph.sb(f"veps{j}", [R, TT]) for j in range(U)]
        rstd = [ph.sb(f"rstd{j}", [R, TT]) for j in range(U)]
        x = [ph.sb(f"x{j}", [R, TT, D]) for j in range(U)]
        nx = [ph.sb(f"nx{j}", [R, TT, D]) for j in range(U)]
        nxT = [ph.sb(f"nxT{j}", [D, TOK]) for j in range(U)]
        qkT = [ph.sb(f"qkT{j}", [D, 2, TOK]) for j in range(U)]
        gelu = [ph.sb(f"gelu{j}", [R, TT, EX]) for j in range(U)]
        gated = [ph.sb(f"gated{j}", [R, TT, EX]) for j in range(U)]
        psT = ph.ps("psT", [128, 512])
        psQK = ph.ps("psQK", [128, 2, 512])
        psE = ph.ps("psE", [128, TT, 512])
        s_w, s_zero, s_wqk = ph.sem("weights_in"), ph.sem("zero_set"), ph.sem("qk_weights")
        s_stats, s_mv, s_veps, s_rstd, s_xn = (ph.sem(n) for n in ("stats", "mv", "veps", "rstd", "normalised"))
        s_turned, s_nxT, s_qk, s_qkT = (ph.sem(n) for n in ("turned", "nxT_written", "qk_multiplied", "qkT_written"))
        s_up, s_gelu, s_gated = ph.sem("expanded"), ph.sem("gelu"), ph.sem("gated")
        s_x_out, s_qk_out, s_g_out = ([ph.sem(f"{n}_out{j}") for j in range(U)] for n in ("x", "qk", "gated"))

        def seq(n, i):
            if n == 0:
                return 2 * i - 1 if not isinstance(i, int) or i > 0 else 0
            v = 2 * i + 2
            return min(v, 2 * B - 1) if isinstance(v, int) else v

        with nc.Block() as block:
            @block.sync
            def _(sp):
                sp.dma_start(w[:], d["expand"]).then_inc(s_w, 16)

                def body(m, j):
                    a = lagged(m, j, NORM, U)
                    if a:
                        wait(sp, s_xn, 3 * seq(0, a.i) + 3)
                        sp.dma_start(d["xn"][bass.ds(a.i, 1)].rearrange("o p t e -> (o p) t e"), x[a.j][:]).then_inc(s_x_out[a.j], 16)
                    a = lagged(m, j, UP, U)
                    if a:
                        wait(sp, s_qkT, a.i + 1)
                        sp.dma_start(d["qkT"][bass.ds(a.i, 1)].rearrange("o e n t -> (o e) n t"), qkT[a.j][0:QK]).then_inc(s_qk_out[a.j], 16)
                        wait(sp, s_gated, a.i + 1)
                        sp.dma_start(d["gated"][bass.ds(a.i, 1)].rearrange("o p t e -> (o p) t e"), gated[a.j][:]).then_inc(s_g_out[a.j], 16)
                turns(sp, U, UP, body)
                for j in range(U):
                    for s in (s_x_out[j], s_qk_out[j], s_g_out[j]):
                        sp.wait_ge(s, 16 * B // U)

            @block.gpsimd
            def _(pool):
                pool.memset(w_qk[:], 0.0).then_inc(s_zero, 1)
                pool.wait_ge(s_zero, 1)
                pool.wait_ge(s_w, 16)
                for n in range(2):
                    pool.tensor_copy(w_qk[:, n, 0:QK], w[:, n * QK:(n + 1) * QK]).then_inc(s_wqk, 1)

                def rstd_of(n, a):
                    p = seq(n, a.i)
                    wait(pool, s_mv, 3 * p + 3)
                    wait(pool, s_rstd, p)
                    stand(pool, g)
                    pool.tensor_scalar(veps[n][:], mv[n][:, :, 1], EPS, None, ALU.add).then_inc(s_veps, 1)
                    wait(pool, s_veps, p + 1)
                    pool.tensor_tensor(rstd[n][:], veps[n][:], g.minus_half[0:R, 0:TT], ALU.pow).then_inc(s_rstd, 1)

                def body(m, j):
                    a = lagged(m, j, STAT, U)
                    if a:
                        rstd_of(0, a)
                    a = lagged(m, j, STAT2, U)
                    if a:
                        rstd_of(1, a)
                turns(pool, U, UP, body)

            @block.vector
            def _(dve):
                def chain(n, a, src, dst, free):
                    p = seq(n, a.i)
                    for t in range(TT):
                        nc.vector.bn_stats(stats[n][:, t, :], src(t)).then_inc(s_stats, 1)
                    wait(dve, s_stats, 3 * p + 3)
                    stand(dve, g)
                    for t in range(TT):
                        nc.vector.bn_aggr(mv[n][:, t, :], stats[n][:, t, :]).then_inc(s_mv, 1)
                    wait(dve, s_rstd, p + 1)
                    free()
                    for t in range(TT):
                        nc.vector.tensor_scalar(dst[:, t, :], src(t), mv[n][:, t, 0:1], rstd[n][:, t:t + 1], ALU.subtract, ALU.mult).then_inc(s_xn, 1)

                def body(m, j):
                    a = lagged(m, j, STAT, U)
                    if a:
                        def free():
                            wait(dve, s_x_out[a.j], 16 * a.m)
                            wait(dve, s_xn, 3 * seq(1, a.i - 2) + 3 if not isinstance(a.i, int) or a.i > 1 else 0)
                        chain(0, a, lambda t: g.h[:, bass.ds(a.i * TT + t, 1), :].rearrange("p o e -> p (o e)"), x[a.j], free)
                    a = lagged(m, j, STAT2, U)
                    if a:
                        wait(dve, s_xn, 3 * seq(0, a.i) + 3)
                        stand(dve, g)
                        chain(1, a, lambda t: x[a.j][:, t, :], nx[a.j],
                              lambda: wait(dve, s_turned, a.i - 1))
                    a = lagged(m, j, UP, U)
                    if a:
                        wait(dve, s_gelu, a.i + 1)
                        wait(dve, s_g_out[a.j], 16 * a.m)
                        nc.vector.tensor_tensor(gated[a.j][:], gelu[a.j][:], psE[0:R, :, 0:EX], ALU.mult).then_inc(s_gated, 1)
                turns(dve, U, UP, body)

            @block.tensor
            def _(pe):
                pe.wait_ge(s_w, 16)
                pe.wait_ge(s_wqk, 2)

                def body(m, j):
                    a = lagged(m, j, NORM2, U)
                    if a:
                        p = seq(1, a.i)
                        wait(pe, s_xn, 3 * p + 3)
                        wait(pe, s_nxT, a.i)
                        for t in range(TT):
                            mm = nc.tensor.transpose(psT[:, t * R:(t + 1) * R], nx[a.j][:, t, :], g.ident[0:R, 0:R])
                        mm.then_inc(s_turned, 1)
                    a = lagged(m, j, UP, U)
                    if a:
                        wait(pe, s_nxT, a.i + 1)
                        wait(pe, s_qkT, a.i)
                        for n in range(2):
                            mm = nc.tensor.matmul(psQK[:, n, 0:TOK], w_qk[:, n, :], nxT[a.j][:], start=True, stop=True)
                        mm.then_inc(s_qk, 1)
                        wait(pe, s_gated, a.i)
                        for t in range(TT):
                            mm = nc.tensor.matmul(psE[0:R, t, :], nxT[a.j][:, t * R:(t + 1) * R], w[:, 2 * QK:], start=True, stop=True)
                        mm.then_inc(s_up, 1)
                turns(pe, U, UP, body)

            @block.scalar
            def _(act):
                def body(m, j):
                    a = lagged(m, j, NORM2, U)
                    if a:
                        wait(act, s_turned, a.i + 1)
                        wait(act, s_up, a.i - 1)
                        nc.scalar.copy(nxT[a.j][:], psT[:, 0:TOK]).then_inc(s_nxT, 1)
                    a = lagged(m, j, UP, U)
                    if a:
                        wait(act, s_qk, a.i + 1)
                        wait(act, s_qk_out[a.j], 16 * a.m)
                        nc.scalar.copy(qkT[a.j][:], psQK[:, :, 0:TOK]).then_inc(s_qkT, 1)
                        wait(act, s_up, a.i + 1)
                        wait(act, s_gated, a.i - 1)
                        nc.scalar.activation(gelu[a.j][:], psE[0:R, :, EX:2 * EX], ACT.Gelu).then_inc(s_gelu, 1)
                turns(act, U, UP, body)


def attention1(nc, g, d):
    U = 2
    LOAD, SCORE, TURN, MIX, CAT, OUT = 0, 1, 2, 3, 4, 5
    PAIRS = [(t, c) for t in range(TT) for c in range(t + 1)]
    with Phase(nc, "at1") as ph:
        proj = ph.sb("project", [128, NCAT, D])
        mult = ph.sb("bias_mult", [R, 1])
        rel = ph.sb("rel", [R, TT, TOK])
        bias = ph.sb("bias", [R, TT, TOK])
        q = [ph.sb(f"qk{j}", [D, 2, TOK]) for j in range(U)]
        x = [ph.sb(f"x{j}", [R, TT, D]) for j in range(U)]
        gated = [ph.sb(f"gated{j}", [R, TT, EX]) for j in range(U)]
        sc = [ph.sb(f"scores{j}", [R, TT, TOK]) for j in range(U)]
        negmax = [ph.sb(f"negmax{j}", [R, TT]) for j in range(U)]
        sums = [ph.sb(f"sums{j}", [R, TT]) for j in range(U)]
        recip = [ph.sb(f"recip{j}", [R, TT]) for j in range(U)]
        probs = [ph.sb(f"probs{j}", [R, TT, TOK]) for j in range(U)]
        pT = [ph.sb(f"probsT{j}", [R, len(PAIRS), R]) for j in range(U)]
        attn = [ph.sb(f"attn{j}", [R, TT, D]) for j in range(U)]
        catT = [ph.sb(f"catT{j}", [128, NCAT, TOK]) for j in range(U)]
        psS = ph.ps("psS", [128, TT, 512])
        psP = ph.ps("psP", [128, 2, 512])
        psA = ph.ps("psA", [128, 512])
        psC = ph.ps("psC", [128, 2, 512])
        psO = psA
        s_w, s_rel, s_bias, s_mask = ph.sem("weights_in"), ph.sem("rel_set"), ph.sem("bias_set"), ph.sem("masked")
        s_zero = ph.sem("zero_set")
        s_q = [ph.sem(f"qk_in{j}") for j in range(U)]
        s_x, s_g = ([ph.sem(f"{n}_in{j}") for j in range(U)] for n in ("x", "gated"))
        s_scored, s_sc, s_max, s_exp, s_recip = (ph.sem(n) for n in ("scored", "biased", "max", "exp", "recip"))
        s_pturn, s_pT, s_mixed, s_attn, s_cturn, s_catT, s_out, s_add, s_h = (ph.sem(n) for n in (
            "probs_turned", "probsT", "mixed", "attn", "cat_turned", "catT", "projected", "x_added", "h_added"))

        with nc.Block() as block:
            @block.sync
            def _(sp):
                sp.dma_start(proj[:], d["project"].rearrange("(c p) e -> p c e", p=128)).then_inc(s_w, 16)
                sp.dma_start(mult[:], d["bias_mult"].broadcast_to([R, 1])).then_inc(s_w, 16)
                sp.wait_ge(s_zero, U)

                def body(m, j):
                    a = lagged(m, j, LOAD, U)
                    if a:
                        wait(sp, s_scored, a.i - 1)
                        sp.dma_start(q[a.j][0:QK], d["qkT"][bass.ds(a.i, 1)].rearrange("o e n t -> (o e) n t")).then_inc(s_q[a.j], 16)
                    a = lagged(m, j, TURN, U)
                    if a:
                        wait(sp, s_cturn, a.i - 1)
                        sp.dma_start(gated[a.j][:], d["gated"][bass.ds(a.i, 1)].rearrange("o p t e -> (o p) t e")).then_inc(s_g[a.j], 16)
                    a = lagged(m, j, MIX, U)
                    if a:
                        wait(sp, s_h, a.i - 1)
                        sp.dma_start(x[a.j][:], d["xn"][bass.ds(a.i, 1)].rearrange("o p t e -> (o p) t e")).then_inc(s_x[a.j], 16)
                turns(sp, U, OUT, body)

            @block.gpsimd
            def _(pool):
                pool.iota(rel[:], pattern=[[-R, TT], [1, TOK]], base=0, channel_multiplier=-1,
                          allow_small_or_imprecise_dtypes=True).then_inc(s_rel, 1)
                for j in range(U):
                    pool.memset(q[j][:], 0.0).then_inc(s_zero, 1)
                pool.wait_ge(s_bias, 1)
                pool.affine_select(out=bias[:], in_=bias[:], compare_op=ALU.is_ge, fill=NEG, base=0,
                                   pattern=[[R, TT], [-1, TOK]], channel_multiplier=1).then_inc(s_mask, 1)

                def body(m, j):
                    a = lagged(m, j, OUT, U)
                    if a:
                        wait(pool, s_add, a.i + 1)
                        pool.tensor_tensor(tile_of(g.h, a.i), tile_of(g.h, a.i), x[a.j][:], ALU.add).then_inc(s_h, 1)
                turns(pool, U, OUT, body)

            @block.tensor
            def _(pe):
                pe.wait_ge(s_w, 32)
                pe.wait_ge(s_zero, U)

                def body(m, j):
                    a = lagged(m, j, OUT, U)
                    if a:
                        wait(pe, s_catT, a.i + 1)
                        wait(pe, s_add, a.i)
                        n = a.i + OUT - MIX
                        wait(pe, s_attn, min(n, B) if isinstance(n, int) else n)
                        for t in range(TT):
                            for c in range(NCAT):
                                mm = nc.tensor.matmul(psO[0:R, t * D:(t + 1) * D], catT[a.j][:, c, t * R:(t + 1) * R], proj[:, c, :],
                                                      start=(c == 0), stop=(c == NCAT - 1))
                        mm.then_inc(s_out, 1)
                    a = lagged(m, j, SCORE, U)
                    if a:
                        wait(pe, s_q[a.j], 16 * (a.m + 1))
                        wait(pe, s_sc, 3 * a.i)
                        for t in range(TT):
                            n = (t + 1) * R
                            mm = nc.tensor.matmul(psS[0:R, t, 0:n], q[a.j][:, 0, t * R:(t + 1) * R], q[a.j][:, 1, 0:n], start=True, stop=True)
                        mm.then_inc(s_scored, 1)
                    a = lagged(m, j, TURN, U)
                    if a:
                        wait(pe, s_exp, 3 * a.i + 3)
                        wait(pe, s_pT, a.i)
                        for n, (t, c) in enumerate(PAIRS):
                            mm = nc.tensor.transpose(psP[0:R, n // 3, (n % 3) * R:(n % 3 + 1) * R], probs[a.j][:, t, c * R:(c + 1) * R], g.ident[0:R, 0:R])
                        mm.then_inc(s_pturn, 1)
                    a = lagged(m, j, CAT, U)
                    if a:
                        wait(pe, s_attn, a.i + 1)
                        wait(pe, s_catT, a.i)
                        for t in range(TT):
                            nc.tensor.transpose(psC[:, 0, t * R:(t + 1) * R], gated[a.j][:, t, 0:128], g.ident[0:R, 0:R])
                            mm = nc.tensor.transpose(psC[:, 1, t * R:(t + 1) * R], attn[a.j][:, t, :], g.ident[0:R, 0:R])
                        mm.then_inc(s_cturn, 1)
                    a = lagged(m, j, MIX, U)
                    if a:
                        wait(pe, s_pT, a.i + 1)
                        wait(pe, s_g[a.j], 16 * (a.m + 1))
                        n = a.i - OUT + MIX + 1
                        wait(pe, s_attn, a.i)
                        wait(pe, s_add, n)
                        for t in range(TT):
                            for c in range(t + 1):
                                mm = nc.tensor.matmul(psA[0:R, t * D:(t + 1) * D], pT[a.j][:, PAIRS.index((t, c)), :], gated[a.j][:, c, 128:256],
                                                      start=(c == 0), stop=(c == t))
                        mm.then_inc(s_mixed, 1)
                turns(pe, U, OUT, body)

            @block.scalar
            def _(act):
                act.wait_ge(s_w, 32)
                act.wait_ge(s_rel, 1)
                nc.scalar.activation(bias[:], rel[:], ACT.Sigmoid, bias=mult[:, 0:1]).then_inc(s_bias, 1)

                def body(m, j):
                    a = lagged(m, j, TURN, U)
                    if a:
                        wait(act, s_max, 3 * a.i + 3)
                        wait(act, s_pturn, a.i - 1)
                        wait(act, s_recip, a.i - 1)
                        for t in range(TT):
                            n = (t + 1) * R
                            nc.scalar.activation(probs[a.j][:, t, 0:n], sc[a.j][:, t, 0:n], ACT.Exp, bias=negmax[a.j][:, t:t + 1],
                                                 accum_out=sums[a.j][:, t:t + 1]).then_inc(s_exp, 1)
                        wait(act, s_pturn, a.i + 1)
                        wait(act, s_mixed, a.i - 1)
                        nc.scalar.copy(pT[a.j][:].rearrange("p (b n) r -> p b (n r)", b=2), psP[0:R, :, 0:3 * R]).then_inc(s_pT, 1)
                    a = lagged(m, j, CAT, U)
                    if a:
                        wait(act, s_cturn, a.i + 1)
                        wait(act, s_out, a.i - 1)
                        nc.scalar.copy(catT[a.j][:], psC[:, :, 0:TOK]).then_inc(s_catT, 1)
                turns(act, U, OUT, body)

            @block.vector
            def _(dve):
                dve.wait_ge(s_mask, 1)

                def body(m, j):
                    a = lagged(m, j, OUT, U)
                    if a:
                        wait(dve, s_out, a.i + 1)
                        wait(dve, s_x[a.j], 16 * (a.m + 1))
                        nc.vector.tensor_tensor(x[a.j][:], psO[0:R, 0:TT * D].rearrange("p (t e) -> p t e", t=TT), x[a.j][:], ALU.add).then_inc(s_add, 1)
                    a = lagged(m, j, SCORE, U)
                    if a:
                        wait(dve, s_scored, a.i + 1)
                        wait(dve, s_exp, 3 * (a.i - 1))
                        for t in range(TT):
                            n = (t + 1) * R
                            nc.vector.scalar_tensor_tensor(sc[a.j][:, t, 0:n], psS[0:R, t, 0:n], 0.25, bias[:, t, 0:n], ALU.mult, ALU.add).then_inc(s_sc, 1)
                        for t in range(TT):
                            n = (t + 1) * R
                            wait(dve, s_sc, 3 * a.i + t + 1)
                            nc.vector.tensor_reduce(negmax[a.j][:, t:t + 1], sc[a.j][:, t, 0:n], AX.X, ALU.max, negate=True).then_inc(s_max, 1)
                    a = lagged(m, j, MIX, U)
                    if a:
                        wait(dve, s_exp, 3 * a.i + 3)
                        wait(dve, s_attn, a.i - 1)
                        nc.vector.reciprocal(recip[a.j][:], sums[a.j][:]).then_inc(s_recip, 1)
                        wait(dve, s_recip, a.i + 1)
                        wait(dve, s_mixed, a.i + 1)
                        wait(dve, s_cturn, a.i - 1)
                        nc.vector.tensor_tensor(attn[a.j][:], psA[0:R, 0:TT * D].rearrange("p (t e) -> p t e", t=TT),
                                                recip[a.j][:].unsqueeze(2).broadcast_to([R, TT, D]), ALU.mult).then_inc(s_attn, 1)
                turns(dve, U, OUT, body)



PHASES = (embed, attention0, ffn0, mix1, attention1, ffn1)


def program(nc, d, upto=99):
    ctx = ExitStack()
    with ctx:
        g = Shared()
        g.h = ctx.enter_context(nc.sbuf_tensor("h", [R, NTILE, D], F32))
        g.ident = ctx.enter_context(nc.sbuf_tensor("ident", [128, 128], F32))
        g.ident16 = ctx.enter_context(nc.sbuf_tensor("ident16", [128, 128], BF16))
        g.minus_half = ctx.enter_context(nc.sbuf_tensor("minus_half", [128, 4], F32))
        g.stand = ctx.enter_context(nc.semaphore("stand"))
        g.blanked = ctx.enter_context(nc.semaphore("rows_blanked"))
        g.sent = [[ctx.enter_context(nc.semaphore(f"sent{layer}_{t}")) for t in range(TT)] for layer in range(2)]
        g.got = [[ctx.enter_context(nc.semaphore(f"rows_in{layer}_{j}")) for j in range(2)] for layer in range(2)]
        scratch(nc, d)
        constants(nc, g)
        for n, phase in enumerate(PHASES):
            if n < upto:
                phase(nc, g, d)
        store(nc, g, d)


def store(nc, g, d):
    with Phase(nc, "store") as ph:
        s_out = ph.sem("out_stored")
        with nc.Block() as block:
            @block.sync
            def _(sp):
                sp.dma_start(d["out"].rearrange("b (t p) e -> p (b t) e", p=R), g.h[:]).then_inc(s_out, 16)
                sp.wait_ge(s_out, 16)


def scratch(nc, d):
    def dram(name, shape, dt=F32):
        return nc.dram_tensor(name, shape, dt, kind="Internal").ap()
    d["xn"] = dram("xn_scratch", (B, R, TT, D))
    d["vone"] = dram("v_scratch", (B, R, TT, NH, 2 * HD))
    d["q_parts"] = dram("q_scratch", (B, NH, HD, 3, TOK), BF16)
    d["xnT"] = dram("xnT_scratch", (B, D, TOK))
    d["owner"] = dram("owner_scratch", (TT * max(FFN0.blocks, FFN1.blocks),), I32)
    for f in (FFN0, FFN1):
        d["xs" + str(f.layer)] = [dram(f"xs{f.layer}_{t}", (f.rows, D)) for t in range(TT)]
        d["ys" + str(f.layer)] = [dram(f"ys{f.layer}_{t}", (f.rows, D)) for t in range(TT)]
    d["qkT"] = dram("qkT_scratch", (B, QK, 2, TOK))
    d["gated"] = dram("gated_scratch", (B, R, TT, EX))
    d["maxima"] = dram("maxima_scratch", (B, 3 * NH, TOK), BF16)
    d["k_parts"] = dram("k_scratch", (B, NH, HD, 3, TOK), BF16)


def laid_out(v):
    def t(a):
        return np.ascontiguousarray(np.swapaxes(np.asarray(a), -1, -2))
    x = np.asarray(v["x"])
    n = x.shape[-1] // 16
    px = x.reshape(B, 3, n, 16, n, 16).transpose(0, 1, 3, 5, 2, 4).reshape(B, KC, 128, NP)
    out = {
        "patches": px.transpose(0, 2, 1, 3),
        "w_tok": t(v["L0_tok_w"]).reshape(KC, 128, D).transpose(1, 0, 2),
        "b_tok": v["L0_tok_b"],
        "txt": v["txt"],
        "wq": t(v["L0_attn_W_q"]), "wk": t(v["L0_attn_W_k"]), "wv": t(v["L0_attn_W_v"]), "wo": t(v["L0_attn_W_o"]),
        "gamma": v["L0_attn_ln_gamma"], "beta": v["L0_attn_ln_beta"],
        "gate0": t(v["L0_ffn_gate_w"]),
        "exp0": np.concatenate([np.asarray(v["L0_ffn_w1"]), np.asarray(v["L0_ffn_w3"]), np.asarray(v["L0_ffn_w2"])], axis=2),
        "sw1_0": v["L0_ffn_sw1"], "sw3_0": v["L0_ffn_sw3"], "sw2_0": v["L0_ffn_sw2"],
        "expand": v["L1_attn_expand"], "project": v["L1_attn_project"],
        "bias_mult": np.asarray(v["L1_attn_position_bias_mult"]).reshape(1, 1),
        "gate1": t(v["L1_ffn_gate_w"]),
        "exp1": np.concatenate([t(v["L1_ffn_w1"]), t(v["L1_ffn_w3"]),
                                t(v["L1_ffn_w2"]).reshape(8, 4, 128, D).transpose(0, 2, 1, 3).reshape(8, 128, 512)], axis=2),
        "sw1_1": t(v["L1_ffn_sw1"]), "sw2_1": t(v["L1_ffn_sw2"]),
    }
    return {k: np.ascontiguousarray(a) for k, a in out.items()}


UPTO = 99


def kernel(**inputs):
    import concourse.bacc as bacc
    from concourse.bass_utils import run_bass_kernel_spmd

    nc = bacc.Bacc("TRN2", target_bir_lowering=False, num_devices=1)
    arrays = laid_out(inputs)
    d = Dram({name: nc.dram_tensor(f"in_{name}", a.shape, mybir.dt.from_np(a.dtype), kind="ExternalInput").ap()
              for name, a in arrays.items()})
    d["out"] = nc.dram_tensor("out_h", (B, TOK, D), F32, kind="ExternalOutput").ap()
    program(nc, d, UPTO)
    r = run_bass_kernel_spmd(nc, [{f"in_{k}": a for k, a in arrays.items()}], core_ids=[0])
    return r.results[0]["out_h"]
```

```python
from contextlib import ExitStack

import numpy as np
import concourse.bass as bass
from concourse import mybir

F32 = mybir.dt.float32
BF16 = mybir.dt.bfloat16
I32 = mybir.dt.int32
U32 = mybir.dt.uint32
ALU = mybir.AluOpType
ACT = mybir.ActivationFunctionType
AX = mybir.AxisListType

D = 128
B = 32
TOK = 324
TT = 3
R = TOK // TT
NP = 196
KC = 6
NH = 8
HD = 16
EPS = 1e-5
NTILE = B * TT
QPART = (0, 0, 1, 1, 0, 2)
KPART = (0, 1, 0, 1, 2, 0)
NB = len(QPART)
SK = NB * HD
NEG = -1.0e30


def wait(eng, sem, value):
    if isinstance(value, int) and value <= 0:
        return
    eng.wait_ge(sem, value)


def stand(eng, g):
    eng.sem_inc(g.stand, 1)


def turns(eng, slots, lag_max, body, count=B):
    first = (-(-lag_max // slots) + 1) * slots
    for it in range(first):
        body(it // slots, it % slots)
    with eng.Fori(first // slots, count // slots) as m:
        for j in range(slots):
            body(m, j)
    for it in range(count // slots * slots, count + lag_max):
        body(it // slots, it % slots)


def lagged(m, j, lag, slots, count=B):
    back, slot = divmod(j - lag, slots)
    visit = m + back
    i = visit * slots + slot
    if isinstance(i, int) and not 0 <= i < count:
        return None
    return Image(j=slot, m=visit, i=i)


class Image:

    def __init__(self, j, m, i):
        self.j, self.m, self.i = j, m, i


class Shared:
    pass


class Dram(dict):
    pass


class Phase:

    def __init__(self, nc, name):
        self.nc, self.name, self.ctx, self.sems = nc, name, ExitStack(), []

    def sb(self, name, shape, dt=F32):
        return self.ctx.enter_context(self.nc.sbuf_tensor(f"{self.name}_{name}", shape, dt))

    def ps(self, name, shape, dt=F32):
        return self.ctx.enter_context(self.nc.psum_tensor(f"{self.name}_{name}", shape, dt))

    def sem(self, name):
        self.sems.append(self.ctx.enter_context(self.nc.semaphore(f"{self.name}_{name}")))
        return self.sems[-1]

    def __enter__(self):
        return self

    def __exit__(self, *a):
        if self.sems and a[0] is None:
            with self.nc.Block() as block:
                @block.gpsimd
                def _(pool):
                    for s in self.sems:
                        pool.sem_clear(s)
        return self.ctx.__exit__(*a)


def tile_of(h, i, k=0, n=TT):
    return h[:, bass.ds(i * TT + k, n), :]


def constants(nc, g):
    with Phase(nc, "const") as ph:
        s_set = ph.sem("set")
        with nc.Block() as block:
            @block.gpsimd
            def _(pool):
                pool.memset(g.minus_half[:], -0.5).then_inc(s_set, 1)
                pool.memset(g.ident[:], 0.0).then_inc(s_set, 1)
                pool.wait_ge(s_set, 2)
                pool.affine_select(out=g.ident[:], in_=g.ident[:], compare_op=ALU.not_equal, fill=1.0, base=0,
                                   pattern=[[-1, 128]], channel_multiplier=1).then_inc(s_set, 1)
                pool.wait_ge(s_set, 3)
                pool.tensor_copy(g.ident16[:], g.ident[:]).then_inc(s_set, 1)


def embed(nc, g, d):
    U = 4
    with Phase(nc, "emb") as ph:
        w_tok = ph.sb("w_tok", [128, KC, D])
        b_tok = ph.sb("b_tok", [R, D])
        wq, wk, wv = (ph.sb(n, [D, D]) for n in ("wq", "wk", "wv"))
        patches = [ph.sb(f"patches{j}", [128, KC, NP]) for j in range(U)]
        stats = [ph.sb(f"stats{j}", [R, TT, 6]) for j in range(U)]
        mv = [ph.sb(f"mv{j}", [R, TT, 2]) for j in range(U)]
        veps = [ph.sb(f"veps{j}", [R, TT]) for j in range(U)]
        rstd = [ph.sb(f"rstd{j}", [R, TT]) for j in range(U)]
        xn = [ph.sb(f"xn{j}", [R, TT, D]) for j in range(U)]
        xnT = [ph.sb(f"xnT{j}", [D, TOK]) for j in range(U)]
        part = [[ph.sb(f"{n}part{j}", [D, 3, TOK], BF16) for j in range(U)] for n in "qk"]
        rest = [[ph.sb(f"{n}rest{j}", [D, TOK]) for j in range(U)] for n in "qk"]
        vone = [ph.sb(f"v_{j}", [R, TT, NH, 2 * HD]) for j in range(U)]
        psH = [ph.ps(f"psH{j}", [128, 512]) for j in range(2)]
        psT = ph.ps("psT", [128, 512])
        psQK = [ph.ps(f"ps{n}", [128, 512]) for n in "qk"]
        psV = ph.ps("psV", [128, 512])
        s_w = ph.sem("weights_in")
        s_txt = ph.sem("text_in")
        s_patches = [ph.sem(f"patches_in{j}") for j in range(U)]
        s_patched = ph.sem("patched")
        s_h = ph.sem("h_written")
        s_stats, s_mv, s_veps, s_rstd, s_xn = (ph.sem(n) for n in ("stats", "mv", "veps", "rstd", "xn_written"))
        s_turned, s_xnT = ph.sem("turned"), ph.sem("xnT_written")
        s_qk, s_v = ph.sem("qk_projected"), ph.sem("v_projected")
        s_part1, s_rest, s_part2, s_part3, s_vone = (ph.sem(n) for n in ("part1", "rest", "part2", "part3", "vone"))
        s_ones = ph.sem("ones_set")
        s_xn_out = [ph.sem(f"xn_out{j}") for j in range(U)]
        s_qk_out = [ph.sem(f"qk_out{j}") for j in range(U)]
        s_v_out = [ph.sem(f"v_out{j}") for j in range(U)]
        LOAD, PATCH, LN, PR = 0, 2, 3, 4

        with nc.Block() as block:
            @block.sync
            def _(sp):
                for dst, src in ((w_tok[:], d["w_tok"]), (b_tok[:], d["b_tok"].partition_broadcast(R)),
                                 (wq[:], d["wq"]), (wk[:], d["wk"]), (wv[:], d["wv"])):
                    sp.dma_start(dst, src).then_inc(s_w, 16)
                n_mid = 2 * R - NP
                mid = g.h[R - n_mid:R, :, :].rearrange("p (b t) e -> p b t e", t=TT)[:, :, 1, :]
                last = g.h[:, :, :].rearrange("p (b t) e -> p b t e", t=TT)[:, :, 2, :]
                sp.dma_start(mid, d["txt"][:, 0:n_mid, :].rearrange("b p e -> p b e")).then_inc(s_txt, 16)
                sp.dma_start(last, d["txt"][:, n_mid:128, :].rearrange("b p e -> p b e")).then_inc(s_txt, 16)

                def body(m, j):
                    a = lagged(m, j, LOAD, U)
                    if a:
                        wait(sp, s_patched, a.i - U + 1)
                        sp.dma_start(patches[a.j][:], d["patches"][bass.ds(a.i, 1)].rearrange("o p c n -> (o p) c n")).then_inc(s_patches[a.j], 16)
                    a = lagged(m, j, LN, U)
                    if a:
                        wait(sp, s_xn, 3 * a.i + 3)
                        sp.dma_start(d["xn"][bass.ds(a.i, 1)].rearrange("o p t e -> (o p) t e"), xn[a.j][:]).then_inc(s_xn_out[a.j], 16)
                    a = lagged(m, j, PR, U)
                    if a:
                        wait(sp, s_vone, a.i + 1)
                        sp.dma_start(d["vone"][bass.ds(a.i, 1)].rearrange("o p t h e -> (o p) t h e"), vone[a.j][:]).then_inc(s_v_out[a.j], 16)
                        wait(sp, s_part1, 2 * a.i + 2)
                        wait(sp, s_part2, 2 * a.i + 2)
                        wait(sp, s_part3, 2 * a.i + 2)
                        for n, dst in enumerate((d["q_parts"], d["k_parts"])):
                            sp.dma_start(dst[bass.ds(a.i, 1)].rearrange("o h e a t -> (o h e) a t"), part[n][a.j][:]).then_inc(s_qk_out[a.j], 16)
                turns(sp, U, PR, body)
                for j in range(U):
                    sp.wait_ge(s_xn_out[j], 16 * B // U)
                    sp.wait_ge(s_v_out[j], 16 * B // U)
                    sp.wait_ge(s_qk_out[j], 32 * B // U)

            @block.tensor
            def _(pe):
                pe.wait_ge(s_w, 80)

                def body(m, j):
                    a = lagged(m, j, PR, U)
                    if a:
                        wait(pe, s_xnT, a.i + 1)
                        wait(pe, s_rest, 2 * a.i)
                        for n, w in enumerate((wq, wk)):
                            nc.tensor.matmul(psQK[n][:, 0:TOK], w[:], xnT[a.j][:], start=True, stop=True).then_inc(s_qk, 1)
                        wait(pe, s_vone, a.i)
                        for t in range(TT):
                            mm = nc.tensor.matmul(psV[0:R, t * D:(t + 1) * D], xnT[a.j][:, t * R:(t + 1) * R], wv[:],
                                                  start=True, stop=True)
                        mm.then_inc(s_v, 1)
                    a = lagged(m, j, PATCH, U)
                    if a:
                        pe.wait_ge(s_patches[a.j], 16 * (a.m + 1))
                        wait(pe, s_h, 2 * a.i - 2)
                        for t, n in enumerate((R, NP - R)):
                            for c in range(KC):
                                mm = nc.tensor.matmul(psH[a.j % 2][0:n, t * D:(t + 1) * D], patches[a.j][:, c, t * R:t * R + n],
                                                      w_tok[:, c, :], start=(c == 0), stop=(c == KC - 1))
                        mm.then_inc(s_patched, 1)
                    a = lagged(m, j, LN, U)
                    if a:
                        wait(pe, s_xn, 3 * a.i + 3)
                        wait(pe, s_xnT, a.i)
                        for t in range(TT):
                            mm = nc.tensor.transpose(psT[:, t * R:(t + 1) * R], xn[a.j][:, t, :], g.ident[0:R, 0:R])
                        mm.then_inc(s_turned, 1)
                turns(pe, U, PR, body)

            @block.vector
            def _(dve):
                dve.wait_ge(s_w, 80)
                dve.wait_ge(s_txt, 32)

                def body(m, j):
                    a = lagged(m, j, LN, U)
                    if a:
                        wait(dve, s_rstd, a.i + 1)
                        wait(dve, s_turned, a.i - 1)
                        wait(dve, s_xn_out[a.j], 16 * a.m)
                        for t in range(TT):
                            nc.vector.tensor_scalar(xn[a.j][:, t, :], g.h[:, bass.ds(a.i * TT + t, 1), :].rearrange("p o e -> p (o e)"),
                                                    mv[a.j][:, t, 0:1], rstd[a.j][:, t:t + 1], ALU.subtract, ALU.mult).then_inc(s_xn, 1)
                    a = lagged(m, j, PR, U)
                    if a:
                        for n in range(2):
                            wait(dve, s_part1, 2 * a.i + n + 1)
                            wait(dve, s_part3, 2 * (a.i - 1))
                            nc.vector.tensor_tensor(rest[n][a.j][:], psQK[n][:, 0:TOK], part[n][a.j][:, 0, :], ALU.subtract).then_inc(s_rest, 1)
                    a = lagged(m, j, PATCH, U)
                    if a:
                        wait(dve, s_patched, a.i + 1)
                        for t, n in enumerate((R, NP - R)):
                            nc.vector.tensor_tensor(g.h[0:n, bass.ds(a.i * TT + t, 1), :].rearrange("p o e -> p (o e)"),
                                                    psH[a.j % 2][0:n, t * D:(t + 1) * D], b_tok[0:n, :], ALU.add).then_inc(s_h, 1)
                        wait(dve, s_h, 2 * a.i + 2)
                        wait(dve, s_mv, 3 * a.i - 3)
                        stand(dve, g)
                        for t in range(TT):
                            nc.vector.bn_stats(stats[a.j][:, t, :], g.h[:, bass.ds(a.i * TT + t, 1), :].rearrange("p o e -> p (o e)")).then_inc(s_stats, 1)
                        wait(dve, s_stats, 3 * a.i + 3)
                        wait(dve, s_xn, 3 * a.i - 3)
                        wait(dve, s_veps, a.i - 1)
                        stand(dve, g)
                        for t in range(TT):
                            nc.vector.bn_aggr(mv[a.j][:, t, :], stats[a.j][:, t, :]).then_inc(s_mv, 1)
                turns(dve, U, PR, body)

            @block.scalar
            def _(act):
                def body(m, j):
                    a = lagged(m, j, PR, U)
                    if a:
                        for n in range(2):
                            wait(act, s_qk, 2 * a.i + n + 1)
                            wait(act, s_qk_out[a.j], 32 * a.m)
                            wait(act, s_part3, 2 * (a.i - 1))
                            nc.scalar.copy(part[n][a.j][:, 0, :], psQK[n][:, 0:TOK]).then_inc(s_part1, 1)
                        wait(act, s_v, a.i + 1)
                        wait(act, s_v_out[a.j], 16 * a.m)
                        if isinstance(a.i, int) and a.i < U:
                            act.wait_ge(s_ones, U)
                        nc.scalar.copy(vone[a.j][:, :, :, 0:HD],
                                       psV[0:R, 0:TT * D].rearrange("p (t h e) -> p t h e", t=TT, h=NH)).then_inc(s_vone, 1)
                    a = lagged(m, j, LN, U)
                    if a:
                        wait(act, s_turned, a.i + 1)
                        wait(act, s_v, a.i - 1)
                        nc.scalar.copy(xnT[a.j][:], psT[:, 0:TOK]).then_inc(s_xnT, 1)
                turns(act, U, PR, body)

            @block.gpsimd
            def _(pool):
                for j in range(U):
                    pool.memset(vone[j][:], 1.0).then_inc(s_ones, 1)

                def parts(a, n):
                    wait(pool, s_rest, 2 * a.i + n + 1)
                    wait(pool, s_qk_out[a.j], 32 * a.m)
                    stand(pool, g)
                    pool.tensor_copy(part[n][a.j][:, 1, :], rest[n][a.j][:]).then_inc(s_part2, 1)
                    wait(pool, s_part2, 2 * a.i + n + 1)
                    pool.tensor_tensor(part[n][a.j][:, 2, :], rest[n][a.j][:], part[n][a.j][:, 1, :], ALU.subtract).then_inc(s_part3, 1)

                def body(m, j):
                    proj = lagged(m, j, PR, U)
                    if proj:
                        parts(proj, 0)
                    a = lagged(m, j, PATCH, U)
                    if a:
                        wait(pool, s_mv, 3 * a.i + 3)
                        wait(pool, s_rstd, a.i - 1)
                        stand(pool, g)
                        pool.tensor_scalar(veps[a.j][:], mv[a.j][:, :, 1], EPS, None, ALU.add).then_inc(s_veps, 1)
                        wait(pool, s_veps, a.i + 1)
                        wait(pool, s_xn, 3 * (a.i - 1))
                        pool.tensor_tensor(rstd[a.j][:], veps[a.j][:], g.minus_half[0:R, 0:TT], ALU.pow).then_inc(s_rstd, 1)
                    if proj:
                        parts(proj, 1)
                turns(pool, U, PR, body)


def attention0(nc, g, d):
    U = 4
    LOAD, SCORE, MAXT, MIX, OUT, NORM = 0, 1, 2, 3, 4, 5
    with Phase(nc, "at0") as ph:
        q_st = [ph.sb(f"q_stack{j}", [SK + 3, NH, TOK], BF16) for j in range(U)]
        k_st = [ph.sb(f"k_stack{j}", [SK + 3, NH, TOK], BF16) for j in range(U)]
        vone = [ph.sb(f"v_{j}", [R, TT, NH, 2 * HD]) for j in range(U)]
        xn = [ph.sb(f"xn{j}", [R, TT * D]) for j in range(U)]
        wo = ph.sb("wo", [D, D])
        gamma, beta = ph.sb("gamma", [R, D]), ph.sb("beta", [R, D])
        negmax = [ph.sb(f"negmax{j}", [R, TT, NH]) for j in range(2)]
        mrest = ph.sb("mrest", [R, TT, NH])
        mpart = [ph.sb(f"mpart{j}", [R, TT, 3 * NH], BF16) for j in range(2)]
        mT = [ph.sb(f"mT{j}", [3 * NH, TOK], BF16) for j in range(2)]
        probs = [ph.sb(f"probs{j}", [R, TT, TOK]) for j in range(2)]
        recip = ph.sb("recip", [R, TT, 4])
        mixed = [ph.sb(f"mixed{j}", [128, 2, TOK]) for j in range(2)]
        ctxv = [ph.sb(f"context{j}", [R, TT, D]) for j in range(2)]
        ctxT = [ph.sb(f"contextT{j}", [D, TOK]) for j in range(2)]
        y = [ph.sb(f"y{j}", [R, TT, D]) for j in range(2)]
        z = [ph.sb(f"z{j}", [R, TT, D]) for j in range(2)]
        stats = ph.sb("stats", [R, TT, 6])
        mv = ph.sb("mv", [R, TT, 2])
        veps, rstd = ph.sb("veps", [R, TT]), ph.sb("rstd", [R, TT])
        psN = ph.ps("psN", [128, TT, 512])
        psS = ph.ps("psS", [128, TT, 512])
        psO = ph.ps("psO", [128, 512])
        psM = ph.ps("psM", [128, 512])
        psM16 = psM[:, :].bitcast(BF16)
        s_w, s_ones = ph.sem("weights_in"), ph.sem("ones_set")
        blank = ph.sb("blank", [128, FFN0.rows // B])
        s_blank, s_blanked = ph.sem("blank_set"), g.blanked
        s_qk = [ph.sem(f"qk_in{j}") for j in range(U)]
        s_vin = [ph.sem(f"v_in{j}") for j in range(U)]
        s_xn = [ph.sem(f"xn_in{j}") for j in range(U)]
        s_mout = [ph.sem(f"max_out{j}") for j in range(U)]
        s_min = [ph.sem(f"max_in{j}") for j in range(U)]
        s_scored, s_max, s_scoredT, s_exp, s_mixed = (ph.sem(n) for n in ("scored", "max", "scoredT", "exp", "mixed"))
        s_heads, s_back = ph.sem("heads_copied"), ph.sem("heads_turned")
        s_mp, s_mturn, s_mT = ph.sem("max_parts"), ph.sem("max_turned"), ph.sem("maxT_written")
        s_recip, s_ctx, s_cturn, s_ctxT = (ph.sem(n) for n in ("recip", "context", "context_turned", "contextT"))
        s_out, s_y, s_stats, s_mv, s_veps, s_rstd = (ph.sem(n) for n in ("projected", "y", "stats", "mv", "veps", "rstd"))
        s_z, s_zg, s_h = ph.sem("normalised"), ph.sem("scaled"), ph.sem("h_added")
        NDMA = 2 * NB

        with nc.Block() as block:
            @block.sync
            def _(sp):
                for dst, src in ((wo[:], d["wo"]), (gamma[:], d["gamma"].partition_broadcast(R)), (beta[:], d["beta"].partition_broadcast(R))):
                    sp.dma_start(dst, src).then_inc(s_w, 16)

                def body(m, j):
                    a = lagged(m, j, LOAD, U)
                    if a:
                        wait(sp, s_scoredT, NH * (a.i - U + 1))
                        for st, parts, src in ((q_st, QPART, d["q_parts"]), (k_st, KPART, d["k_parts"])):
                            for r, n in enumerate(parts):
                                sp.dma_start(st[a.j][r * HD:(r + 1) * HD, :, :],
                                             src[bass.ds(a.i, 1), :, :, n, :].rearrange("o h e t -> (o e) h t")).then_inc(s_qk[a.j], 16)
                    a = lagged(m, j, MAXT, U)
                    if a:
                        wait(sp, s_mixed, NH * (a.i - U + 1))
                        sp.dma_start(vone[a.j][:], d["vone"][bass.ds(a.i, 1)].rearrange("o p t h e -> (o p) t h e")).then_inc(s_vin[a.j], 16)
                        wait(sp, s_y, a.i - U + 1)
                        sp.dma_start(xn[a.j][:], d["xn"][bass.ds(a.i, 1)].rearrange("o p t e -> (o p) (t e)")).then_inc(s_xn[a.j], 16)
                        wait(sp, s_mT, a.i + 1)
                        sp.dma_start(d["maxima"][bass.ds(a.i, 1)].rearrange("o a t -> (o a) t"), mT[a.j % 2][:]).then_inc(s_mout[a.j], 16)
                        wait(sp, s_mout[a.j], 16 * (a.m + 1))
                        sp.dma_start(q_st[a.j][SK:SK + 3, :, :], d["maxima"][bass.ds(a.i, 1)].rearrange("o (a h) t -> (o a) h t", a=3)).then_inc(s_min[a.j], 16)
                turns(sp, U, MAXT, body)

            @block.tensor
            def _(pe):
                pe.wait_ge(s_w, 48)
                pe.wait_ge(s_ones, U)

                def mix(a, k):
                    wait(pe, s_exp, NH * a.i + k + 1)
                    if k % 4 == 0:
                        wait(pe, s_heads, 2 * a.i + k // 4)
                    for c in range(TT):
                        mm = nc.tensor.matmul(psO[32 * (k % 4):32 * (k % 4) + 32, 0:TOK], vone[a.j][:, c, k, :], probs[k % 2][:, c, :],
                                              start=(c == 0), stop=(c == TT - 1), tile_position=(0, 32 * (k % 4)))
                    mm.then_inc(s_mixed, 1)

                def body(m, j):
                    score, mx, mixi, out = (lagged(m, j, lag, U) for lag in (SCORE, MAXT, MIX, OUT))
                    for k in range(NH):
                        if mixi:
                            if k == 0:
                                wait(pe, s_min[mixi.j], 16 * (mixi.m + 1))
                                wait(pe, s_vin[mixi.j], 16 * (mixi.m + 1))
                            wait(pe, s_exp, NH * mixi.i + k)
                            for c in range(TT):
                                mm = nc.tensor.matmul(psS[0:R, c, 0:TOK], k_st[mixi.j][:, k, c * R:(c + 1) * R],
                                                      q_st[mixi.j][:, k, :], start=True, stop=True)
                            mm.then_inc(s_scoredT, 1)
                            if k > 0:
                                mix(mixi, k - 1)
                        if out and 1 <= k <= 2:
                            wait(pe, s_heads, 2 * out.i + k)
                            wait(pe, s_ctx, 2 * out.i + k - 1)
                            wait(pe, s_max, TT * (NH * score.i + k) if score else TT * NH * B)
                            for t in range(TT):
                                mm = nc.tensor.transpose(psN[0:R, t, TOK:TOK + 128], mixed[out.j % 2][:, k - 1, t * R:(t + 1) * R], g.ident[:])
                            mm.then_inc(s_back, 1)
                        if score:
                            if k == 0:
                                wait(pe, s_qk[score.j], 16 * NDMA * (score.m + 1))
                            if k == 3 and out:
                                wait(pe, s_ctx, 2 * out.i + 2)
                            for t in range(TT):
                                wait(pe, s_max, TT * (NH * score.i + k - 1) + t + 1)
                                nc.tensor.matmul(psN[0:R, t, 0:TOK], q_st[score.j][0:SK, k, t * R:(t + 1) * R],
                                                 k_st[score.j][0:SK, k, :], start=True, stop=True).then_inc(s_scored, 1)
                        if mx and k == 2:
                            wait(pe, s_mp, 4 * mx.i + 4)
                            wait(pe, s_y, mx.i - OUT + MAXT)
                            for t in range(TT):
                                mm = nc.tensor.transpose(psM16[0:3 * NH, t * R:(t + 1) * R], mpart[mx.j % 2][:, t, :], g.ident16[0:R, 0:R])
                            mm.then_inc(s_mturn, 1)
                        if out and k == 4:
                            wait(pe, s_ctx, 2 * out.i + 2)
                            n = out.i + OUT - MAXT + 1
                            wait(pe, s_mT, min(n, B) if isinstance(n, int) else n)
                            for t in range(TT):
                                mm = nc.tensor.transpose(psM[:, t * R:(t + 1) * R], ctxv[out.j % 2][:, t, :], g.ident[0:R, 0:R])
                            mm.then_inc(s_cturn, 1)
                        if out and k == 6:
                            wait(pe, s_ctxT, out.i + 1)
                            for t in range(TT):
                                mm = nc.tensor.matmul(psM[0:R, t * D:(t + 1) * D], ctxT[out.j % 2][:, t * R:(t + 1) * R], wo[:],
                                                      start=True, stop=True)
                            mm.then_inc(s_out, 1)
                    if mixi:
                        mix(mixi, NH - 1)
                turns(pe, U, NORM, body)

            @block.scalar
            def _(act):
                def heads(a, n):
                    wait(act, s_mixed, NH * a.i + 4 * n + 4)
                    wait(act, s_back, 2 * (a.i - 1))
                    nc.scalar.copy(mixed[a.j % 2][:, n, :], psO[:, 0:TOK]).then_inc(s_heads, 1)

                def body(m, j):
                    mx, mixi, out = (lagged(m, j, lag, U) for lag in (MAXT, MIX, OUT))
                    for k in range(NH):
                        if mixi:
                            wait(act, s_scoredT, NH * mixi.i + k + 1)
                            wait(act, s_mixed, NH * mixi.i + k - 1)
                            nc.scalar.activation(probs[k % 2][:], psS[0:R, :, 0:TOK], ACT.Exp, scale=0.25).then_inc(s_exp, 1)
                        if mixi and k == 4:
                            heads(mixi, 0)
                        if mx and k == 2:
                            wait(act, s_mturn, mx.i + 1)
                            if isinstance(mx.i, int) and mx.i < 2:
                                pass
                            else:
                                wait(act, s_mout[(mx.j + 2) % U], 16 * (mx.m + (0 if mx.j < 2 else 1)))
                            nc.scalar.copy(mT[mx.j % 2][:], psM16[0:3 * NH, 0:TOK]).then_inc(s_mT, 1)
                        if out and k == 4:
                            wait(act, s_cturn, out.i + 1)
                            wait(act, s_out, out.i - 1)
                            nc.scalar.copy(ctxT[out.j % 2][:], psM[:, 0:TOK]).then_inc(s_ctxT, 1)
                    if mixi:
                        heads(mixi, 1)
                turns(act, U, NORM, body)

            @block.vector
            def _(dve):
                for j in range(U):
                    nc.vector.memset(k_st[j][SK:SK + 3, :, :], 1.0).then_inc(s_ones, 1)
                dve.wait_ge(s_w, 48)

                def body(m, j):
                    score, out, norm = (lagged(m, j, lag, U) for lag in (SCORE, OUT, NORM))
                    for k in range(NH):
                        if score:
                            if k == 0:
                                wait(dve, s_mp, 4 * (score.i - 1))
                            for t in range(TT):
                                wait(dve, s_scored, TT * (NH * score.i + k) + t + 1)
                                nc.vector.tensor_reduce(negmax[score.j % 2][:, t, k:k + 1], psN[0:R, t, 0:TOK], AX.X, ALU.max, negate=True).then_inc(s_max, 1)
                        if norm and k == 4:
                            wait(dve, s_rstd, norm.i + 1)
                            wait(dve, s_h, norm.i - 1)
                            for t in range(TT):
                                nc.vector.tensor_scalar(z[norm.j % 2][:, t, :], y[norm.j % 2][:, t, :], mv[:, t, 0:1], rstd[:, t:t + 1],
                                                        ALU.subtract, ALU.mult).then_inc(s_z, 1)
                        if out and 1 <= k <= 2:
                            n = 2 * out.i + k - 1
                            turned = psN[0:R, :, TOK:TOK + 128].rearrange("p t (h e) -> p t h e", e=2 * HD)
                            wait(dve, s_back, n + 1)
                            wait(dve, s_ctx, n)
                            nc.vector.reciprocal(recip[:], turned[:, :, :, HD]).then_inc(s_recip, 1)
                            wait(dve, s_recip, n + 1)
                            wait(dve, s_cturn, out.i - 1)
                            nc.vector.tensor_tensor(ctxv[out.j % 2][:, :, (k - 1) * 64:k * 64].rearrange("p t (h e) -> p t h e", e=HD),
                                                    turned[:, :, :, 0:HD], recip[:].unsqueeze(3).broadcast_to([R, TT, 4, HD]),
                                                    ALU.mult).then_inc(s_ctx, 1)
                        if out and k == 6:
                            wait(dve, s_out, out.i + 1)
                            wait(dve, s_xn[out.j], 16 * (out.m + 1))
                            nc.vector.tensor_tensor(y[out.j % 2][:].rearrange("p t e -> p (t e)"), psM[0:R, 0:TT * D], xn[out.j][:], ALU.add).then_inc(s_y, 1)
                            wait(dve, s_y, out.i + 1)
                            stand(dve, g)
                            for t in range(TT):
                                nc.vector.bn_stats(stats[:, t, :], y[out.j % 2][:, t, :]).then_inc(s_stats, 1)
                            wait(dve, s_stats, 3 * out.i + 3)
                            wait(dve, s_veps, out.i)
                            wait(dve, s_z, 3 * out.i)
                            stand(dve, g)
                            for t in range(TT):
                                nc.vector.bn_aggr(mv[:, t, :], stats[:, t, :]).then_inc(s_mv, 1)
                turns(dve, U, NORM, body)

            @block.gpsimd
            def _(pool):
                pool.wait_ge(s_w, 48)
                pool.memset(blank[:], 0.0).then_inc(s_blank, 1)
                pool.wait_ge(s_blank, 1)

                def body(m, j):
                    mx, out, norm = (lagged(m, j, lag, U) for lag in (MAXT, OUT, NORM))
                    if mx:
                        mp, nm = mpart[mx.j % 2], negmax[mx.j % 2]
                        wait(pool, s_max, TT * NH * (mx.i + 1))
                        wait(pool, s_mturn, mx.i - 1)
                        stand(pool, g)
                        pool.tensor_copy(mp[:, :, 0:NH], nm[:]).then_inc(s_mp, 1)
                        wait(pool, s_mp, 4 * mx.i + 1)
                        pool.tensor_tensor(mrest[:], nm[:], mp[:, :, 0:NH], ALU.subtract).then_inc(s_mp, 1)
                        wait(pool, s_mp, 4 * mx.i + 2)
                        stand(pool, g)
                        pool.tensor_copy(mp[:, :, NH:2 * NH], mrest[:]).then_inc(s_mp, 1)
                        wait(pool, s_mp, 4 * mx.i + 3)
                        pool.tensor_tensor(mp[:, :, 2 * NH:3 * NH], mrest[:], mp[:, :, NH:2 * NH], ALU.subtract).then_inc(s_mp, 1)
                    if mx:
                        for f in (FFN0, FFN1):
                            n = f.rows // B
                            for xs in d["xs" + str(f.layer)]:
                                pool.dma_start(xs.rearrange("(p m) e -> p (m e)", p=128)[:, bass.ds(mx.i * n, n)],
                                               blank[:, 0:n]).then_inc(s_blanked, 16)
                    if norm:
                        zz = z[norm.j % 2]
                        wait(pool, s_z, 3 * norm.i + 3)
                        pool.tensor_tensor(zz[:], zz[:], gamma[:].unsqueeze(1).broadcast_to([R, TT, D]), ALU.mult).then_inc(s_zg, 1)
                        wait(pool, s_zg, 2 * norm.i + 1)
                        pool.tensor_tensor(zz[:], zz[:], beta[:].unsqueeze(1).broadcast_to([R, TT, D]), ALU.add).then_inc(s_zg, 1)
                        wait(pool, s_zg, 2 * norm.i + 2)
                        pool.tensor_tensor(tile_of(g.h, norm.i), tile_of(g.h, norm.i), zz[:], ALU.add).then_inc(s_h, 1)
                    if out:
                        wait(pool, s_mv, 3 * out.i + 3)
                        wait(pool, s_rstd, out.i)
                        stand(pool, g)
                        pool.tensor_scalar(veps[:], mv[:, :, 1], EPS, None, ALU.add).then_inc(s_veps, 1)
                        wait(pool, s_veps, out.i + 1)
                        wait(pool, s_z, 3 * out.i)
                        pool.tensor_tensor(rstd[:], veps[:], g.minus_half[0:R, 0:TT], ALU.pow).then_inc(s_rstd, 1)
                turns(pool, U, NORM, body)
                pool.wait_ge(s_blanked, 16 * 2 * TT * B)


class Ffn:

    def __init__(self, layer, experts, k, chunks, shared, act_shared, fused):
        self.layer, self.E, self.K, self.C = layer, experts, k, chunks
        self.I = chunks * 128
        self.W = 3 * self.I
        self.shared = shared
        self.act_shared, self.gated = act_shared, fused
        self.G = 4 // chunks
        self.blocks = -(-(B * R * k // 128 + experts) // 4) * 4
        self.rows = self.blocks * 128


FFN0 = Ffn(0, 64, 8, 1, (128, 128, 96), ACT.Silu, True)
FFN1 = Ffn(1, 8, 1, 4, (128, 128, 128, 128), ACT.Gelu, False)


def ffn(nc, g, d, f, after):
    with Phase(nc, f"ffn{f.layer}") as own:
        r = Shared()
        r.top = own.sb("top", [R, NTILE, 8])
        r.expert = own.sb("expert", [R, NTILE, 8])
        r.pos = own.sb("pos", [R, NTILE, f.K], I32)
        r.counts = own.sb("counts", [128, TT, f.E])
        r.expert_row = own.sb("expert_row", [1, TT * f.blocks], I32)
        r.w = own.sb("experts", [128, f.E * f.W])
        r.s_w = own.sem("experts_in")
        with Phase(nc, f"rank{f.layer}") as ranks:
            r.rank = ranks.sb("rank", [R, NTILE, f.E])
            r.iota = ranks.sb("iota", [R, f.E])
            route(nc, g, d, f, r)
            lists(nc, g, d, f, r)
            scatter(nc, g, d, f, r)
        experts(nc, g, d, f, r)
        after(nc, g, d, f, r)


def route(nc, g, d, f, r):
    U = 4
    STAT, NORM, GATE, RANK = 0, 1, 2, 3
    E = f.E
    with Phase(nc, f"route{f.layer}") as ph:
        gate = ph.sb("gate", [D, E])
        before = ph.sb("before", [R, R], BF16)
        ones = ph.sb("ones", [R, 128], BF16)
        stats = [ph.sb(f"stats{j}", [R, TT, 6]) for j in range(U)]
        mv = [ph.sb(f"mv{j}", [R, TT, 2]) for j in range(U)]
        veps = [ph.sb(f"veps{j}", [R, TT]) for j in range(U)]
        rstd = [ph.sb(f"rstd{j}", [R, TT]) for j in range(U)]
        xn = [ph.sb(f"xn{j}", [R, TT, D]) for j in range(U)]
        xnT = [ph.sb(f"xnT{j}", [D, TOK]) for j in range(U)]
        logits = [ph.sb(f"logits{j}", [R, TT, E]) for j in range(U)]
        rep = ph.sb("replaced", [R, TT, E])
        top8 = [ph.sb(f"top8_{j}", [R, TT, 8]) for j in range(U)]
        where = ph.sb("where", [R, TT, 8], U32)
        mask = [ph.sb(f"mask{j}", [R, TT, E], BF16) for j in range(U)]
        total = ph.sb("gate_total", [R, NTILE])
        psT = ph.ps("psT", [128, 512])
        psG = ph.ps("psG", [128, 512])
        psR = ph.ps("psR", [128, 512])
        psC = ph.ps("psC", [128, 512])
        s_w, s_set = ph.sem("weights_in"), ph.sem("constants_set")
        s_stats, s_mv, s_veps, s_rstd, s_xn = (ph.sem(n) for n in ("stats", "mv", "veps", "rstd", "xn_written"))
        s_turned, s_xnT, s_gated, s_logits = (ph.sem(n) for n in ("turned", "xnT_written", "gated", "logits"))
        s_kept, s_first = ph.sem("top_kept"), ph.sem("first_taken")
        s_top, s_where, s_expert, s_rep, s_mask = (ph.sem(n) for n in ("top", "where", "expert", "replaced", "mask"))
        s_rankps, s_rank, s_count = ph.sem("rank_multiplied"), ph.sem("rank_written"), ph.sem("counts_added")
        s_exp, s_soft = ph.sem("gates_exp"), ph.sem("softmax_step")
        s_xn_out = [ph.sem(f"xn_out{j}") for j in range(U)]
        s_xnT_out = [ph.sem(f"xnT_out{j}") for j in range(U)]
        top_all = r.top[:, :, 0:f.K]

        with nc.Block() as block:
            @block.sync
            def _(sp):
                sp.dma_start(gate[:], d["gate" + str(f.layer)]).then_inc(s_w, 16)

                def body(m, j):
                    a = lagged(m, j, NORM, U)
                    if a:
                        wait(sp, s_xn, 3 * a.i + 3)
                        sp.dma_start(d["xn"][bass.ds(a.i, 1)].rearrange("o p t e -> (o p) t e"), xn[a.j][:]).then_inc(s_xn_out[a.j], 16)
                        wait(sp, s_xnT, a.i + 1)
                        sp.dma_start(d["xnT"][bass.ds(a.i, 1)].rearrange("o e t -> (o e) t"), xnT[a.j][:]).then_inc(s_xnT_out[a.j], 16)
                turns(sp, U, RANK, body)
                for j in range(U):
                    sp.wait_ge(s_xn_out[j], 16 * B // U)
                    sp.wait_ge(s_xnT_out[j], 16 * B // U)

            @block.gpsimd
            def _(pool):
                pool.memset(ones[:], 1.0).then_inc(s_set, 1)
                pool.memset(before[:], 1.0).then_inc(s_set, 1)
                pool.memset(r.counts[:], 0.0).then_inc(s_set, 1)
                pool.iota(r.iota[:], pattern=[[1, E]], base=0, channel_multiplier=0,
                          allow_small_or_imprecise_dtypes=True).then_inc(s_set, 1)
                pool.wait_ge(s_set, 4)
                pool.affine_select(out=before[:], in_=before[:], compare_op=ALU.is_ge, fill=0.0, base=-1,
                                   pattern=[[1, R]], channel_multiplier=-1).then_inc(s_set, 1)

                def body(m, j):
                    a = lagged(m, j, STAT, U)
                    if a:
                        wait(pool, s_mv, 3 * a.i + 3)
                        wait(pool, s_rstd, a.i - 1)
                        stand(pool, g)
                        pool.tensor_scalar(veps[a.j][:], mv[a.j][:, :, 1], EPS, None, ALU.add).then_inc(s_veps, 1)
                        wait(pool, s_veps, a.i + 1)
                        wait(pool, s_xn, 3 * (a.i - 1))
                        pool.tensor_tensor(rstd[a.j][:], veps[a.j][:], g.minus_half[0:R, 0:TT], ALU.pow).then_inc(s_rstd, 1)
                turns(pool, U, RANK, body)

            @block.tensor
            def _(pe):
                pe.wait_ge(s_w, 16)
                pe.wait_ge(s_set, 5)

                def body(m, j):
                    a = lagged(m, j, GATE, U)
                    if a:
                        wait(pe, s_xnT, a.i + 1)
                        wait(pe, s_logits, a.i)
                        for t in range(TT):
                            mm = nc.tensor.matmul(psG[0:R, t * E:(t + 1) * E], xnT[a.j][:, t * R:(t + 1) * R], gate[:], start=True, stop=True)
                        mm.then_inc(s_gated, 1)
                    a = lagged(m, j, RANK, U)
                    if a:
                        wait(pe, s_mask, a.i + 1)
                        wait(pe, s_rank, a.i)
                        wait(pe, s_count, a.i)
                        mk = mask[a.j][:].rearrange("p t e -> p (t e)")
                        nc.tensor.matmul(psR[0:R, 0:TT * E], before[:], mk, start=True, stop=True)
                        nc.tensor.matmul(psC[:, 0:TT * E], ones[:], mk, start=True, stop=True).then_inc(s_rankps, 1)
                    a = lagged(m, j, NORM, U)
                    if a:
                        wait(pe, s_xn, 3 * a.i + 3)
                        wait(pe, s_xnT, a.i)
                        for t in range(TT):
                            mm = nc.tensor.transpose(psT[:, t * R:(t + 1) * R], xn[a.j][:, t, :], g.ident[0:R, 0:R])
                        mm.then_inc(s_turned, 1)
                turns(pe, U, RANK, body)

            @block.scalar
            def _(act):
                def body(m, j):
                    a = lagged(m, j, GATE, U)
                    if a:
                        wait(act, s_gated, a.i + 1)
                        wait(act, s_rep if f.K > 1 else s_where, 3 * (a.i - 1))
                        nc.scalar.copy(logits[a.j][:].rearrange("p t e -> p (t e)"), psG[0:R, 0:TT * E]).then_inc(s_logits, 1)
                    a = lagged(m, j, NORM, U)
                    if a:
                        wait(act, s_turned, a.i + 1)
                        wait(act, s_gated, a.i - 1)
                        wait(act, s_xnT_out[a.j], 16 * a.m)
                        nc.scalar.copy(xnT[a.j][:], psT[:, 0:TOK]).then_inc(s_xnT, 1)
                turns(act, U, RANK, body)
                act.wait_ge(s_soft, 1)
                nc.scalar.activation(top_all, top_all, ACT.Exp).then_inc(s_exp, 1)

            @block.vector
            def _(dve):
                dve.wait_ge(s_set, 5)

                def tile1(t3, i, t):
                    return t3[:, bass.ds(i * TT + t, 1), :].rearrange("p o e -> p (o e)")

                def body(m, j):
                    a = lagged(m, j, NORM, U)
                    if a:
                        wait(dve, s_rstd, a.i + 1)
                        wait(dve, s_turned, a.i - 1)
                        wait(dve, s_xn_out[a.j], 16 * a.m)
                        for t in range(TT):
                            nc.vector.tensor_scalar(xn[a.j][:, t, :], tile1(g.h, a.i, t), mv[a.j][:, t, 0:1], rstd[a.j][:, t:t + 1],
                                                    ALU.subtract, ALU.mult).then_inc(s_xn, 1)
                    a = lagged(m, j, STAT, U)
                    if a:
                        wait(dve, s_mv, 3 * a.i - 3)
                        stand(dve, g)
                        for t in range(TT):
                            nc.vector.bn_stats(stats[a.j][:, t, :], tile1(g.h, a.i, t)).then_inc(s_stats, 1)
                        wait(dve, s_stats, 3 * a.i + 3)
                        wait(dve, s_xn, 3 * a.i - 3)
                        wait(dve, s_veps, a.i - 1)
                        stand(dve, g)
                        for t in range(TT):
                            nc.vector.bn_aggr(mv[a.j][:, t, :], stats[a.j][:, t, :]).then_inc(s_mv, 1)
                    a = lagged(m, j, GATE, U)
                    if a:
                        wait(dve, s_logits, a.i + 1)
                        wait(dve, s_kept, a.i - 1)
                        stand(dve, g)
                        for t in range(TT):
                            nc.vector.max(top8[a.j][:, t, :], logits[a.j][:, t, :]).then_inc(s_top, 1)
                        wait(dve, s_top, 3 * a.i + 3)
                        wait(dve, s_expert, a.i)
                        stand(dve, g)
                        for t in range(TT):
                            nc.vector.max_index(where[:, t, :], top8[a.j][:, t, :], logits[a.j][:, t, :]).then_inc(s_where, 1)
                        if f.K > 1:
                            wait(dve, s_mask, a.i)
                            stand(dve, g)
                            for t in range(TT):
                                nc.vector.match_replace(rep[:, t, :], top8[a.j][:, t, :], logits[a.j][:, t, :], NEG).then_inc(s_rep, 1)
                        nc.vector.tensor_copy(tile_of(r.top, a.i), top8[a.j][:]).then_inc(s_kept, 1)
                        wait(dve, s_where, 3 * a.i + 3)
                        nc.vector.tensor_copy(tile_of(r.expert, a.i), where[:]).then_inc(s_expert, 1)
                        wait(dve, s_rankps, a.i - 1)
                        if f.K > 1:
                            wait(dve, s_rep, 3 * a.i + 3)
                            nc.vector.tensor_tensor(mask[a.j][:], rep[:], logits[a.j][:], ALU.not_equal).then_inc(s_mask, 1)
                        else:
                            wait(dve, s_expert, a.i + 1)
                            nc.vector.tensor_tensor(mask[a.j][:], r.iota[:].unsqueeze(1).broadcast_to([R, TT, E]),
                                                    tile_of(r.expert, a.i)[:, :, 0:1].broadcast_to([R, TT, E]), ALU.is_equal).then_inc(s_mask, 1)
                    a = lagged(m, j, RANK, U)
                    if a:
                        wait(dve, s_rankps, a.i + 1)
                        wait(dve, s_count, a.i)
                        nc.vector.tensor_tensor(tile_of(r.rank, a.i), psR[0:R, 0:TT * E].rearrange("p (t e) -> p t e", t=TT),
                                                r.counts[0:R], ALU.add).then_inc(s_rank, 1)
                        wait(dve, s_rank, a.i + 1)
                        nc.vector.tensor_tensor(r.counts[:], psC[:, 0:TT * E].rearrange("p (t e) -> p t e", t=TT), r.counts[:], ALU.add).then_inc(s_count, 1)
                turns(dve, U, RANK, body)
                dve.wait_ge(s_where, 3 * B)
                if f.K > 1:
                    dve.wait_ge(s_rep, 3 * B)
                dve.wait_ge(s_kept, B)
                nc.vector.tensor_copy(total[:], r.top[:, :, 0]).then_inc(s_first, 1)
                dve.wait_ge(s_first, 1)
                nc.vector.tensor_tensor(top_all, top_all, total[:].unsqueeze(2).broadcast_to([R, NTILE, f.K]), ALU.subtract).then_inc(s_soft, 1)
                dve.wait_ge(s_exp, 1)
                nc.vector.tensor_reduce(total[:], top_all, AX.X, ALU.add).then_inc(s_soft, 1)
                dve.wait_ge(s_soft, 2)
                nc.vector.reciprocal(total[:], total[:]).then_inc(s_soft, 1)
                dve.wait_ge(s_soft, 3)
                nc.vector.tensor_tensor(top_all, top_all, total[:].unsqueeze(2).broadcast_to([R, NTILE, f.K]), ALU.mult).then_inc(s_soft, 1)


def lists(nc, g, d, f, r):
    E = f.E
    pad = E // 2
    chunks = -(-f.blocks // 128)
    with Phase(nc, f"lists{f.layer}") as ph:
        whole = ph.sb("whole", [128, TT, E], I32)
        nblk = ph.sb("nblk", [128, TT, E])
        run = [ph.sb(f"run{n}", [128, TT, pad + E]) for n in range(2)]
        block_no = ph.sb("block_no", [128, chunks])
        below = ph.sb("below", [128, E])
        owner = ph.sb("owner", [128, TT, chunks])
        owner_i = ph.sb("owner_i", [128, TT, chunks], I32)
        s_iota, s_step, s_out, s_in = (ph.sem(n) for n in ("iota_set", "step", "table_out", "table_in"))
        with nc.Block() as block:
            @block.gpsimd
            def _(pool):
                pool.iota(block_no[:], pattern=[[128, chunks]], base=0, channel_multiplier=1,
                          allow_small_or_imprecise_dtypes=True).then_inc(s_iota, 1)

            @block.vector
            def _(dve):
                done = [0]

                def step(ins):
                    done[0] += 1
                    ins.then_inc(s_step, 1)
                    dve.wait_ge(s_step, done[0])
                step(nc.vector.memset(run[0][:], 0.0))
                step(nc.vector.memset(run[1][:], 0.0))
                step(nc.vector.tensor_scalar(whole[:], r.counts[:], 127.0, None, ALU.add))
                step(nc.vector.tensor_scalar(whole[:], whole[:], 7, None, ALU.logical_shift_right))
                step(nc.vector.tensor_copy(nblk[:], whole[:]))
                step(nc.vector.tensor_scalar(nblk[:], nblk[:], 1.0, None, ALU.max))
                step(nc.vector.tensor_copy(run[0][:, :, pad:], nblk[:]))
                now, s = 0, 1
                while s < E:
                    step(nc.vector.tensor_tensor(run[1 - now][:, :, pad:], run[now][:, :, pad:], run[now][:, :, pad - s:pad + E - s], ALU.add))
                    now, s = 1 - now, 2 * s
                last = run[now][:, :, pad:]
                step(nc.vector.tensor_tensor(nblk[:], last, nblk[:], ALU.subtract))
                step(nc.vector.tensor_scalar(r.counts[:], nblk[:], 128.0, None, ALU.mult))
                dve.wait_ge(s_iota, 1)
                for t in range(TT):
                    for c in range(chunks):
                        step(nc.vector.tensor_scalar(below[:], run[now][:, t, pad:], block_no[:, c:c + 1], None, ALU.is_le))
                        step(nc.vector.tensor_reduce(owner[:, t, c:c + 1], below[:], AX.X, ALU.add))
                step(nc.vector.tensor_scalar(owner[:], owner[:], float(E - 1), None, ALU.min))
                step(nc.vector.tensor_copy(owner_i[:], owner[:]))

            @block.sync
            def _(sp):
                sp.wait_ge(s_step, 9 + E.bit_length() - 1 + 2 * TT * chunks + 2)
                for t in range(TT):
                    for c in range(chunks):
                        n = min(128, f.blocks - 128 * c)
                        sp.dma_start(d["owner"][t * f.blocks + 128 * c:t * f.blocks + 128 * c + n].unsqueeze(1),
                                     owner_i[0:n, t, c:c + 1]).then_inc(s_out, 16)
                sp.wait_ge(s_out, 16 * TT * chunks)
                sp.dma_start(r.expert_row[:], d["owner"][0:TT * f.blocks].unsqueeze(0)).then_inc(s_in, 16)
                sp.wait_ge(s_in, 16)


def scatter(nc, g, d, f, r):
    U = 2
    LOAD, PLACE, SEND, HID, ADD = 0, 1, 2, 1, 2
    E, K = f.E, f.K
    xs = d["xs" + str(f.layer)]
    NC = len(f.shared)
    per = 2 if f.gated else 1
    with Phase(nc, f"scat{f.layer}") as ph:
        xn = [ph.sb(f"xn{j}", [R, TT, D]) for j in range(2 * U)]
        xnT = [ph.sb(f"xnT{j}", [D, TOK]) for j in range(U)]
        hot = ph.sb("hot", [R, TT * K, E])
        posf = ph.sb("posf", [R, TT * K])
        pos = [ph.sb(f"pos{j}", [R, TT * K], I32) for j in range(U)]
        w_in = ph.sb("shared_in", [D, per, sum(f.shared)])
        w_out = ph.sb("shared_out", [128, NC, D])
        HS = 1 if f.gated else U
        hid = [ph.sb(f"hid{j}", [128, NC, TOK]) for j in range(HS)]
        psA = [ph.ps(f"psA{n}", [128, 512]) for n in range(2)]
        psB = [ph.ps(f"psB{n}", [128, 512]) for n in range(2)]
        psY = ph.ps("psY", [128, 512])
        s_w = ph.sem("weights_in")
        s_xn = [ph.sem(f"xn_in{j}") for j in range(2 * U)]
        s_xnT = [ph.sem(f"xnT_in{j}") for j in range(U)]
        s_row, s_hot, s_pick, s_posf, s_pos, s_posall = (ph.sem(n) for n in ("row", "hot", "picked", "posf", "pos", "pos_kept"))
        s_sent = g.sent[f.layer]
        s_in, s_act, s_hid, s_down, s_h = (ph.sem(n) for n in ("in_multiplied", "activated", "hidden", "down", "h_added"))

        with nc.Block() as block:
            @block.sync
            def _(sp):
                lo = 0
                for c, w in enumerate(f.shared):
                    sp.dma_start(w_out[0:w, c, :], d["sw2_" + str(f.layer)][lo:lo + w, :]).then_inc(s_w, 16)
                    lo += w
                sp.dma_start(w_in[:, 0, :], d["sw1_" + str(f.layer)]).then_inc(s_w, 16)
                if f.gated:
                    sp.dma_start(w_in[:, 1, :], d["sw3_" + str(f.layer)]).then_inc(s_w, 16)

                share = f.E * f.W // B

                def body(m, j):
                    a = lagged(m, j, LOAD, 2 * U)
                    if a:
                        for t in range(TT):
                            wait(sp, s_sent[t], 16 * K * (a.i - 2 * U + 1))
                        sp.dma_start(xn[a.j][:], d["xn"][bass.ds(a.i, 1)].rearrange("o p t e -> (o p) t e")).then_inc(s_xn[a.j], 16)
                        wait(sp, s_in, NC * (a.i - 1))
                        sp.dma_start(xnT[a.j % U][:], d["xnT"][bass.ds(a.i, 1)].rearrange("o e t -> (o e) t")).then_inc(s_xnT[a.j % U], 16)
                        sp.dma_start(r.w[:, bass.ds(a.i * share, share)], d["exp" + str(f.layer)][:, bass.ds(a.i * share, share)]).then_inc(r.s_w, 16)
                turns(sp, 2 * U, SEND, body)

            @block.gpsimd
            def _(pool):
                def body(m, j):
                    a = lagged(m, j, SEND, 2 * U)
                    if a:
                        wait(pool, s_pos, a.i + 1)
                        stand(pool, g)
                        wait(pool, s_xn[a.j], 16 * (a.m + 1))
                        stand(pool, g)
                        for k in range(K):
                            for t in range(TT):
                                n = 16 * (K * a.i + k)
                                if not (isinstance(n, int) and n <= 0):
                                    pool.wait_ge(s_sent[t], n)
                                    stand(pool, g)
                                pool.indirect_dma_start(xs[t], bass.IndirectOffsetOnAxis(ap=pos[a.j % U][:, t * K + k:t * K + k + 1], axis=0),
                                                        xn[a.j][:, t, :], None).then_inc(s_sent[t], 16)
                turns(pool, 2 * U, SEND, body)
                for t in range(TT):
                    pool.wait_ge(s_sent[t], 16 * K * B)

            @block.tensor
            def _(pe):
                pe.wait_ge(s_w, 16 * (NC + per))

                def body(m, j):
                    a = lagged(m, j, ADD, U)
                    if a:
                        wait(pe, s_hid, NC * a.i + NC)
                        wait(pe, s_h, a.i)
                        for t in range(TT):
                            for c, w in enumerate(f.shared):
                                mm = nc.tensor.matmul(psY[0:R, t * D:(t + 1) * D], hid[a.j % HS][0:w, c, t * R:(t + 1) * R], w_out[0:w, c, :],
                                                      start=(c == 0), stop=(c == NC - 1))
                        mm.then_inc(s_down, 1)
                    a = lagged(m, j, HID, U)
                    if a:
                        wait(pe, s_xnT[a.j], 16 * (a.m + 1))
                        lo = 0
                        for c, w in enumerate(f.shared):
                            n = (a.j * NC + c) % 2
                            wait(pe, s_hid, NC * a.i + c - 1)
                            mm = nc.tensor.matmul(psA[n][0:w, 0:TOK], w_in[:, 0, lo:lo + w], xnT[a.j][:], start=True, stop=True)
                            if f.gated:
                                mm = nc.tensor.matmul(psB[n][0:w, 0:TOK], w_in[:, 1, lo:lo + w], xnT[a.j][:], start=True, stop=True)
                            mm.then_inc(s_in, 1)
                            lo += w
                turns(pe, U, ADD, body)

            @block.scalar
            def _(act):
                def body(m, j):
                    a = lagged(m, j, HID, U)
                    if a:
                        for c, w in enumerate(f.shared):
                            n = (a.j * NC + c) % 2
                            wait(act, s_in, NC * a.i + c + 1)
                            if f.gated:
                                wait(act, s_down, a.i - HS + 1)
                                nc.scalar.activation(hid[a.j % HS][0:w, c, :], psA[n][0:w, 0:TOK], f.act_shared).then_inc(s_act, 1)
                            else:
                                wait(act, s_down, a.i - HS + 1)
                                nc.scalar.activation(hid[a.j % HS][0:w, c, :], psA[n][0:w, 0:TOK], f.act_shared).then_inc(s_hid, 1)
                turns(act, U, ADD, body)

            @block.vector
            def _(dve):
                def body(m, j):
                    a = lagged(m, j, HID, U)
                    if a and f.gated:
                        for c, w in enumerate(f.shared):
                            n = (a.j * NC + c) % 2
                            wait(dve, s_act, NC * a.i + c + 1)
                            nc.vector.tensor_tensor(hid[a.j % HS][0:w, c, :], hid[a.j % HS][0:w, c, :], psB[n][0:w, 0:TOK], ALU.mult).then_inc(s_hid, 1)
                    a = lagged(m, j, PLACE, U)
                    if a:
                        rank = tile_of(r.rank, a.i)
                        nc.vector.tensor_tensor(rank, rank, r.counts[0:R], ALU.add).then_inc(s_row, 1)
                        wait(dve, s_posf, a.i)
                        chosen = tile_of(r.expert, a.i)[:, :, 0:K]
                        hot4 = hot[:].rearrange("p (t k) e -> p t k e", k=K)
                        for t in range(TT):
                            nc.vector.tensor_tensor(hot4[:, t], r.iota[:].unsqueeze(1).broadcast_to([R, K, E]),
                                                    chosen[:, t].unsqueeze(2).broadcast_to([R, K, E]), ALU.is_equal).then_inc(s_hot, 1)
                        wait(dve, s_hot, 3 * a.i + 3)
                        wait(dve, s_row, a.i + 1)
                        nc.vector.tensor_tensor(hot4, hot4, rank.unsqueeze(2).broadcast_to([R, TT, K, E]), ALU.mult).then_inc(s_pick, 1)
                        wait(dve, s_pick, a.i + 1)
                        wait(dve, s_posall, a.i)
                        nc.vector.tensor_reduce(posf[:], hot[:], AX.X, ALU.add).then_inc(s_posf, 1)
                        wait(dve, s_posf, a.i + 1)
                        for t in range(TT):
                            wait(dve, s_sent[t], 16 * K * (a.i - 1))
                        nc.vector.tensor_copy(pos[a.j][:], posf[:]).then_inc(s_pos, 1)
                        nc.vector.tensor_copy(tile_of(r.pos, a.i).rearrange("p t k -> p (t k)"), posf[:]).then_inc(s_posall, 1)
                    a = lagged(m, j, ADD, U)
                    if a:
                        wait(dve, s_down, a.i + 1)
                        nc.vector.tensor_tensor(tile_of(g.h, a.i), psY[0:R, 0:TT * D].rearrange("p (t e) -> p t e", t=TT), tile_of(g.h, a.i),
                                                ALU.add).then_inc(s_h, 1)
                turns(dve, U, ADD, body)


def experts(nc, g, d, f, r):
    U = 4
    LOAD, TURN, UP, BACK, DOWN = 0, 2, 3, 4, 5
    xs, ys = d["xs" + str(f.layer)], d["ys" + str(f.layer)]
    I, C, G = f.I, f.C, f.G
    N = f.blocks // G
    ROUNDS = N // U - 1
    ADDS = B * f.K // (ROUNDS * U)
    assert ADDS * ROUNDS * U == B * f.K and f.K % ADDS == 0
    with Phase(nc, f"exp{f.layer}") as ph:
        w = r.w
        x = [ph.sb(f"x{j}", [128, G, D]) for j in range(U)]
        xT = [ph.sb(f"xT{j}", [D, G * 128]) for j in range(2)]
        hid = [ph.sb(f"hid{j}", [128, G * I]) for j in range(2)]
        hidT = [ph.sb(f"hidT{j}", [128, G * I]) for j in range(2)]
        y = [ph.sb(f"y{j}", [128, G, D]) for j in range(U)]
        rows = Rows(ph, f, 0, g.got[f.layer])
        psX = [ph.ps(f"psX{j}", [128, 512]) for j in range(2)]
        psH = [ph.ps(f"psH{j}", [128, 2, 512]) for j in range(2)]
        psT = ph.ps("psT", [128, 512])
        psY = ph.ps("psY", [128, 512])
        s_x = [ph.sem(f"x_in{j}") for j in range(U)]
        s_y_out = [ph.sem(f"y_out{j}") for j in range(U)]
        s_xturn, s_xT, s_up, s_silu, s_hid, s_hturn, s_hT, s_down, s_y = (ph.sem(n) for n in (
            "x_turned", "xT_written", "up", "silu", "hidden", "hidden_turned", "hiddenT", "down", "y_written"))
        if C == 1:
            h1, h3 = ([p[:].rearrange("p n (b c e) -> p (n b) c e", b=2, e=I)[:, :, k, :] for p in psH] for k in range(2))
        else:
            h1, h3 = ([p[:, k, :].unsqueeze(1) for p in psH] for k in range(2))
        visits = [-(-(N - j) // U) for j in range(U)]

        def by_block(tile):
            return tile[:].rearrange("p (b e) -> p b e", e=I)

        def each_group(eng, lag_max, body):
            for t in range(TT):
                turns(eng, U, lag_max, lambda m, j: body(t, t * N, m, j), N)

        def freed(base, a):
            return base if isinstance(a.i, int) and a.i < U else base + a.i - U + 1

        with nc.Block() as block:
            @block.sync
            def _(sp):
                def body(t, base, m, j):
                    a = lagged(m, j, LOAD, U, N)
                    if a:
                        wait(sp, s_xturn, freed(base, a))
                        sp.dma_start(x[a.j][:], xs[t][bass.ds(a.i * G * 128, G * 128), :].rearrange("(b p) e -> p b e", p=128)
                                     ).then_inc(s_x[a.j], 16)
                each_group(sp, DOWN, body)
                for j in range(U):
                    sp.wait_ge(s_y_out[j], 16 * TT * visits[j])

            @block.tensor
            def _(pe):
                pe.wait_ge(r.s_w, 16 * B)

                def weights(t, a):
                    _, owners = nc.values_load_multi_w_load_instructions(
                        r.expert_row[0:1, bass.ds(a.i * G + t * f.blocks, G)], engines=[mybir.EngineType.PE],
                        min_val=0, max_val=f.E - 1, skip_runtime_bounds_check_because="lists() clamps them to the last expert and counts from zero")
                    return [e * f.W for e in owners]

                def body(t, base, m, j):
                    a = lagged(m, j, TURN, U, N)
                    if a:
                        n = a.j % 2
                        wait(pe, s_x[a.j], 16 * (a.m + 1 + t * visits[a.j]))
                        wait(pe, s_xT, base + a.i - 1)
                        for b in range(G):
                            mm = nc.tensor.transpose(psX[n][:, b * 128:(b + 1) * 128], x[a.j][:, b, :], g.ident[:])
                        mm.then_inc(s_xturn, 1)
                    a = lagged(m, j, UP, U, N)
                    if a:
                        n = a.j % 2
                        at = weights(t, a)
                        wait(pe, s_xT, base + a.i + 1)
                        wait(pe, s_hid, base + a.i - 1)
                        if C == 1:
                            for b in range(G):
                                mm = nc.tensor.matmul(psH[n][:, b // 2, (b % 2) * 2 * I:(b % 2 + 1) * 2 * I], xT[n][:, b * 128:(b + 1) * 128],
                                                      w[:, bass.ds(at[b], 2 * I)], start=True, stop=True)
                        else:
                            for k in range(2):
                                mm = nc.tensor.matmul(psH[n][:, k, :], xT[n][:], w[:, bass.ds(at[0] + k * I, I)], start=True, stop=True)
                        mm.then_inc(s_up, 1)
                    a = lagged(m, j, BACK, U, N)
                    if a:
                        n = a.j % 2
                        wait(pe, s_hid, base + a.i + 1)
                        wait(pe, s_hT, base + a.i)
                        for c in range(G * C):
                            mm = nc.tensor.transpose(psT[:, c * 128:(c + 1) * 128], hid[n][:, c * 128:(c + 1) * 128], g.ident[:])
                        mm.then_inc(s_hturn, 1)
                    a = lagged(m, j, DOWN, U, N)
                    if a:
                        n = a.j % 2
                        at = weights(t, a)
                        wait(pe, s_hT, base + a.i + 1)
                        wait(pe, s_y, base + a.i)
                        for b in range(G):
                            for c in range(C):
                                mm = nc.tensor.matmul(psY[:, b * D:(b + 1) * D], hidT[n][:, (b * C + c) * 128:(b * C + c + 1) * 128],
                                                      w[:, bass.ds(at[b] + 2 * I + c * D, D)], start=(c == 0), stop=(c == C - 1))
                        mm.then_inc(s_down, 1)
                each_group(pe, DOWN, body)

            @block.scalar
            def _(act):
                def body(t, base, m, j):
                    a = lagged(m, j, TURN, U, N)
                    if a:
                        wait(act, s_xturn, base + a.i + 1)
                        wait(act, s_up, base + a.i - 1)
                        nc.scalar.copy(xT[a.j % 2][:], psX[a.j % 2][:, 0:G * 128]).then_inc(s_xT, 1)
                    a = lagged(m, j, UP, U, N)
                    if a:
                        wait(act, s_up, base + a.i + 1)
                        wait(act, s_hturn, base + a.i - 1)
                        nc.scalar.activation(by_block(hid[a.j % 2]), h1[a.j % 2], ACT.Silu).then_inc(s_silu, 1)
                    a = lagged(m, j, DOWN, U, N)
                    if a:
                        wait(act, s_y, base + a.i + 1)
                        act.dma_start(ys[t][bass.ds(a.i * G * 128, G * 128), :].rearrange("(b p) e -> p b e", p=128),
                                      y[a.j][:]).then_inc(s_y_out[a.j], 16)
                each_group(act, DOWN, body)

            @block.vector
            def _(dve):
                def body(t, base, m, j):
                    a = lagged(m, j, UP, U, N)
                    if a:
                        n = a.j % 2
                        wait(dve, s_silu, base + a.i + 1)
                        nc.vector.tensor_tensor(by_block(hid[n]), by_block(hid[n]), h3[n], ALU.mult).then_inc(s_hid, 1)
                    a = lagged(m, j, BACK, U, N)
                    if a:
                        n = a.j % 2
                        wait(dve, s_hturn, base + a.i + 1)
                        wait(dve, s_down, base + a.i - 1)
                        nc.vector.tensor_copy(hidT[n][:], psT[:, 0:G * I]).then_inc(s_hT, 1)
                    a = lagged(m, j, DOWN, U, N)
                    if a:
                        wait(dve, s_down, base + a.i + 1)
                        wait(dve, s_y_out[a.j], 16 * (a.m + t * visits[a.j]))
                        nc.vector.tensor_copy(y[a.j][:].rearrange("p b e -> p (b e)"), psY[:, 0:G * D]).then_inc(s_y, 1)
                    if t > 0 and not (isinstance(m, int) and not 1 <= m <= ROUNDS):
                        per = f.K // ADDS
                        k = j % per * ADDS
                        images = U // per
                        u = j // per
                        a = Image(j=u % 2, m=(m - 1) * (images // 2) + u // 2, i=(m - 1) * images + u)
                        rows.add(nc, dve, g, r, a, t - 1, k, ADDS)
                each_group(dve, DOWN, body)

            @block.gpsimd
            def _(pool):
                for t in range(TT - 1):
                    for j in range(U):
                        pool.wait_ge(s_y_out[j], 16 * (t + 1) * visits[j])
                    stand(pool, g)

                    def body(m, j):
                        rows.fetch(nc, pool, g, d, r, lagged(m, j, 0, 2), t)
                    turns(pool, 2, 0, body)


class Rows:

    def __init__(self, ph, f, first, arrived):
        self.f, self.first, self.slots, self.arrived = f, first, len(arrived), arrived
        self.got = [ph.sb(f"rows{j}", [R, f.K, D]) for j in range(self.slots)]
        self.pos = [ph.sb(f"pos{j}", [R, f.K], I32) for j in range(self.slots)]
        self.s_pos, self.s_add = ph.sem("pos"), ph.sem("rows_added")

    def fetch(self, nc, pool, g, d, r, a, t, ks=None):
        f, n = self.f, (t - self.first) * B + a.i
        ks = ks or range(f.K)
        if ks[0] == 0:
            wait(pool, self.s_add, f.K * (n - self.slots + 1))
            stand(pool, g)
            pool.tensor_copy(self.pos[a.j][:], tile_of(r.pos, a.i, t, 1).rearrange("p o k -> p (o k)")).then_inc(self.s_pos, 1)
            wait(pool, self.s_pos, n + 1)
            stand(pool, g)
        for k in ks:
            pool.indirect_dma_start(self.got[a.j][:, k, :], None, d["ys" + str(f.layer)][t],
                                    bass.IndirectOffsetOnAxis(ap=self.pos[a.j][:, k:k + 1], axis=0)).then_inc(self.arrived[a.j], 16)

    def add(self, nc, dve, g, r, a, t, k, count):
        f, n = self.f, (t - self.first) * B + a.i
        if k == 0:
            visit = a.m + (t - self.first) * B // self.slots
            wait(dve, self.arrived[a.j], 16 * f.K * (visit + 1))
        at = bass.ds(a.i * TT + t, 1)
        hh = g.h[:, at, :].rearrange("p o e -> p (o e)")
        for kk in range(k, k + count):
            if kk > 0:
                wait(dve, self.s_add, f.K * n + kk)
            nc.vector.scalar_tensor_tensor(hh, self.got[a.j][:, kk, :], r.top[:, at, kk:kk + 1].rearrange("p o e -> p (o e)"), hh,
                                           ALU.mult, ALU.add).then_inc(self.s_add, 1)


def combine(nc, g, d, f, r):
    STORES = 8
    with Phase(nc, f"comb{f.layer}") as ph:
        rows = Rows(ph, f, TT - 1, g.got_last[f.layer])
        n = rows.slots
        s_out = ph.sem("out_stored")
        with nc.Block() as block:
            @block.gpsimd
            def _(pool):
                turns(pool, n, 0, lambda m, j: rows.fetch(nc, pool, g, d, r, lagged(m, j, 0, n), TT - 1))

            @block.vector
            def _(dve):
                turns(dve, n, 0, lambda m, j: rows.add(nc, dve, g, r, lagged(m, j, 0, n), TT - 1, 0, f.K))

            @block.sync
            def _(sp):
                per = B // STORES
                for c in range(STORES):
                    sp.wait_ge(rows.s_add, f.K * per * (c + 1))
                    sp.dma_start(d["out"][c * per:(c + 1) * per].rearrange("b (t p) e -> p (b t) e", p=R),
                                 g.h[:, c * per * TT:(c + 1) * per * TT, :]).then_inc(s_out, 16)
                sp.wait_ge(s_out, 16 * STORES)


def ffn0(nc, g, d):
    ffn(nc, g, d, FFN0, mix1)


def ffn1(nc, g, d):
    ffn(nc, g, d, FFN1, combine)


QK = 16
EX = 256
NCAT = EX // 128


def mix1(nc, g, d, f, r):
    U = 2
    FETCH, STAT, NORM, NORM2, UP = 0, 1, 2, 3, 4
    HALF = f.K // 2
    with Phase(nc, "mix") as ph:
        w = ph.sb("expand", [D, 2 * QK + 2 * EX])
        w_qk = ph.sb("expand_qk", [D, 2, 128])
        rows = Rows(ph, f, TT - 1, g.got_last[f.layer])
        stats = [ph.sb(f"stats{n}", [R, TT, 6]) for n in range(2)]
        mv = [ph.sb(f"mv{n}", [R, TT, 2]) for n in range(2)]
        veps = [ph.sb(f"veps{n}", [R, TT]) for n in range(2)]
        rstd = [ph.sb(f"rstd{n}", [R, TT]) for n in range(2)]
        x = [ph.sb(f"x{j}", [R, TT, D]) for j in range(U)]
        nx = [ph.sb(f"nx{j}", [R, TT, D]) for j in range(U)]
        nxT = [ph.sb(f"nxT{j}", [D, TOK]) for j in range(U)]
        qkT = [ph.sb(f"qkT{j}", [D, 2, TOK]) for j in range(U)]
        gelu = [ph.sb(f"gelu{j}", [R, TT, EX]) for j in range(U)]
        gated = [ph.sb(f"gated{j}", [R, TT, EX]) for j in range(U)]
        psT = ph.ps("psT", [128, 512])
        psQK = ph.ps("psQK", [128, 2, 512])
        psE = ph.ps("psE", [128, TT, 512])
        s_w, s_zero, s_wqk = ph.sem("weights_in"), ph.sem("zero_set"), ph.sem("qk_weights")
        s_stats, s_mv, s_veps, s_rstd, s_norm = ([ph.sem(f"{n}{k}") for k in range(2)] for n in ("stats", "mv", "veps", "rstd", "normalised"))
        s_turned, s_nxT, s_qk, s_qkT = (ph.sem(n) for n in ("turned", "nxT_written", "qk_multiplied", "qkT_written"))
        s_up, s_gelu, s_gated = ph.sem("expanded"), ph.sem("gelu"), ph.sem("gated")
        s_x_out, s_qk_out, s_g_out = ([ph.sem(f"{n}_out{j}") for j in range(U)] for n in ("x", "qk", "gated"))

        with nc.Block() as block:
            @block.sync
            def _(sp):
                sp.dma_start(w[:], d["expand"]).then_inc(s_w, 16)

                def body(m, j):
                    a = lagged(m, j, NORM, U)
                    if a:
                        wait(sp, s_norm[0], 3 * a.i + 3)
                        sp.dma_start(d["xn"][bass.ds(a.i, 1)].rearrange("o p t e -> (o p) t e"), x[a.j][:]).then_inc(s_x_out[a.j], 16)
                    a = lagged(m, j, UP, U)
                    if a:
                        wait(sp, s_qkT, a.i + 1)
                        sp.dma_start(d["qkT"][bass.ds(a.i, 1)].rearrange("o e n t -> (o e) n t"), qkT[a.j][0:QK]).then_inc(s_qk_out[a.j], 16)
                        wait(sp, s_gated, a.i + 1)
                        sp.dma_start(d["gated"][bass.ds(a.i, 1)].rearrange("o p t e -> (o p) t e"), gated[a.j][:]).then_inc(s_g_out[a.j], 16)
                turns(sp, U, UP, body)
                for j in range(U):
                    for s in (s_x_out[j], s_qk_out[j], s_g_out[j]):
                        sp.wait_ge(s, 16 * B // U)

            @block.gpsimd
            def _(pool):
                pool.memset(w_qk[:], 0.0).then_inc(s_zero, 1)
                pool.wait_ge(s_zero, 1)
                pool.wait_ge(s_w, 16)
                for n in range(2):
                    pool.tensor_copy(w_qk[:, n, 0:QK], w[:, n * QK:(n + 1) * QK]).then_inc(s_wqk, 1)

                def rstd_of(n, a):
                    wait(pool, s_mv[n], 3 * a.i + 3)
                    wait(pool, s_rstd[n], a.i)
                    stand(pool, g)
                    pool.tensor_scalar(veps[n][:], mv[n][:, :, 1], EPS, None, ALU.add).then_inc(s_veps[n], 1)
                    wait(pool, s_veps[n], a.i + 1)
                    wait(pool, s_norm[n], 3 * a.i)
                    pool.tensor_tensor(rstd[n][:], veps[n][:], g.minus_half[0:R, 0:TT], ALU.pow).then_inc(s_rstd[n], 1)

                def body(m, j):
                    fetch, stat, norm = (lagged(m, j, lag, U) for lag in (FETCH, STAT, NORM))
                    if fetch:
                        rows.fetch(nc, pool, g, d, r, fetch, TT - 1, range(0, HALF))
                    if norm:
                        rstd_of(1, norm)
                    if fetch:
                        rows.fetch(nc, pool, g, d, r, fetch, TT - 1, range(HALF, f.K))
                    if stat:
                        rstd_of(0, stat)
                turns(pool, U, UP, body)

            @block.vector
            def _(dve):
                def statistics(n, a, src):
                    wait(dve, s_mv[n], 3 * a.i)
                    stand(dve, g)
                    for t in range(TT):
                        nc.vector.bn_stats(stats[n][:, t, :], src(t)).then_inc(s_stats[n], 1)
                    wait(dve, s_stats[n], 3 * a.i + 3)
                    wait(dve, s_norm[n], 3 * a.i)
                    wait(dve, s_veps[n], a.i)
                    stand(dve, g)
                    for t in range(TT):
                        nc.vector.bn_aggr(mv[n][:, t, :], stats[n][:, t, :]).then_inc(s_mv[n], 1)

                def normalise(n, a, src, dst):
                    for t in range(TT):
                        nc.vector.tensor_scalar(dst[:, t, :], src(t), mv[n][:, t, 0:1], rstd[n][:, t:t + 1], ALU.subtract, ALU.mult).then_inc(s_norm[n], 1)

                def h_tile(a):
                    return lambda t: g.h[:, bass.ds(a.i * TT + t, 1), :].rearrange("p o e -> p (o e)")

                def body(m, j):
                    a = lagged(m, j, NORM, U)
                    if a:
                        wait(dve, s_rstd[0], a.i + 1)
                        wait(dve, s_x_out[a.j], 16 * a.m)
                        wait(dve, s_norm[1], 3 * (a.i - 1))
                        normalise(0, a, h_tile(a), x[a.j])
                    a = lagged(m, j, NORM2, U)
                    if a:
                        wait(dve, s_rstd[1], a.i + 1)
                        wait(dve, s_turned, a.i - 1)
                        normalise(1, a, lambda t: x[a.j][:, t, :], nx[a.j])
                    a = lagged(m, j, NORM, U)
                    if a:
                        wait(dve, s_norm[0], 3 * a.i + 3)
                        statistics(1, a, lambda t: x[a.j][:, t, :])
                    a = lagged(m, j, STAT, U)
                    if a:
                        rows.add(nc, dve, g, r, a, TT - 1, 0, f.K)
                        wait(dve, rows.s_add, f.K * (a.i + 1))
                        statistics(0, a, h_tile(a))
                    a = lagged(m, j, UP, U)
                    if a:
                        wait(dve, s_gelu, a.i + 1)
                        wait(dve, s_g_out[a.j], 16 * a.m)
                        nc.vector.tensor_tensor(gated[a.j][:], gelu[a.j][:], psE[0:R, :, 0:EX], ALU.mult).then_inc(s_gated, 1)
                turns(dve, U, UP, body)

            @block.tensor
            def _(pe):
                pe.wait_ge(s_w, 16)
                pe.wait_ge(s_wqk, 2)

                def body(m, j):
                    a = lagged(m, j, UP, U)
                    if a:
                        wait(pe, s_nxT, a.i + 1)
                        wait(pe, s_qkT, a.i)
                        for n in range(2):
                            mm = nc.tensor.matmul(psQK[:, n, 0:TOK], w_qk[:, n, :], nxT[a.j][:], start=True, stop=True)
                        mm.then_inc(s_qk, 1)
                        wait(pe, s_gated, a.i)
                        for t in range(TT):
                            mm = nc.tensor.matmul(psE[0:R, t, :], nxT[a.j][:, t * R:(t + 1) * R], w[:, 2 * QK:], start=True, stop=True)
                        mm.then_inc(s_up, 1)
                    a = lagged(m, j, NORM2, U)
                    if a:
                        wait(pe, s_norm[1], 3 * a.i + 3)
                        wait(pe, s_nxT, a.i)
                        for t in range(TT):
                            mm = nc.tensor.transpose(psT[:, t * R:(t + 1) * R], nx[a.j][:, t, :], g.ident[0:R, 0:R])
                        mm.then_inc(s_turned, 1)
                turns(pe, U, UP, body)

            @block.scalar
            def _(act):
                def body(m, j):
                    a = lagged(m, j, UP, U)
                    if a:
                        wait(act, s_qk, a.i + 1)
                        wait(act, s_qk_out[a.j], 16 * a.m)
                        nc.scalar.copy(qkT[a.j][:], psQK[:, :, 0:TOK]).then_inc(s_qkT, 1)
                        wait(act, s_up, a.i + 1)
                        wait(act, s_gated, a.i - 1)
                        nc.scalar.activation(gelu[a.j][:], psE[0:R, :, EX:2 * EX], ACT.Gelu).then_inc(s_gelu, 1)
                    a = lagged(m, j, NORM2, U)
                    if a:
                        wait(act, s_turned, a.i + 1)
                        wait(act, s_up, a.i - 1)
                        nc.scalar.copy(nxT[a.j][:], psT[:, 0:TOK]).then_inc(s_nxT, 1)
                turns(act, U, UP, body)


def attention1(nc, g, d):
    U = 2
    LOAD, SCORE, TURN, MIX, CAT, OUT = 0, 1, 2, 3, 4, 5
    PAIRS = [(t, c) for t in range(TT) for c in range(t + 1)]
    with Phase(nc, "at1") as ph:
        proj = ph.sb("project", [128, NCAT, D])
        mult = ph.sb("bias_mult", [R, 1])
        rel = ph.sb("rel", [R, TT, TOK])
        bias = ph.sb("bias", [R, TT, TOK])
        q = [ph.sb(f"qk{j}", [D, 2, TOK]) for j in range(U)]
        x = [ph.sb(f"x{j}", [R, TT, D]) for j in range(U)]
        gated = [ph.sb(f"gated{j}", [R, TT, EX]) for j in range(U)]
        sc = [ph.sb(f"scores{j}", [R, TT, TOK]) for j in range(U)]
        negmax = [ph.sb(f"negmax{j}", [R, TT]) for j in range(U)]
        sums = [ph.sb(f"sums{j}", [R, TT]) for j in range(U)]
        recip = [ph.sb(f"recip{j}", [R, TT]) for j in range(U)]
        probs = [ph.sb(f"probs{j}", [R, TT, TOK]) for j in range(U)]
        pT = [ph.sb(f"probsT{j}", [R, len(PAIRS), R]) for j in range(U)]
        attn = [ph.sb(f"attn{j}", [R, TT, D]) for j in range(U)]
        catT = [ph.sb(f"catT{j}", [128, NCAT, TOK]) for j in range(U)]
        psS = ph.ps("psS", [128, TT, 512])
        psP = ph.ps("psP", [128, 2, 512])
        psA = ph.ps("psA", [128, 512])
        psC = ph.ps("psC", [128, 2, 512])
        psO = psA
        s_w, s_rel, s_bias, s_mask = ph.sem("weights_in"), ph.sem("rel_set"), ph.sem("bias_set"), ph.sem("masked")
        s_zero = ph.sem("zero_set")
        s_q = [ph.sem(f"qk_in{j}") for j in range(U)]
        s_x, s_g = ([ph.sem(f"{n}_in{j}") for j in range(U)] for n in ("x", "gated"))
        s_scored, s_sc, s_max, s_exp, s_recip = (ph.sem(n) for n in ("scored", "biased", "max", "exp", "recip"))
        s_pturn, s_pT, s_mixed, s_attn, s_cturn, s_catT, s_out, s_add, s_h = (ph.sem(n) for n in (
            "probs_turned", "probsT", "mixed", "attn", "cat_turned", "catT", "projected", "x_added", "h_added"))

        with nc.Block() as block:
            @block.sync
            def _(sp):
                sp.dma_start(proj[:], d["project"].rearrange("(c p) e -> p c e", p=128)).then_inc(s_w, 16)
                sp.dma_start(mult[:], d["bias_mult"].broadcast_to([R, 1])).then_inc(s_w, 16)
                sp.wait_ge(s_zero, U)

                def body(m, j):
                    a = lagged(m, j, LOAD, U)
                    if a:
                        wait(sp, s_scored, a.i - 1)
                        sp.dma_start(q[a.j][0:QK], d["qkT"][bass.ds(a.i, 1)].rearrange("o e n t -> (o e) n t")).then_inc(s_q[a.j], 16)
                    a = lagged(m, j, TURN, U)
                    if a:
                        wait(sp, s_cturn, a.i - 1)
                        sp.dma_start(gated[a.j][:], d["gated"][bass.ds(a.i, 1)].rearrange("o p t e -> (o p) t e")).then_inc(s_g[a.j], 16)
                    a = lagged(m, j, MIX, U)
                    if a:
                        wait(sp, s_h, a.i - 1)
                        sp.dma_start(x[a.j][:], d["xn"][bass.ds(a.i, 1)].rearrange("o p t e -> (o p) t e")).then_inc(s_x[a.j], 16)
                turns(sp, U, OUT, body)

            @block.gpsimd
            def _(pool):
                pool.iota(rel[:], pattern=[[-R, TT], [1, TOK]], base=0, channel_multiplier=-1,
                          allow_small_or_imprecise_dtypes=True).then_inc(s_rel, 1)
                for j in range(U):
                    pool.memset(q[j][:], 0.0).then_inc(s_zero, 1)
                pool.wait_ge(s_bias, 1)
                pool.affine_select(out=bias[:], in_=bias[:], compare_op=ALU.is_ge, fill=NEG, base=0,
                                   pattern=[[R, TT], [-1, TOK]], channel_multiplier=1).then_inc(s_mask, 1)

                def body(m, j):
                    a = lagged(m, j, OUT, U)
                    if a:
                        wait(pool, s_add, a.i + 1)
                        pool.tensor_tensor(tile_of(g.h, a.i), tile_of(g.h, a.i), x[a.j][:], ALU.add).then_inc(s_h, 1)
                turns(pool, U, OUT, body)

            @block.tensor
            def _(pe):
                pe.wait_ge(s_w, 32)
                pe.wait_ge(s_zero, U)

                def body(m, j):
                    a = lagged(m, j, SCORE, U)
                    if a:
                        wait(pe, s_q[a.j], 16 * (a.m + 1))
                        wait(pe, s_sc, 3 * a.i)
                        for t in range(TT):
                            n = (t + 1) * R
                            mm = nc.tensor.matmul(psS[0:R, t, 0:n], q[a.j][:, 0, t * R:(t + 1) * R], q[a.j][:, 1, 0:n], start=True, stop=True)
                        mm.then_inc(s_scored, 1)
                    a = lagged(m, j, OUT, U)
                    if a:
                        wait(pe, s_catT, a.i + 1)
                        wait(pe, s_add, a.i)
                        n = a.i + OUT - MIX
                        wait(pe, s_attn, min(n, B) if isinstance(n, int) else n)
                        for t in range(TT):
                            for c in range(NCAT):
                                mm = nc.tensor.matmul(psO[0:R, t * D:(t + 1) * D], catT[a.j][:, c, t * R:(t + 1) * R], proj[:, c, :],
                                                      start=(c == 0), stop=(c == NCAT - 1))
                        mm.then_inc(s_out, 1)
                    a = lagged(m, j, TURN, U)
                    if a:
                        wait(pe, s_exp, 3 * a.i + 3)
                        wait(pe, s_pT, a.i)
                        for n, (t, c) in enumerate(PAIRS):
                            mm = nc.tensor.transpose(psP[0:R, n // 3, (n % 3) * R:(n % 3 + 1) * R], probs[a.j][:, t, c * R:(c + 1) * R], g.ident[0:R, 0:R])
                        mm.then_inc(s_pturn, 1)
                    a = lagged(m, j, CAT, U)
                    if a:
                        wait(pe, s_attn, a.i + 1)
                        wait(pe, s_catT, a.i)
                        for t in range(TT):
                            nc.tensor.transpose(psC[:, 0, t * R:(t + 1) * R], gated[a.j][:, t, 0:128], g.ident[0:R, 0:R])
                            mm = nc.tensor.transpose(psC[:, 1, t * R:(t + 1) * R], attn[a.j][:, t, :], g.ident[0:R, 0:R])
                        mm.then_inc(s_cturn, 1)
                    a = lagged(m, j, MIX, U)
                    if a:
                        wait(pe, s_pT, a.i + 1)
                        wait(pe, s_g[a.j], 16 * (a.m + 1))
                        n = a.i - OUT + MIX + 1
                        wait(pe, s_attn, a.i)
                        wait(pe, s_add, n)
                        for t in range(TT):
                            for c in range(t + 1):
                                mm = nc.tensor.matmul(psA[0:R, t * D:(t + 1) * D], pT[a.j][:, PAIRS.index((t, c)), :], gated[a.j][:, c, 128:256],
                                                      start=(c == 0), stop=(c == t))
                        mm.then_inc(s_mixed, 1)
                turns(pe, U, OUT, body)

            @block.scalar
            def _(act):
                act.wait_ge(s_w, 32)
                act.wait_ge(s_rel, 1)
                nc.scalar.activation(bias[:], rel[:], ACT.Sigmoid, bias=mult[:, 0:1]).then_inc(s_bias, 1)

                def body(m, j):
                    a = lagged(m, j, TURN, U)
                    if a:
                        wait(act, s_max, 3 * a.i + 3)
                        wait(act, s_pturn, a.i - 1)
                        wait(act, s_recip, a.i - 1)
                        for t in range(TT):
                            n = (t + 1) * R
                            nc.scalar.activation(probs[a.j][:, t, 0:n], sc[a.j][:, t, 0:n], ACT.Exp, bias=negmax[a.j][:, t:t + 1],
                                                 accum_out=sums[a.j][:, t:t + 1]).then_inc(s_exp, 1)
                        wait(act, s_pturn, a.i + 1)
                        wait(act, s_mixed, a.i - 1)
                        nc.scalar.copy(pT[a.j][:].rearrange("p (b n) r -> p b (n r)", b=2), psP[0:R, :, 0:3 * R]).then_inc(s_pT, 1)
                    a = lagged(m, j, CAT, U)
                    if a:
                        wait(act, s_cturn, a.i + 1)
                        wait(act, s_out, a.i - 1)
                        nc.scalar.copy(catT[a.j][:], psC[:, :, 0:TOK]).then_inc(s_catT, 1)
                turns(act, U, OUT, body)

            @block.vector
            def _(dve):
                dve.wait_ge(s_mask, 1)

                def body(m, j):
                    a = lagged(m, j, SCORE, U)
                    if a:
                        wait(dve, s_scored, a.i + 1)
                        wait(dve, s_exp, 3 * (a.i - 1))
                        for t in range(TT):
                            n = (t + 1) * R
                            nc.vector.scalar_tensor_tensor(sc[a.j][:, t, 0:n], psS[0:R, t, 0:n], 0.25, bias[:, t, 0:n], ALU.mult, ALU.add).then_inc(s_sc, 1)
                        for t in range(TT):
                            n = (t + 1) * R
                            wait(dve, s_sc, 3 * a.i + t + 1)
                            nc.vector.tensor_reduce(negmax[a.j][:, t:t + 1], sc[a.j][:, t, 0:n], AX.X, ALU.max, negate=True).then_inc(s_max, 1)
                    a = lagged(m, j, OUT, U)
                    if a:
                        wait(dve, s_out, a.i + 1)
                        wait(dve, s_x[a.j], 16 * (a.m + 1))
                        nc.vector.tensor_tensor(x[a.j][:], psO[0:R, 0:TT * D].rearrange("p (t e) -> p t e", t=TT), x[a.j][:], ALU.add).then_inc(s_add, 1)
                    a = lagged(m, j, MIX, U)
                    if a:
                        wait(dve, s_exp, 3 * a.i + 3)
                        wait(dve, s_attn, a.i - 1)
                        nc.vector.reciprocal(recip[a.j][:], sums[a.j][:]).then_inc(s_recip, 1)
                        wait(dve, s_recip, a.i + 1)
                        wait(dve, s_mixed, a.i + 1)
                        wait(dve, s_cturn, a.i - 1)
                        nc.vector.tensor_tensor(attn[a.j][:], psA[0:R, 0:TT * D].rearrange("p (t e) -> p t e", t=TT),
                                                recip[a.j][:].unsqueeze(2).broadcast_to([R, TT, D]), ALU.mult).then_inc(s_attn, 1)
                turns(dve, U, OUT, body)



PHASES = (embed, attention0, ffn0, attention1, ffn1)


def program(nc, d):
    ctx = ExitStack()
    with ctx:
        g = Shared()
        g.h = ctx.enter_context(nc.sbuf_tensor("h", [R, NTILE, D], F32))
        g.ident = ctx.enter_context(nc.sbuf_tensor("ident", [128, 128], F32))
        g.ident16 = ctx.enter_context(nc.sbuf_tensor("ident16", [128, 128], BF16))
        g.minus_half = ctx.enter_context(nc.sbuf_tensor("minus_half", [128, 4], F32))
        g.stand = ctx.enter_context(nc.semaphore("stand"))
        g.blanked = ctx.enter_context(nc.semaphore("rows_blanked"))
        g.sent = [[ctx.enter_context(nc.semaphore(f"sent{layer}_{t}")) for t in range(TT)] for layer in range(2)]
        g.got = [[ctx.enter_context(nc.semaphore(f"rows_in{layer}_{j}")) for j in range(2)] for layer in range(2)]
        g.got_last = [[ctx.enter_context(nc.semaphore(f"last_rows_in{layer}_{j}")) for j in range(n)] for layer, n in enumerate((2, 4))]
        scratch(nc, d)
        constants(nc, g)
        for phase in PHASES:
            phase(nc, g, d)


def scratch(nc, d):
    def dram(name, shape, dt=F32):
        return nc.dram_tensor(name, shape, dt, kind="Internal").ap()
    d["xn"] = dram("xn_scratch", (B, R, TT, D))
    d["vone"] = dram("v_scratch", (B, R, TT, NH, 2 * HD))
    d["q_parts"] = dram("q_scratch", (B, NH, HD, 3, TOK), BF16)
    d["xnT"] = dram("xnT_scratch", (B, D, TOK))
    d["owner"] = dram("owner_scratch", (TT * max(FFN0.blocks, FFN1.blocks),), I32)
    for f in (FFN0, FFN1):
        d["xs" + str(f.layer)] = [dram(f"xs{f.layer}_{t}", (f.rows, D)) for t in range(TT)]
        d["ys" + str(f.layer)] = [dram(f"ys{f.layer}_{t}", (f.rows, D)) for t in range(TT)]
    d["qkT"] = dram("qkT_scratch", (B, QK, 2, TOK))
    d["gated"] = dram("gated_scratch", (B, R, TT, EX))
    d["maxima"] = dram("maxima_scratch", (B, 3 * NH, TOK), BF16)
    d["k_parts"] = dram("k_scratch", (B, NH, HD, 3, TOK), BF16)


def laid_out(v):
    def t(a):
        return np.ascontiguousarray(np.swapaxes(np.asarray(a), -1, -2))

    def by_expert(parts):
        return np.concatenate(parts, axis=2).transpose(1, 0, 2).reshape(128, -1)
    x = np.asarray(v["x"])
    n = x.shape[-1] // 16
    px = x.reshape(B, 3, n, 16, n, 16).transpose(0, 1, 3, 5, 2, 4).reshape(B, KC, 128, NP)
    out = {
        "patches": px.transpose(0, 2, 1, 3),
        "w_tok": t(v["L0_tok_w"]).reshape(KC, 128, D).transpose(1, 0, 2),
        "b_tok": v["L0_tok_b"],
        "txt": v["txt"],
        "wq": t(v["L0_attn_W_q"]), "wk": t(v["L0_attn_W_k"]), "wv": t(v["L0_attn_W_v"]), "wo": t(v["L0_attn_W_o"]),
        "gamma": v["L0_attn_ln_gamma"], "beta": v["L0_attn_ln_beta"],
        "gate0": t(v["L0_ffn_gate_w"]),
        "exp0": by_expert([np.asarray(v["L0_ffn_w1"]), np.asarray(v["L0_ffn_w3"]), np.asarray(v["L0_ffn_w2"])]),
        "sw1_0": v["L0_ffn_sw1"], "sw3_0": v["L0_ffn_sw3"], "sw2_0": v["L0_ffn_sw2"],
        "expand": v["L1_attn_expand"], "project": v["L1_attn_project"],
        "bias_mult": np.asarray(v["L1_attn_position_bias_mult"]).reshape(1, 1),
        "gate1": t(v["L1_ffn_gate_w"]),
        "exp1": by_expert([t(v["L1_ffn_w1"]), t(v["L1_ffn_w3"]),
                                t(v["L1_ffn_w2"]).reshape(8, 4, 128, D).transpose(0, 2, 1, 3).reshape(8, 128, 512)]),
        "sw1_1": t(v["L1_ffn_sw1"]), "sw2_1": t(v["L1_ffn_sw2"]),
    }
    return {k: np.ascontiguousarray(a) for k, a in out.items()}


def kernel(**inputs):
    import concourse.bacc as bacc
    from concourse.bass_utils import run_bass_kernel_spmd

    nc = bacc.Bacc("TRN2", target_bir_lowering=False, num_devices=1)
    arrays = laid_out(inputs)
    d = Dram({name: nc.dram_tensor(f"in_{name}", a.shape, mybir.dt.from_np(a.dtype), kind="ExternalInput").ap()
              for name, a in arrays.items()})
    d["out"] = nc.dram_tensor("out_h", (B, TOK, D), F32, kind="ExternalOutput").ap()
    program(nc, d)
    r = run_bass_kernel_spmd(nc, [{f"in_{k}": a for k, a in arrays.items()}], core_ids=[0])
    return r.results[0]["out_h"]
```
